# Optimizing a Trainium2 kernel written in Bass

```python
import numpy as np
import jax
import jax.numpy as jnp

def _softmax(x, axis=-1):
    return jax.nn.softmax(x, axis=axis)

def _gelu(x):
    return jax.nn.gelu(x, approximate=True)

def _silu(x):
    return jax.nn.silu(x)

def _sigmoid(x):
    return jax.nn.sigmoid(x)

def _layernorm(x, axis=-1, eps=1e-05):
    m = jnp.mean(x, axis=axis, keepdims=True)
    v = jnp.var(x, axis=axis, keepdims=True)
    return (x - m) / jnp.sqrt(v + eps)

def _scatter_add(tgt, idx, src, axis=0):
    return tgt.at[idx].add(src)

def _segment_sum(src, seg, n):
    return jax.ops.segment_sum(src, seg, n)
kernel_name = 'mk_xattn_ffn_d1_seqx_r4_634a4f'

def setup_inputs(seed: int=0):
    np.random.seed(seed)
    _w = jnp.asarray

    def _rec_inputs():
        import jax
        import jax.numpy as jnp
        _rk = jax.random.key(seed)
        x = 0.000341 + 1 * jax.random.normal(jax.random.fold_in(_rk, 1), (8, 256, 512), jnp.float32)
        _lenS = 256 - jax.random.randint(jax.random.fold_in(_rk, 7), (8,), 0, max(1, 256 // 4) + 1, jnp.int32)
        _lenS2 = 256 - jax.random.randint(jax.random.fold_in(_rk, 8), (8,), 0, max(1, 256 // 4) + 1, jnp.int32)
        _ctx_2048P = jax.random.normal(jax.random.fold_in(_rk, 11), (8, 16, 512), jnp.float32)
        _ctx_2048c = jax.random.dirichlet(jax.random.fold_in(_rk, 511), 0.3 * jnp.ones((16,), jnp.float32), (8, 256))
        _ctx_2048t = jnp.einsum('bsk,bkd->bsd', _ctx_2048c, _ctx_2048P)
        _ctx_2048t = _ctx_2048t * jax.lax.rsqrt(jnp.mean(jnp.square(_ctx_2048t)) + 1e-12) * 0.953939
        ctx_2048 = -1.47943e-05 + 1.00017 * (_ctx_2048t + 0.3 * jax.random.normal(jax.random.fold_in(_rk, 611), (8, 256, 512), jnp.float32))
        return (x, ctx_2048)
    x, ctx_2048 = _rec_inputs()

    def _L0_xattn_setup():
        import jax, jax.numpy as jnp
        import numpy as np

        def _wkv(time_decay, time_first, k, v):
            w = -jnp.exp(time_decay)
            u = time_first
            B, T, C = k.shape
            aa = jnp.zeros((B, C), dtype=k.dtype)
            bb = jnp.zeros((B, C), dtype=k.dtype)
            pp = jnp.full((B, C), -1e+38, dtype=k.dtype)

            def step(carry, kv_t):
                aa, bb, pp = carry
                kt, vt = kv_t
                ww = u + kt
                q = jnp.maximum(pp, ww)
                e1 = jnp.exp(pp - q)
                e2 = jnp.exp(ww - q)
                y_t = (e1 * aa + e2 * vt) / (e1 * bb + e2)
                ww2 = pp + w
                q2 = jnp.maximum(ww2, kt)
                e1b = jnp.exp(ww2 - q2)
                e2b = jnp.exp(kt - q2)
                new_carry = (e1b * aa + e2b * vt, e1b * bb + e2b, q2)
                return (new_carry, y_t)
            ks = jnp.transpose(k, (1, 0, 2))
            vs = jnp.transpose(v, (1, 0, 2))
            _, ys = jax.lax.scan(step, (aa, bb, pp), (ks, vs))
            return jnp.transpose(ys, (1, 0, 2))
        key = jax.random.key(seed)
        k1, k2, k3, k4 = jax.random.split(key, 4)
        B, T, C = (8, 256, 512)
        return {'batch_size': B, 'seq_len': T, 'embedding_dim': C, 'time_decay': jax.random.normal(k1, (C,), dtype=jnp.float32), 'time_first': jax.random.normal(k2, (C,), dtype=jnp.float32), 'k': jax.random.normal(k3, (B, T, C), dtype=jnp.float32), 'v': jax.random.normal(k4, (B, T, C), dtype=jnp.float32)}
    _L0_xattn_all = _L0_xattn_setup()
    _L0_xattn_in = {k: v for k, v in _L0_xattn_all.items() if k in ('time_decay', 'time_first')}
    del _L0_xattn_all

    def _L0_ffn_setup():
        import jax, jax.numpy as jnp
        import numpy as np
        TOP_K = 6
        N_GROUP = 8
        TOPK_GROUP = 3
        CAPACITY = 192
        RSF = 1.0
        key = jax.random.key(seed)
        ks = jax.random.split(key, 8)
        B, S, H = (1, 1024, 512)
        E, M = (64, 352)
        MS = 704
        sc = 0.02
        return {'hidden_states': jax.random.normal(ks[0], (B, S, H), jnp.float32), 'gate_weight': jax.random.normal(ks[1], (E, H), jnp.float32) * sc, 'Wg': jax.random.normal(ks[2], (E, M, H), jnp.float32) * sc, 'Wu': jax.random.normal(ks[3], (E, M, H), jnp.float32) * sc, 'Wd': jax.random.normal(ks[4], (E, H, M), jnp.float32) * sc, 'Sg': jax.random.normal(ks[5], (MS, H), jnp.float32) * sc, 'Su': jax.random.normal(ks[6], (MS, H), jnp.float32) * sc, 'Sd': jax.random.normal(ks[7], (H, MS), jnp.float32) * sc}
    _L0_ffn_all = _L0_ffn_setup()
    _L0_ffn_in = {k: v for k, v in _L0_ffn_all.items() if k in ('gate_weight', 'Wg', 'Wu', 'Wd', 'Sg', 'Su', 'Sd')}
    del _L0_ffn_all
    return {'x': x, 'ctx_2048': ctx_2048, 'L0_xattn_time_decay': _L0_xattn_in['time_decay'], 'L0_xattn_time_first': _L0_xattn_in['time_first'], 'L0_ffn_gate_weight': _L0_ffn_in['gate_weight'], 'L0_ffn_Wg': _L0_ffn_in['Wg'], 'L0_ffn_Wu': _L0_ffn_in['Wu'], 'L0_ffn_Wd': _L0_ffn_in['Wd'], 'L0_ffn_Sg': _L0_ffn_in['Sg'], 'L0_ffn_Su': _L0_ffn_in['Su'], 'L0_ffn_Sd': _L0_ffn_in['Sd']}

def reference(x, ctx_2048, L0_xattn_time_decay, L0_xattn_time_first, L0_ffn_gate_weight, L0_ffn_Wg, L0_ffn_Wu, L0_ffn_Wd, L0_ffn_Sg, L0_ffn_Su, L0_ffn_Sd):
    import jax
    import jax.numpy as jnp

    def _L0_xattn_ref(batch_size, seq_len, embedding_dim, time_decay, time_first, k, v):
        import jax, jax.numpy as jnp
        import numpy as np

        def _wkv(time_decay, time_first, k, v):
            w = -jnp.exp(time_decay)
            u = time_first
            B, T, C = k.shape
            aa = jnp.zeros((B, C), dtype=k.dtype)
            bb = jnp.zeros((B, C), dtype=k.dtype)
            pp = jnp.full((B, C), -1e+38, dtype=k.dtype)

            def step(carry, kv_t):
                aa, bb, pp = carry
                kt, vt = kv_t
                ww = u + kt
                q = jnp.maximum(pp, ww)
                e1 = jnp.exp(pp - q)
                e2 = jnp.exp(ww - q)
                y_t = (e1 * aa + e2 * vt) / (e1 * bb + e2)
                ww2 = pp + w
                q2 = jnp.maximum(ww2, kt)
                e1b = jnp.exp(ww2 - q2)
                e2b = jnp.exp(kt - q2)
                new_carry = (e1b * aa + e2b * vt, e1b * bb + e2b, q2)
                return (new_carry, y_t)
            ks = jnp.transpose(k, (1, 0, 2))
            vs = jnp.transpose(v, (1, 0, 2))
            _, ys = jax.lax.scan(step, (aa, bb, pp), (ks, vs))
            return jnp.transpose(ys, (1, 0, 2))
        assert seq_len <= 256
        return _wkv(time_decay, time_first, k, v)

    def _L0_ffn_ref(hidden_states, gate_weight, Wg, Wu, Wd, Sg, Su, Sd):
        import jax, jax.numpy as jnp
        import numpy as np
        TOP_K = 6
        N_GROUP = 8
        TOPK_GROUP = 3
        CAPACITY = 192
        RSF = 1.0
        B, S, H = hidden_states.shape
        E, M, _ = Wg.shape
        K, NG, TG, C = (TOP_K, N_GROUP, TOPK_GROUP, CAPACITY)
        x = hidden_states.reshape(-1, H)
        T = x.shape[0]
        logits = x.astype(jnp.float32) @ gate_weight.astype(jnp.float32).T
        scores = jax.nn.softmax(logits, axis=-1)
        group_scores = scores.reshape(T, NG, E // NG).max(axis=-1)
        _, gidx = jax.lax.top_k(group_scores, TG)
        gmask = jnp.zeros((T, NG), scores.dtype).at[jnp.arange(T)[:, None], gidx].set(1.0)
        smask = jnp.repeat(gmask, E // NG, axis=1)
        tmp_scores = jnp.where(smask > 0, scores, 0.0)
        topk_w, topk_i = jax.lax.top_k(tmp_scores, K)
        topk_w = topk_w * RSF
        flat = topk_i.reshape(-1)
        oh = jax.nn.one_hot(flat, E, dtype=jnp.int32)
        pos = jnp.sum(jnp.cumsum(oh, axis=0) * oh, axis=-1) - 1
        slot = flat * C + jnp.minimum(pos, C - 1)
        tok = jnp.arange(T * K) // K
        buf = jnp.zeros((E * C, H), x.dtype).at[slot].set(x[tok]).reshape(E, C, H)
        g = jnp.einsum('ech,emh->ecm', buf, Wg)
        u = jnp.einsum('ech,emh->ecm', buf, Wu)
        out = jnp.einsum('ecm,ehm->ech', jax.nn.silu(g) * u, Wd).reshape(E * C, H)
        yk = out[slot].reshape(T, K, H)
        y = jnp.sum(yk * topk_w[..., None].astype(yk.dtype), axis=1)
        shared = jax.nn.silu(x @ Sg.T) * (x @ Su.T) @ Sd.T
        return (y + shared).reshape(B, S, H)
    x = x + _L0_xattn_ref(8, 256, 512, L0_xattn_time_decay, L0_xattn_time_first, _layernorm(x, axis=-1), ctx_2048)
    x = x + _L0_ffn_ref(_layernorm(x, axis=-1), L0_ffn_gate_weight, L0_ffn_Wg, L0_ffn_Wu, L0_ffn_Wd, L0_ffn_Sg, L0_ffn_Su, L0_ffn_Sd)
    return x

_drawn_inputs = setup_inputs


def setup_inputs(seed=0):
    import zlib

    import numpy as np

    out = dict(_drawn_inputs(seed))
    spreads = {}
    factors = {'L0_ffn_gate_weight': 8.0,
     'L0_ffn_Wg': 8.0,
     'L0_ffn_Wu': 8.0,
     'L0_ffn_Wd': 8.0,
     'L0_ffn_Sg': 8.0,
     'L0_ffn_Su': 8.0,
     'L0_ffn_Sd': 8.0}
    for name, (base, spread) in spreads.items():
        noise = np.random.default_rng([zlib.crc32(name.encode()), seed]).standard_normal(out[name].shape)
        drawn = base * np.exp(spread * noise) if base else spread * noise
        out[name] = jnp.asarray(drawn.astype(out[name].dtype))
    for name, factor in factors.items():
        out[name] = (out[name] * factor).astype(out[name].dtype)
    return out
```

```python
import concourse.bass as bass
from concourse import mybir
from contextlib import ExitStack

F32, F32R, BF16, U32 = (mybir.dt.float32, mybir.dt.float32r, mybir.dt.bfloat16, mybir.dt.uint32)
ALU = mybir.AluOpType
ACT = mybir.ActivationFunctionType
AX = mybir.AxisListType

P = 128
BATCH, SEQ, D = 8, 256, 512
TOK = BATCH * SEQ
NT = SEQ // P
DC = D // P
EXP, M, CAP = 64, 352, 192
GROUPS, TOPG, TOPK = 8, 3, 6
GE = EXP // GROUPS
HALF = CAP // 2
MS = 704
MC = [(m, min(P, M - m)) for m in range(0, M, P)]
SC = [(m, min(P, MS - m)) for m in range(0, MS, P)]
EPS = 1e-5
NEG = -1e38
LAST_ROW = TOK
DUMP_ROW = TOK + EXP
ROWS = DUMP_ROW + CAP
HX = D + EXP
PAD = SEQ + 1


def build(nc, x, ctxv, decay, first, gate, wgu, wd, sgu, sd, out):
    hx_dram = nc.dram_tensor("hx_rows", (ROWS, HX), F32, kind="Internal").ap()
    y_dram = nc.dram_tensor("y_rows", (ROWS, D), F32, kind="Internal").ap()

    ctx = ExitStack()
    with ctx:
        def in_stack(stack):
            return lambda name, shape, dt=F32: stack.enter_context(nc.sbuf_tensor(name, shape, dt))

        def sem(name):
            return ctx.enter_context(nc.semaphore(name))

        sb = in_stack(ctx)
        psum = [ctx.enter_context(nc.psum_tensor(f"bank{i}", [P, 512], F32)) for i in range(8)]

        ident = sb("ident", [P, P])
        gtab = [sb(f"gather_ids{h}", [HALF, EXP], U32) for h in range(2)]
        stab = sb("scatter_ids1", [HALF, EXP], U32)
        is_last = sb("is_last", [HALF, 1])
        not_last = sb("not_last", [HALF, 1])
        xall = sb("xall", [P, BATCH * NT, D])
        ovfT = sb("ovfT", [EXP, TOK])
        raw_gu = [sb(f"raw_gu{s}", [P, DC, 2 * M]) for s in range(2)]
        raw_d = [sb(f"raw_d{s}", [P, len(MC), D]) for s in range(2)]

        shared_stack = ExitStack()
        sbs = in_stack(shared_stack)
        base_shared = nc.sbuf_base
        sgu_sb = sbs("sgu_sb", [P, DC, 2 * MS])
        sd_sb = sbs("sd_sb", [P, len(SC), D])
        shid = sbs("shid", [P, len(SC), SEQ])
        th = sbs("th", [P, 2, SEQ])
        hT = sbs("hT", [P, DC, SEQ])
        base_front = nc.sbuf_base

        front_stack = ExitStack()
        sbf = in_stack(front_stack)
        kn = sbf("kn", [P, NT, D])
        kb = sbf("kb", [P, DC, PAD])
        v = sbf("v", [P, DC, SEQ])
        wrep = sbf("wrep", [P, DC, PAD])
        pp = sbf("pp", [P, DC, PAD])
        d1 = sbf("d1", [P, DC, SEQ])
        d2 = sbf("d2", [P, DC, SEQ])
        d3 = sbf("d3", [P, DC, SEQ])
        e1 = sbf("e1", [P, DC, SEQ])
        e1b = sbf("e1b", [P, DC, PAD])
        e2b = sbf("e2b", [P, DC, PAD])
        e2bv = sbf("e2bv", [P, DC, PAD])
        aa = sbf("aa", [P, DC, PAD])
        bb = sbf("bb", [P, DC, PAD])
        hx = sbf("hx", [P, NT, HX])
        gate_sb = sbf("gate_sb", [P, DC, EXP])
        wdec = sbf("wdec", [P, DC])
        ufirst = sbf("ufirst", [P, DC])
        nufirst = sbf("nufirst", [P, DC])
        st6 = sbf("st6", [P, NT, 6])
        mv1 = sbf("mv1", [P, NT, 2])
        mv2 = sbf("mv2", [P, NT, 2])
        ve = sbf("ve", [P, NT])
        rstd1 = sbf("rstd1", [P, NT])
        rstd2 = sbf("rstd2", [P, NT])
        eps_t = sbf("eps_t", [P, NT])
        mhalf = sbf("mhalf", [P, NT])
        lstrict = sbf("lstrict", [P, P], BF16)
        ones = sbf("ones", [P, P], BF16)
        iota_e = sbf("iota_e", [P, EXP])
        iota_ci = sbf("iota_ci", [P, CAP])
        iota_c = sbf("iota_c", [P, CAP], BF16)
        tri = sbf("tri", [P, GROUPS, GROUPS])
        pid1 = sbf("pid1", [P, 1])
        tokid = sbf("tokid", [P, NT])
        tileno = sbf("tileno", [P, NT])
        nmx = sbf("nmx", [P, NT])
        ssum = sbf("ssum", [P, NT])
        rsum = sbf("rsum", [P, NT])
        ex = sbf("ex", [P, NT, EXP])
        gm = sbf("gm", [P, NT, GROUPS])
        ggt = sbf("ggt", [P, NT, GROUPS, GROUPS])
        geq = sbf("geq", [P, NT, GROUPS, GROUPS])
        gcnt = sbf("gcnt", [P, NT, GROUPS])
        tmp = sbf("tmp", [P, NT, EXP])
        v8 = sbf("v8", [P, NT, 8])
        i8 = sbf("i8", [P, NT, 8], U32)
        i6 = sbf("i6", [P, NT, TOPK])
        eq6 = sbf("eq6", [P, NT, TOPK, EXP], BF16)
        pe6 = sbf("pe6", [P, NT, TOPK, EXP])
        mask = sbf("mask", [P, NT, EXP])
        maskb = sbf("maskb", [P, NT, EXP], BF16)
        cum = sbf("cum", [P, EXP], BF16)
        lastt = sbf("lastt", [P, P])
        posel = sbf("posel", [P, NT, TOPK])
        ovf = sbf("ovf", [P, NT, EXP])
        slot1h = sbf("slot1h", [P, NT, TOPK, CAP], BF16)
        val1h = sbf("val1h", [P, NT, TOPK, 2 * EXP], BF16)
        tabs = sbf("tabs", [HALF, 2, 2 * EXP])
        tval = sbf("tval", [HALF, 2, EXP])
        tz = sbf("tz", [HALF, 2, EXP])
        unused = sbf("unused", [HALF, 2])
        lastr = sbf("lastr", [HALF, EXP])
        lcol = sbf("lcol", [EXP, 1])
        lmat = sbf("lmat", [EXP, HALF])
        zrow = sbf("zrow", [P, HX])
        front_top = nc.sbuf_base
        front_stack.close()
        shared_stack.close()

        whi_gu, wlo_gu, whi_d, wlo_d = [None] * 2, [None] * 2, [None] * 2, [None] * 2

        def weight_slot(s):
            whi_gu[s] = sb(f"whi_gu{s}", [P, DC, 2 * M], F32R)
            wlo_gu[s] = sb(f"wlo_gu{s}", [P, DC, 2 * M], F32R)
            whi_d[s] = sb(f"whi_d{s}", [P, len(MC), D], F32R)
            wlo_d[s] = sb(f"wlo_d{s}", [P, len(MC), D], F32R)

        weight_slot(1)
        assert base_shared < nc.sbuf_base <= base_front, (base_shared, nc.sbuf_base, base_front)
        if base_front > nc.sbuf_base:
            sb("gap", [P, base_front - nc.sbuf_base], mybir.dt.uint8)
        weight_slot(0)
        xg = [sb(f"xg{s}", [HALF, 2, HX]) for s in range(2)]
        xhi = [sb(f"xhi{s}", [P, DC, CAP], F32R) for s in range(2)]
        xlo = [sb(f"xlo{s}", [P, DC, CAP], F32R) for s in range(2)]
        wcol = [sb(f"wcol{s}", [HALF, 2]) for s in range(2)]
        sil = sb("sil", [P, 2, CAP])
        hid = sb("hid", [P, 2, CAP])
        hhi = sb("hhi", [P, len(MC), CAP], F32R)
        hlo = sb("hlo", [P, len(MC), CAP], F32R)
        oT = sb("oT", [P, DC, CAP])
        rows = [sb(f"rows{s}", [HALF, 2, D]) for s in range(2)]
        gi = [[sb(f"gi{s}{h}", [HALF, 1], U32) for h in range(2)] for s in range(2)]
        si = [[sb(f"si{s}{h}", [HALF, 1], U32) for h in range(2)] for s in range(2)]
        last_out = sb("last_out", [EXP, D])

        T = [psum[0], psum[1]]
        UP = [psum[2], psum[3]]
        DN = psum[4]
        G = psum[5]
        logits = G[:, 0:NT * EXP].rearrange("p (t e) -> p t e", t=NT)
        pos = G[:, P:P + NT * EXP].rearrange("p (t e) -> p t e", t=NT)
        ovf_ps = G[:, 2 * P:3 * P]
        TAB = [psum[6], psum[7]]
        XT = [psum[0], psum[1]]
        GU = [psum[2], psum[3]]
        OT = [psum[4], psum[5]]
        RW = [psum[6], psum[7]]

        names = """params x_in v_in gate_in shared_w shared_d zero_out hx_out y_out consts dve_const act_const dve_step pool_step
            kn_ready k_tr kb_ready pp_ready d1_ready d2_ready d3_ready decay_ready inject_ready injv_ready e1_ready e2_ready n2_ready
            yT_ready y_tr stat2 rstd2_ready h_ready h_tr hT_ready gate_done mx_ready ex_ready mask_ready hx_ready pos_done
            ovf_ready ovf_tr ovfT_ready onehot_ready tab_done stat1 rstd1_ready
            up_done th_ready hid_done shid_done down_done y_evac
            last_ready last_tr lmat_ready lastr_done tables_ready
            wgu_in0 wgu_in1 wd_in0 wd_in1 whi_gu_done wlo_gu_done whi_d_done wlo_d_done
            gathered0 gathered1 gi_ready si_ready x_tr xhi_done xlo_done gu_done sil_done mul_done hhi_done hlo_done held
            o_done oT_done r_tr rows_done added fin_last fin_ps fin_add fin_out"""
        S = {n: sem(n) for n in names.split()}
        y_back = [sem(f"y_back{b}") for b in range(BATCH)]

        def wait(eng, name, count):
            if not isinstance(count, int) or count > 0:
                eng.wait_ge(S[name], count)

        def hold(eng):
            eng.sem_inc(S["held"], 1)

        block = ctx.enter_context(nc.Block())

        def front_steps(eng, step):
            step(0)
            step(1)
            with eng.Fori(2, BATCH - 1) as i:
                step(i)
            step(BATCH - 1)

        def expert_steps(eng, step):
            for e in range(3):
                step(e, e % 2)
            with eng.Fori(1, EXP // 2 - 1) as t:
                step(2 * t + 1, 1)
                step(2 * t + 2, 0)
            step(EXP - 1, 1)

        def nth(e, s):
            return e // 2 if isinstance(e, int) else (e - s) // 2

        @block.sync
        def _(sp):
            sp.dma_start(wdec[:, :], decay).then_inc(S["params"], 16)
            sp.dma_start(ufirst[:, :], first).then_inc(S["params"], 16)
            sp.dma_start(xall[:, 0:NT, :], x[0].rearrange("(t p) d -> p t d", p=P)).then_inc(S["x_in"], 16)
            sp.dma_start(v[:, :, :], ctxv[0]).then_inc(S["v_in"], 16)
            sp.dma_start(gate_sb[:, :, :], gate).then_inc(S["gate_in"], 16)

            def step(i):
                last = isinstance(i, int) and i == BATCH - 1
                if not last:
                    wait(sp, "x_in", 16 * (i + 1))
                    sp.dma_start(xall[:, bass.ds(NT * (i + 1), NT), :],
                                 x[bass.ds(i + 1, 1)].rearrange("b (t p) d -> p (b t) d", p=P)).then_inc(S["x_in"], 16)
                    wait(sp, "n2_ready", i + 1)
                    sp.dma_start(v[:, :, :], ctxv[bass.ds(i + 1, 1)].rearrange("b p g t -> (b p) g t")).then_inc(S["v_in"], 16)
                wait(sp, "hx_ready", i + 1)
                sp.dma_start(hx_dram[bass.ds(i * SEQ, SEQ), :].rearrange("(t p) d -> p t d", p=P),
                             hx[:, :, :]).then_inc(S["hx_out"], 16)
                if not (isinstance(i, int) and i == 0):
                    wait(sp, "y_evac", NT * i)
                    sp.dma_start(y_dram[bass.ds((i - 1) * SEQ, SEQ), :].rearrange("(t p) d -> p t d", p=P),
                                 xall[:, bass.ds(NT * (i - 1), NT), :]).then_inc(S["y_out"], 16)

            front_steps(sp, step)
            wait(sp, "y_evac", NT * BATCH)
            sp.dma_start(y_dram[(BATCH - 1) * SEQ:TOK, :].rearrange("(t p) d -> p t d", p=P),
                         xall[:, NT * (BATCH - 1):NT * BATCH, :]).then_inc(S["y_out"], 16)

            def load(e, s):
                wait(sp, "wlo_gu_done", DC * (e - 1))
                sp.dma_start(raw_gu[s][:, :, :], wgu[bass.ds(e, 1)].rearrange("e p k m -> (e p) k m")).then_inc(S[f"wgu_in{s}"], 16)
                wait(sp, "wlo_d_done", e - 1)
                sp.dma_start(raw_d[s][:, 0:2, :], wd[bass.ds(e, 1), 0:2 * P, :].rearrange("e (c p) d -> p (e c) d", p=P)).then_inc(S[f"wd_in{s}"], 16)
                sp.dma_start(raw_d[s][0:MC[2][1], 2, :], wd[bass.ds(e, 1), 2 * P:M, :].rearrange("e p d -> (e p) d")).then_inc(S[f"wd_in{s}"], 16)

            load(2, 0)
            load(3, 1)
            with sp.Fori(2, EXP // 2) as t:
                load(2 * t, 0)
                load(2 * t + 1, 1)

            wait(sp, "added", 32 * EXP)
            sp.dma_start(last_out[:, :], y_dram[LAST_ROW:DUMP_ROW, :]).then_inc(S["fin_last"], 16)
            for b in range(BATCH):
                sp.dma_start(xall[:, NT * b:NT * (b + 1), :],
                             y_dram[b * SEQ:(b + 1) * SEQ, :].rearrange("(t p) d -> p t d", p=P)).then_inc(y_back[b], 16)
            for b in range(BATCH):
                wait(sp, "fin_add", NT * (b + 1))
                sp.dma_start(out[b].rearrange("(t p) d -> p t d", p=P), xall[:, NT * b:NT * (b + 1), :]).then_inc(S["fin_out"], 16)
            wait(sp, "fin_out", 16 * BATCH)
            wait(sp, "y_out", 16 * BATCH)
            wait(sp, "hx_out", 16 * BATCH)
            wait(sp, "zero_out", 64)

        @block.gpsimd
        def _(pool):
            nc.gpsimd.memset(ident[:, :], 0.0).then_inc(S["pool_step"], 1)
            nc.gpsimd.memset(ones[:, :], 1.0).then_inc(S["pool_step"], 1)
            nc.gpsimd.memset(tri[:, :, :], 1.0).then_inc(S["pool_step"], 1)
            nc.gpsimd.memset(is_last[:, :], 0.0).then_inc(S["pool_step"], 1)
            nc.gpsimd.memset(not_last[:, :], 1.0).then_inc(S["pool_step"], 1)
            nc.gpsimd.memset(lmat[:, :], 0.0)
            nc.gpsimd.memset(zrow[:, :], 0.0).then_inc(S["pool_step"], 1)
            nc.gpsimd.memset(eps_t[:, :], EPS).then_inc(S["pool_step"], 1)
            nc.gpsimd.memset(mhalf[:, :], -0.5).then_inc(S["pool_step"], 1)
            pool.wait_ge(S["pool_step"], 8)
            nc.gpsimd.affine_select(out=ident[:, :], in_=ident[:, :], compare_op=ALU.not_equal, fill=1.0, base=0,
                                    pattern=[[-1, P]], channel_multiplier=1)
            nc.gpsimd.affine_select(out=lstrict[:, :], in_=ones[:, :], compare_op=ALU.is_gt, fill=0.0, base=0,
                                    pattern=[[1, P]], channel_multiplier=-1)
            nc.gpsimd.affine_select(out=tri[:, :, :], in_=tri[:, :, :], compare_op=ALU.is_gt, fill=0.0, base=0,
                                    pattern=[[1, GROUPS], [-1, GROUPS]], channel_multiplier=0)
            nc.gpsimd.affine_select(out=is_last[:, :], in_=is_last[:, :], compare_op=ALU.not_equal, fill=1.0,
                                    base=-(HALF - 1), pattern=[[0, 1]], channel_multiplier=1)
            nc.gpsimd.affine_select(out=not_last[:, :], in_=not_last[:, :], compare_op=ALU.not_equal, fill=0.0,
                                    base=-(HALF - 1), pattern=[[0, 1]], channel_multiplier=1)
            fl = dict(allow_small_or_imprecise_dtypes=True)
            nc.gpsimd.iota(iota_e[:, :], [[1, EXP]], base=0, channel_multiplier=0, **fl)
            nc.gpsimd.iota(iota_ci[:, :], [[1, CAP]], base=0, channel_multiplier=0, **fl)
            nc.gpsimd.iota(pid1[:, :], [[0, 1]], base=1, channel_multiplier=1, **fl)
            nc.gpsimd.iota(tokid[:, :], [[P, NT]], base=0, channel_multiplier=1, **fl)
            nc.gpsimd.iota(tileno[:, :], [[1, NT]], base=0, channel_multiplier=0, **fl)
            nc.gpsimd.iota(unused[:, :], [[HALF, 2]], base=DUMP_ROW + 1, channel_multiplier=1, **fl)
            nc.gpsimd.iota(lastr[:, :], [[1, EXP]], base=LAST_ROW, channel_multiplier=0, **fl).then_inc(S["consts"], 1)
            pool.wait_ge(S["consts"], 1)
            for r in range(TOK, ROWS, P):
                pool.dma_start(hx_dram[r:r + P, :], zrow[:, :]).then_inc(S["zero_out"], 16)
                pool.dma_start(y_dram[r:r + P, :], zrow[:, 0:D]).then_inc(S["zero_out"], 16)

            done = [8]

            def rstd(mv, to, stat, ready, n, k):
                wait(pool, stat, n + 1)
                nc.gpsimd.tensor_tensor(ve[:, :], mv[:, :, 1], eps_t[:, :], ALU.add).then_inc(S["pool_step"], 1)
                pool.wait_ge(S["pool_step"], 8 + k)
                nc.gpsimd.tensor_tensor(to[:, :], ve[:, :], mhalf[:, :], ALU.pow).then_inc(S[ready], 1)

            rstd(mv1, rstd1, "stat1", "rstd1_ready", 0, 1)

            def step(i):
                last = isinstance(i, int) and i == BATCH - 1
                kcur, ppcur, ppprev = kb[:, :, 1:PAD], pp[:, :, 1:PAD], pp[:, :, 0:SEQ]
                wait(pool, "pp_ready", i + 1)
                nc.gpsimd.tensor_tensor(d2[:, :, :], kcur, ppcur, ALU.subtract).then_inc(S["d2_ready"], 1)
                nc.gpsimd.tensor_tensor(d3[:, :, :], ppprev, kcur, ALU.subtract).then_inc(S["d3_ready"], 1)
                wait(pool, "v_in", 16 * (i + 1))
                wait(pool, "inject_ready", i + 1)
                nc.gpsimd.tensor_tensor(e2bv[:, :, 1:PAD], e2b[:, :, 1:PAD], v[:, :, :], ALU.mult).then_inc(S["injv_ready"], 1)
                wait(pool, "e2_ready", i + 1)
                nc.gpsimd.tensor_tensor(d2[:, :, :], d3[:, :, :], v[:, :, :], ALU.mult).then_inc(S["n2_ready"], 1)
                rstd(mv2, rstd2, "stat2", "rstd2_ready", i, 2 * i + 2)
                if not last:
                    rstd(mv1, rstd1, "stat1", "rstd1_ready", i + 1, 2 * i + 3)

            front_steps(pool, step)

            def gather(e, s):
                wait(pool, "x_tr", e - 1)
                wait(pool, "xhi_done", e - 1)
                for h in range(2):
                    c = nc.gpsimd.tensor_copy(gi[s][h][:, :], gtab[h][:, bass.ds(e, 1)])
                c.then_inc(S["gi_ready"], 1)
                wait(pool, "gi_ready", e + 1)
                hold(pool)
                for h in range(2):
                    pool.indirect_dma_start(out=xg[s][:, h, :], out_offset=None, in_=hx_dram[:, :],
                                            in_offset=bass.IndirectOffsetOnAxis(ap=gi[s][h][:, :], axis=0),
                                            bounds_check=ROWS - 1, oob_is_err=True).then_inc(S[f"gathered{s}"], 16)

            def add(e, s):
                for h, tab in enumerate((gtab[0], stab)):
                    c = nc.gpsimd.tensor_copy(si[s][h][:, :], tab[:, bass.ds(e, 1)])
                c.then_inc(S["si_ready"], 1)
                wait(pool, "si_ready", e + 1)
                wait(pool, "rows_done", e + 1)
                wait(pool, "added", 32 * e)
                hold(pool)
                for h in range(2):
                    pool.indirect_dma_start(out=y_dram[:, :], out_offset=bass.IndirectOffsetOnAxis(ap=si[s][h][:, :], axis=0),
                                            in_=rows[s][:, h, :], in_offset=None, bounds_check=ROWS - 1, oob_is_err=True,
                                            compute_op=ALU.add).then_inc(S["added"], 16)

            wait(pool, "tables_ready", 1)
            wait(pool, "hx_out", 16 * BATCH)
            wait(pool, "zero_out", 64)
            gather(0, 0)
            wait(pool, "y_out", 16 * BATCH)

            def expert(e, s):
                if not (isinstance(e, int) and e == EXP - 1):
                    gather(e + 1, 1 - s)
                if not (isinstance(e, int) and e == 0):
                    add(e - 1, 1 - s)

            expert_steps(pool, expert)
            add(EXP - 1, 1)

        @block.scalar
        def _(act):
            act.dma_start(sgu_sb[:, :, :], sgu).then_inc(S["shared_w"], 16)
            act.dma_start(sd_sb[:, 0:5, :], sd[0:5 * P, :].rearrange("(c p) d -> p c d", p=P)).then_inc(S["shared_d"], 16)
            act.dma_start(sd_sb[0:SC[5][1], 5, :], sd[5 * P:MS, :]).then_inc(S["shared_d"], 16)
            for e in range(2):
                act.dma_start(raw_gu[e][:, :, :], wgu[e]).then_inc(S[f"wgu_in{e}"], 16)
                act.dma_start(raw_d[e][:, 0:2, :], wd[e, 0:2 * P, :].rearrange("(c p) d -> p c d", p=P)).then_inc(S[f"wd_in{e}"], 16)
                act.dma_start(raw_d[e][0:MC[2][1], 2, :], wd[e, 2 * P:M, :]).then_inc(S[f"wd_in{e}"], 16)
            act.wait_ge(S["params"], 32)
            nc.scalar.activation(wdec[:, :], wdec[:, :], ACT.Exp).then_inc(S["act_const"], 1)
            nc.scalar.activation(nufirst[:, :], ufirst[:, :], ACT.Copy, scale=-1.0).then_inc(S["act_const"], 1)
            act.wait_ge(S["dve_const"], 1)

            def evac_k(n):
                wait(act, "k_tr", n + 1)
                for h in range(2):
                    c = nc.scalar.activation(kb[:, 2 * h:2 * h + 2, 1:PAD], T[h][:, :].rearrange("p (g t) -> p g t", g=2), ACT.Copy)
                c.then_inc(S["kb_ready"], 1)

            def tanh(j, m):
                w = SC[m][1]
                wait(act, "up_done", 6 * j + m + 1)
                nc.scalar.activation(th[0:w, m % 2, :], UP[m % 2][0:w, 0:SEQ], ACT.Tanh, scale=0.5).then_inc(S["th_ready"], 1)

            def step(i):
                some = not (isinstance(i, int) and i == 0)
                last = isinstance(i, int) and i == BATCH - 1
                wait(act, "d1_ready", i + 1)
                for g in range(DC):
                    c = nc.scalar.activation(e1b[:, g, 1:PAD], d1[:, g, :], ACT.Exp, bias=wdec[:, g:g + 1])
                c.then_inc(S["decay_ready"], 1)
                if some:
                    tanh(i - 1, 0)
                wait(act, "d2_ready", i + 1)
                nc.scalar.activation(e2b[:, :, 1:PAD], d2[:, :, :], ACT.Exp).then_inc(S["inject_ready"], 1)
                wait(act, "d3_ready", i + 1)
                for g in range(DC):
                    c = nc.scalar.activation(e1[:, g, :], d3[:, g, :], ACT.Relu, bias=ufirst[:, g:g + 1], scale=-1.0)
                c.then_inc(S["act_const"], 1)
                if some:
                    tanh(i - 1, 1)
                for g in range(DC):
                    c = nc.scalar.activation(d3[:, g, :], d3[:, g, :], ACT.Relu, bias=nufirst[:, g:g + 1])
                c.then_inc(S["act_const"], 1)
                wait(act, "act_const", 2 * i + 3)
                nc.scalar.activation(e1[:, :, :], e1[:, :, :], ACT.Exp, scale=-1.0).then_inc(S["e1_ready"], 1)
                wait(act, "act_const", 2 * i + 4)
                nc.scalar.activation(d3[:, :, :], d3[:, :, :], ACT.Exp, scale=-1.0).then_inc(S["e2_ready"], 1)
                if some:
                    for m in range(2, 6):
                        tanh(i - 1, m)
                wait(act, "h_tr", i + 1)
                for h in range(2):
                    c = nc.scalar.activation(hT[:, 2 * h:2 * h + 2, :], T[h][:, :].rearrange("p (g t) -> p g t", g=2), ACT.Copy)
                c.then_inc(S["hT_ready"], 1)
                if not last:
                    evac_k(i + 1)
                wait(act, "mx_ready", i + 1)
                for t in range(NT):
                    c = nc.scalar.activation(ex[:, t, :], logits[:, t, :], ACT.Exp, bias=nmx[:, t:t + 1], accum_out=ssum[:, t:t + 1])
                c.then_inc(S["ex_ready"], 1)
                wait(act, "ovf_tr", i + 1)
                for t in range(NT):
                    c = nc.scalar.activation(ovfT[:, bass.ds((i * NT + t) * P, P)], ovf_ps[t * EXP:(t + 1) * EXP, :], ACT.Copy)
                c.then_inc(S["ovfT_ready"], 1)

            evac_k(0)
            front_steps(act, step)

            def whi(e, s, k):
                wait(act, f"wgu_in{s}", 16 * (nth(e, s) + 1))
                wait(act, "gu_done", 3 * (e - 1))
                nc.scalar.activation(whi_gu[s][:, k, :], raw_gu[s][:, k, :], ACT.Copy).then_inc(S["whi_gu_done"], 1)

            def whid(e, s):
                wait(act, f"wd_in{s}", 32 * (nth(e, s) + 1))
                wait(act, "o_done", e - 1)
                nc.scalar.activation(whi_d[s][:, 0:2, :], raw_d[s][:, 0:2, :], ACT.Copy)
                w = MC[2][1]
                nc.scalar.activation(whi_d[s][0:w, 2, :], raw_d[s][0:w, 2, :], ACT.Copy).then_inc(S["whi_d_done"], 1)

            def take_x(e, s):
                wait(act, "x_tr", e + 1)
                for h in range(2):
                    nc.scalar.activation(xhi[s][:, 2 * h:2 * h + 2, :], XT[h][:, 0:2 * CAP].rearrange("p (g c) -> p g c", g=2), ACT.Copy)
                wait(act, "rows_done", e - 1)
                nc.scalar.activation(wcol[s][:, 0:1], xg[s][:, 0, bass.ds(e + D, 1)], ACT.Copy)
                nc.scalar.activation(wcol[s][:, 1:2], xg[s][:, 1, bass.ds(e + D, 1)], ACT.Identity, bias=is_last[:, :],
                                     scale=not_last[:, :]).then_inc(S["xhi_done"], 1)

            def silu(e, s, c):
                w = MC[c][1]
                b = (s + c) % 2
                wait(act, "gu_done", 3 * e + c + 1)
                wait(act, "mul_done", 3 * e + c - 1)
                nc.scalar.activation(sil[0:w, b, :], GU[b][0:w, 0:CAP], ACT.Silu).then_inc(S["sil_done"], 1)

            def weigh(e, s):
                wait(act, "r_tr", e + 1)
                wait(act, "added", 32 * (e - 1))
                for h in range(2):
                    c = nc.scalar.activation(rows[s][:, h, :], RW[h][0:HALF, :], ACT.Copy, scale=wcol[s][:, h:h + 1])
                c.then_inc(S["rows_done"], 1)

            tanh(BATCH - 1, 0)
            tanh(BATCH - 1, 1)
            act.wait_ge(S["tables_ready"], 1)
            for m in range(2, 6):
                whi(0, 0, m - 2)
                tanh(BATCH - 1, m)
            whid(0, 0)
            take_x(0, 0)
            act.wait_ge(S["y_evac"], NT * BATCH)

            def expert(e, s):
                some = not (isinstance(e, int) and e == 0)
                last = isinstance(e, int) and e == EXP - 1
                if not last:
                    whi(e + 1, 1 - s, 0)
                silu(e, s, 0)
                if not last:
                    whi(e + 1, 1 - s, 1)
                silu(e, s, 1)
                if not last:
                    whi(e + 1, 1 - s, 2)
                silu(e, s, 2)
                if some:
                    weigh(e - 1, 1 - s)
                if not last:
                    take_x(e + 1, 1 - s)
                    whi(e + 1, 1 - s, 3)
                    whid(e + 1, 1 - s)
                wait(act, "o_done", e + 1)
                for h in range(2):
                    c = nc.scalar.activation(oT[:, 2 * h:2 * h + 2, :], OT[h][:, 0:2 * CAP].rearrange("p (g c) -> p g c", g=2), ACT.Copy)
                c.then_inc(S["oT_done"], 1)

            expert_steps(act, expert)
            weigh(EXP - 1, 1)

        @block.vector
        def _(dve):
            V = nc.vector
            steps = [0, 0]

            def count(i, n):
                return i * steps[0] + n

            dve.wait_ge(S["consts"], 1)
            V.memset(wrep[:, :, :], 1.0).then_inc(S["dve_step"], 1)
            V.memset(kb[:, :, 0:1], NEG)
            V.memset(e1b[:, :, 0:1], 0.0)
            V.memset(e2b[:, :, 0:1], 0.0)
            V.memset(e2bv[:, :, 0:1], 0.0)
            V.memset(cum[:, :], 0.0)
            V.memset(lastt[:, :], 0.0).then_inc(S["dve_step"], 1)
            dve.wait_ge(S["act_const"], 2)
            V.tensor_scalar(wdec[:, :], wdec[:, :], -1.0, None, ALU.mult).then_inc(S["dve_step"], 1)
            V.tensor_copy(iota_c[:, :], iota_ci[:, :]).then_inc(S["dve_step"], 1)
            dve.wait_ge(S["dve_step"], 4)
            V.memset(iota_c[:, CAP - 1:CAP], -1.0)
            for g in range(DC):
                V.tensor_scalar(wrep[:, g, 1:PAD], wrep[:, g, 1:PAD], wdec[:, g:g + 1], None, ALU.mult)
            V.memset(wrep[:, :, 0:1], NEG).then_inc(S["dve_const"], 1)
            dve.wait_ge(S["dve_const"], 1)
            first_count = 4

            cur = [0, 0]

            def link(ins):
                cur[1] += 1
                ins.then_inc(S["dve_step"], 1)
                dve.wait_ge(S["dve_step"], first_count + chain_at(cur[0]) + cur[1])

            def chain_at(i):
                return 0 if isinstance(i, int) and i < 0 else HEAD + i * BODY

            HEAD, BODY = 1, 32

            def stats(n, mv, ready):
                hold(dve)
                for t in range(NT):
                    r = V.bn_stats(st6[:, t, :], xall[:, bass.ds(NT * n + t, 1), :].rearrange("p a d -> p (a d)"))
                link(r)
                hold(dve)
                for t in range(NT):
                    r = V.bn_aggr(mv[:, t, :], st6[:, t, :])
                r.then_inc(S[ready], 1)

            def normalise(n, to, mv, rstd, ready_in, ready):
                wait(dve, ready_in, n + 1)
                for t in range(NT):
                    r = V.tensor_scalar(to[:, t, 0:D], xall[:, bass.ds(NT * n + t, 1), :].rearrange("p a d -> p (a d)"),
                                        mv[:, t, 0:1], rstd[:, t:t + 1], ALU.subtract, ALU.mult)
                if ready:
                    r.then_inc(S[ready], 1)

            def product(j, m):
                w = SC[m][1]
                wait(dve, "th_ready", 6 * j + m + 1)
                V.scalar_tensor_tensor(th[0:w, m % 2, :], th[0:w, m % 2, :], 1.0, UP[m % 2][0:w, 0:SEQ], ALU.add, ALU.mult).then_inc(S["shid_done"], 1)
                wait(dve, "shid_done", 6 * j + m + 1)
                if m == 0:
                    wait(dve, "down_done", NT * j)
                V.scalar_tensor_tensor(shid[0:w, m, :], th[0:w, m % 2, :], 0.5, UP[m % 2][0:w, SEQ:2 * SEQ], ALU.mult, ALU.mult).then_inc(S["hid_done"], 1)

            def take_y(j, t):
                wait(dve, "down_done", NT * j + t + 1)
                xt = xall[:, bass.ds(NT * j + t, 1), :].rearrange("p a d -> p (a d)")
                V.tensor_tensor(xt, xt, DN[:, :], ALU.add).then_inc(S["y_evac"], 1)

            def flat(a):
                return a[:, :, :].rearrange("p g t -> p (g t)")

            def step(i):
                cur[0], cur[1] = i, 0
                some = not (isinstance(i, int) and i == 0)
                last = isinstance(i, int) and i == BATCH - 1
                ppcur, ppprev = pp[:, :, 1:PAD], pp[:, :, 0:SEQ]
                wait(dve, "kb_ready", i + 1)
                link(V.tensor_tensor_scan(flat(pp), flat(wrep), flat(kb), NEG, ALU.add, ALU.max))
                V.tensor_tensor(d1[:, :, :], ppprev, ppcur, ALU.subtract).then_inc(S["d1_ready"], 1)
                V.tensor_copy(st6[:, 0, 0:1], pid1[:, :]).then_inc(S["pp_ready"], 1)
                if some:
                    product(i - 1, 0)
                wait(dve, "decay_ready", i + 1)
                wait(dve, "inject_ready", i + 1)
                link(V.tensor_tensor_scan(flat(bb), flat(e1b), flat(e2b), 0.0, ALU.mult, ALU.add))
                if some:
                    product(i - 1, 1)
                wait(dve, "injv_ready", i + 1)
                link(V.tensor_tensor_scan(flat(aa), flat(e1b), flat(e2bv), 0.0, ALU.mult, ALU.add))
                if some:
                    product(i - 1, 2)
                wait(dve, "e1_ready", i + 1)
                link(V.tensor_tensor(d1[:, :, :], e1[:, :, :], bb[:, :, 0:SEQ], ALU.mult))
                wait(dve, "e2_ready", i + 1)
                link(V.tensor_tensor(d1[:, :, :], d1[:, :, :], d3[:, :, :], ALU.add))
                if some:
                    product(i - 1, 3)
                link(V.reciprocal(d1[:, :, :], d1[:, :, :]))
                link(V.tensor_tensor(e1[:, :, :], e1[:, :, :], aa[:, :, 0:SEQ], ALU.mult))
                wait(dve, "n2_ready", i + 1)
                link(V.tensor_tensor(e1[:, :, :], e1[:, :, :], d2[:, :, :], ALU.add))
                V.tensor_tensor(e1[:, :, :], e1[:, :, :], d1[:, :, :], ALU.mult).then_inc(S["yT_ready"], 1)
                if some:
                    product(i - 1, 4)
                wait(dve, "y_tr", i + 1)
                for t in range(NT):
                    xt = xall[:, bass.ds(NT * i + t, 1), :].rearrange("p a d -> p (a d)")
                    r = V.tensor_tensor(xt, xt, T[t][:, :], ALU.add)
                link(r)
                stats(i, mv2, "stat2")
                if some:
                    product(i - 1, 5)
                wait(dve, "hx_out", 16 * i)
                normalise(i, hx, mv2, rstd2, "rstd2_ready", "h_ready")
                if not last:
                    wait(dve, "x_in", 16 * (i + 2))
                    stats(i + 1, mv1, "stat1")
                    normalise(i + 1, kn, mv1, rstd1, "rstd1_ready", "kn_ready")
                else:
                    link(V.tensor_copy(st6[:, 0, 0:1], pid1[:, :]))
                if some:
                    take_y(i - 1, 0)
                wait(dve, "gate_done", i + 1)
                V.tensor_reduce(nmx[:, :], logits, AX.X, ALU.max, negate=True).then_inc(S["mx_ready"], 1)
                wait(dve, "ex_ready", i + 1)
                link(V.reciprocal(rsum[:, :], ssum[:, :]))
                link(V.tensor_tensor(ex[:, :, :], ex[:, :, :], rsum[:, :].unsqueeze(2).to_broadcast([P, NT, EXP]), ALU.mult))
                link(V.tensor_reduce(gm[:, :, :], ex[:, :, :].rearrange("p t (g j) -> p t g j", g=GROUPS), AX.X, ALU.max))
                for t in range(NT):
                    other = gm[:, t, :].unsqueeze(1).to_broadcast([P, GROUPS, GROUPS])
                    own = gm[:, t, :].unsqueeze(2).to_broadcast([P, GROUPS, GROUPS])
                    V.tensor_tensor(ggt[:, t], other, own, ALU.is_gt)
                    r = V.tensor_tensor(geq[:, t], other, own, ALU.is_equal)
                link(r)
                link(V.tensor_tensor(geq[:], geq[:], tri[:, :, :].unsqueeze(1).to_broadcast([P, NT, GROUPS, GROUPS]), ALU.mult))
                link(V.tensor_tensor(ggt[:], ggt[:], geq[:], ALU.add))
                link(V.tensor_reduce(gcnt[:, :, :], ggt[:], AX.X, ALU.add))
                link(V.tensor_scalar(gcnt[:, :, :], gcnt[:, :, :], float(TOPG), None, ALU.is_lt))
                link(V.tensor_tensor(tmp[:, :, :].rearrange("p t (g j) -> p t g j", g=GROUPS),
                                     ex[:, :, :].rearrange("p t (g j) -> p t g j", g=GROUPS),
                                     gcnt[:, :, :].unsqueeze(3).to_broadcast([P, NT, GROUPS, GE]), ALU.mult))
                hold(dve)
                for t in range(NT):
                    r = V.max(v8[:, t, :], tmp[:, t, :])
                link(r)
                hold(dve)
                for t in range(NT):
                    r = V.max_index(i8[:, t, :], v8[:, t, :], tmp[:, t, :])
                link(r)
                link(V.tensor_copy(i6[:, :, :], i8[:, :, 0:TOPK]))
                for t in range(NT):
                    r = V.tensor_tensor(eq6[:, t], iota_e[:, :].unsqueeze(1).to_broadcast([P, TOPK, EXP]),
                                        i6[:, t, :].unsqueeze(2).to_broadcast([P, TOPK, EXP]), ALU.is_equal)
                link(r)
                link(V.tensor_reduce(mask[:, :, :], eq6[:].rearrange("p t j e -> p t e j"), AX.X, ALU.add))
                V.tensor_copy(maskb[:, :, :], mask[:, :, :]).then_inc(S["mask_ready"], 1)
                V.tensor_tensor(hx[:, :, D:HX], mask[:, :, :], tmp[:, :, :], ALU.mult).then_inc(S["hx_ready"], 1)
                for t in range(NT):
                    link(V.scalar_tensor_tensor(lastt[:, 0:EXP], mask[:, t, :], tokid[:, t:t + 1], lastt[:, 0:EXP], ALU.mult, ALU.max))
                wait(dve, "pos_done", i + 1)
                for t in range(NT):
                    r = V.tensor_tensor(pe6[:, t], eq6[:, t], pos[:, t, :].unsqueeze(1).to_broadcast([P, TOPK, EXP]), ALU.mult)
                link(r)
                link(V.tensor_reduce(posel[:, :, :], pe6[:], AX.X, ALU.add))
                wait(dve, "hx_ready", i + 1)
                V.scalar_tensor_tensor(ovf[:, :, :], pos, float(CAP - 1), hx[:, :, D:HX], ALU.is_ge, ALU.mult).then_inc(S["ovf_ready"], 1)
                for t in range(NT):
                    link(V.tensor_tensor(cum[:, :], cum[:, :], maskb[:, t, :], ALU.add))
                for t in range(NT):
                    for j in range(TOPK):
                        V.tensor_scalar(slot1h[:, t, j, :], iota_c[:, :], posel[:, t, j:j + 1], None, ALU.is_equal)
                    V.tensor_scalar(val1h[:, t, :, 0:EXP], eq6[:, t], pid1[:, :], None, ALU.mult)
                    r = V.tensor_scalar(val1h[:, t, :, EXP:2 * EXP], eq6[:, t], tileno[:, t:t + 1], None, ALU.mult)
                r.then_inc(S["onehot_ready"], 1)
                wait(dve, "onehot_ready", i + 1)
                V.tensor_scalar(tokid[:, :], tokid[:, :], float(SEQ), None, ALU.add)
                link(V.tensor_scalar(tileno[:, :], tileno[:, :], float(NT), None, ALU.add))
                if some:
                    take_y(i - 1, 1)
                COUNTS.append(cur[1])

            COUNTS = []
            cur[0], cur[1] = -1, 0
            dve.wait_ge(S["x_in"], 16)
            stats(0, mv1, "stat1")
            normalise(0, kn, mv1, rstd1, "rstd1_ready", "kn_ready")
            while cur[1] < HEAD:
                link(V.tensor_copy(st6[:, 0, 0:1], pid1[:, :]))
            front_steps(dve, step)
            assert set(COUNTS) == {BODY}, COUNTS

            n0 = first_count + HEAD + BATCH * BODY
            m0 = [0]

            def tail_link(ins):
                m0[0] += 1
                ins.then_inc(S["dve_step"], 1)
                dve.wait_ge(S["dve_step"], n0 + m0[0])

            V.tensor_copy(st6[:, 0, 0:1], pid1[:, :]).then_inc(S["last_ready"], 1)
            dve.wait_ge(S["tab_done"], BATCH)
            for h in range(2):
                r = V.tensor_copy(tabs[:, h, :], TAB[h][0:HALF, 0:2 * EXP])
            tail_link(r)
            for h in range(2):
                tail_link(V.scalar_tensor_tensor(tval[:, h, :], tabs[:, h, EXP:2 * EXP], float(P), tabs[:, h, 0:EXP], ALU.mult, ALU.add))
                tail_link(V.tensor_scalar(tz[:, h, :], tval[:, h, :], 0.0, None, ALU.is_equal))
                tail_link(V.scalar_tensor_tensor(tval[:, h, :], tz[:, h, :], unused[:, h:h + 1], tval[:, h, :], ALU.mult, ALU.add))
                tail_link(V.tensor_scalar(tval[:, h, :], tval[:, h, :], -1.0, None, ALU.add))
            V.tensor_copy(gtab[0][:, :], tval[:, 0, :])
            dve.wait_ge(S["last_tr"], 1)
            tail_link(V.tensor_reduce(lcol[:, :], G[0:EXP, 3 * P:4 * P], AX.X, ALU.max))
            V.tensor_copy(lmat[:, HALF - 1:HALF], lcol[:, :]).then_inc(S["lmat_ready"], 1)
            tail_link(V.tensor_scalar(tval[:, 1, :], tval[:, 1, :], not_last[:, :], None, ALU.mult))
            tail_link(V.scalar_tensor_tensor(tz[:, 1, :], lastr[:, :], is_last[:, :], tval[:, 1, :], ALU.mult, ALU.add))
            V.tensor_copy(stab[:, :], tz[:, 1, :])
            dve.wait_ge(S["lastr_done"], 1)
            V.tensor_tensor(gtab[1][:, :], tval[:, 1, :], T[0][0:HALF, 0:EXP], ALU.add).then_inc(S["tables_ready"], 1)

            def wlo(e, s, k):
                wait(dve, "whi_gu_done", DC * e + k + 1)
                V.tensor_tensor(wlo_gu[s][:, k, :], raw_gu[s][:, k, :], whi_gu[s][:, k, :].bitcast(F32), ALU.subtract).then_inc(S["wlo_gu_done"], 1)

            def wlod(e, s):
                wait(dve, "whi_d_done", e + 1)
                V.tensor_tensor(wlo_d[s][:, 0:2, :], raw_d[s][:, 0:2, :], whi_d[s][:, 0:2, :].bitcast(F32), ALU.subtract)
                w = MC[2][1]
                V.tensor_tensor(wlo_d[s][0:w, 2, :], raw_d[s][0:w, 2, :], whi_d[s][0:w, 2, :].bitcast(F32), ALU.subtract).then_inc(S["wlo_d_done"], 1)

            def xrest(e, s):
                wait(dve, "xhi_done", e + 1)
                for h in range(2):
                    r = V.tensor_tensor(xlo[s][:, 2 * h:2 * h + 2, :], XT[h][:, 0:2 * CAP].rearrange("p (g c) -> p g c", g=2),
                                        xhi[s][:, 2 * h:2 * h + 2, :].bitcast(F32), ALU.subtract)
                r.then_inc(S["xlo_done"], 1)

            def hidden(e, s, c):
                w = MC[c][1]
                b = (s + c) % 2
                wait(dve, "sil_done", 3 * e + c + 1)
                V.tensor_tensor(hid[0:w, b, :], sil[0:w, b, :], GU[b][0:w, CAP:2 * CAP], ALU.mult).then_inc(S["mul_done"], 1)
                wait(dve, "mul_done", 3 * e + c + 1)
                V.tensor_copy(hhi[0:w, c, :], hid[0:w, b, :]).then_inc(S["hhi_done"], 1)
                wait(dve, "hhi_done", 3 * e + c + 1)
                V.tensor_tensor(hlo[0:w, c, :], hid[0:w, b, :], hhi[0:w, c, :].bitcast(F32), ALU.subtract).then_inc(S["hlo_done"], 1)

            product(BATCH - 1, 0)
            product(BATCH - 1, 1)
            for m in range(2, 6):
                wlo(0, 0, m - 2)
                product(BATCH - 1, m)
            wlod(0, 0)
            for t in range(NT):
                take_y(BATCH - 1, t)
            xrest(0, 0)

            def expert(e, s):
                last = isinstance(e, int) and e == EXP - 1
                for c in range(3):
                    if not last:
                        wlo(e + 1, 1 - s, c)
                    hidden(e, s, c)
                if not last:
                    xrest(e + 1, 1 - s)
                    wlo(e + 1, 1 - s, 3)
                    wlod(e + 1, 1 - s)

            expert_steps(dve, expert)

            for n in range(BATCH * NT):
                if n % NT == 0:
                    dve.wait_ge(y_back[n // NT], 16)
                dve.wait_ge(S["fin_ps"], n + 1)
                V.tensor_tensor(xall[:, n, :], xall[:, n, :], psum[n % 8][:, :], ALU.add).then_inc(S["fin_add"], 1)

        @block.tensor
        def _(pe):
            mm, tr = nc.tensor.matmul, nc.tensor.transpose

            def transpose_in(src, done):
                for g in range(DC):
                    for t in range(NT):
                        r = tr(T[g // 2][:, (g % 2) * SEQ + t * P:(g % 2) * SEQ + (t + 1) * P], src[:, t, g * P:(g + 1) * P], ident[:, :])
                r.then_inc(S[done], 1)

            def up(j, m):
                m0, w = SC[m]
                wait(pe, "hid_done", 6 * j + m - 1)
                for q in range(2):
                    for k in range(DC):
                        r = mm(UP[m % 2][0:w, q * SEQ:(q + 1) * SEQ], sgu_sb[:, k, q * MS + m0:q * MS + m0 + w], hT[:, k, :],
                               start=(k == 0), stop=(k == DC - 1))
                r.then_inc(S["up_done"], 1)

            def down(j, t):
                if t == 0:
                    wait(pe, "hid_done", 6 * (j + 1))
                wait(pe, "y_evac", NT * j + t)
                for m, (m0, w) in enumerate(SC):
                    r = mm(DN[:, :], shid[0:w, m, t * P:(t + 1) * P], sd_sb[0:w, m, :], start=(m == 0), stop=(m == len(SC) - 1))
                r.then_inc(S["down_done"], 1)

            def step(i):
                some = not (isinstance(i, int) and i == 0)
                first, last = not some, isinstance(i, int) and i == BATCH - 1
                if some:
                    for m in range(5):
                        up(i - 1, m)
                wait(pe, "yT_ready", i + 1)
                for t in range(NT):
                    for g in range(DC):
                        r = tr(T[t][:, g * P:(g + 1) * P], e1[:, g, t * P:(t + 1) * P], ident[:, :])
                r.then_inc(S["y_tr"], 1)
                if some:
                    up(i - 1, 5)
                wait(pe, "h_ready", i + 1)
                transpose_in(hx, "h_tr")
                if some:
                    down(i - 1, 0)
                wait(pe, "hT_ready", i + 1)
                wait(pe, "ovfT_ready", i)
                for t in range(NT):
                    for k in range(DC):
                        r = mm(logits[:, t, :], hT[:, k, t * P:(t + 1) * P], gate_sb[:, k, :], start=(k == 0), stop=(k == DC - 1))
                r.then_inc(S["gate_done"], 1)
                if not last:
                    wait(pe, "kn_ready", i + 2)
                    transpose_in(kn, "k_tr")
                wait(pe, "mask_ready", i + 1)
                for t in range(NT):
                    mm(pos[:, t, :], ones[:, :], cum[:, :], start=True, stop=False)
                    if t:
                        mm(pos[:, t, :], ones[:, :], maskb[:, 0, :], start=False, stop=False)
                    r = mm(pos[:, t, :], lstrict[:, :], maskb[:, t, :], start=False, stop=True)
                r.then_inc(S["pos_done"], 1)
                if some:
                    down(i - 1, 1)
                wait(pe, "ovf_ready", i + 1)
                tr(ovf_ps, ovf[:, :, :].rearrange("p t e -> p (t e)"), ident[:, :]).then_inc(S["ovf_tr"], 1)
                wait(pe, "onehot_ready", i + 1)
                for h in range(2):
                    for t in range(NT):
                        for j in range(TOPK):
                            r = mm(TAB[h][0:HALF, 0:2 * EXP], slot1h[:, t, j, h * HALF:(h + 1) * HALF], val1h[:, t, j, :],
                                   start=(first and t == 0 and j == 0), stop=(last and t == NT - 1 and j == TOPK - 1))
                r.then_inc(S["tab_done"], 1)

            wait(pe, "consts", 1)
            wait(pe, "kn_ready", 1)
            transpose_in(kn, "k_tr")
            pe.wait_ge(S["gate_in"], 16)
            pe.wait_ge(S["shared_w"], 16)
            pe.wait_ge(S["shared_d"], 32)
            front_steps(pe, step)
            wait(pe, "ovfT_ready", BATCH)
            wait(pe, "last_ready", 1)
            tr(G[:, 3 * P:4 * P], lastt[:, :], ident[:, :]).then_inc(S["last_tr"], 1)
            wait(pe, "lmat_ready", 1)
            mm(T[0][0:HALF, 0:EXP], lmat[:, :], ident[0:EXP, 0:EXP], start=True, stop=True).then_inc(S["lastr_done"], 1)
            for m in range(6):
                up(BATCH - 1, m)
            for t in range(NT):
                down(BATCH - 1, t)

            def bring_x(e, s):
                wait(pe, f"gathered{s}", 32 * (nth(e, s) + 1))
                wait(pe, "xlo_done", e)
                for k in range(DC):
                    for h in range(2):
                        at = (k % 2) * CAP + h * HALF
                        r = tr(XT[k // 2][:, at:at + HALF], xg[s][:, h, k * P:(k + 1) * P], ident[0:HALF, 0:HALF])
                r.then_inc(S["x_tr"], 1)

            def gate_up(e, s, c):
                m0, w = MC[c]
                b = (s + c) % 2
                if c == 0:
                    wait(pe, "xlo_done", e + 1)
                    wait(pe, "wlo_gu_done", DC * (e + 1))
                wait(pe, "mul_done", 3 * e + c - 1)
                for q in range(2):
                    for k in range(DC):
                        col = slice(q * M + m0, q * M + m0 + w)
                        for n, (a, z) in enumerate(((whi_gu, xhi), (whi_gu, xlo), (wlo_gu, xhi))):
                            r = mm(GU[b][0:w, q * CAP:(q + 1) * CAP], a[s][:, k, col], z[s][:, k, :],
                                   start=(k == 0 and n == 0), stop=(k == DC - 1 and n == 2))
                r.then_inc(S["gu_done"], 1)

            def down_rows(e, s):
                wait(pe, "hlo_done", 3 * (e + 1))
                wait(pe, "wlo_d_done", e + 1)
                wait(pe, "oT_done", e)
                for g in range(DC):
                    o = OT[g // 2][:, (g % 2) * CAP:(g % 2 + 1) * CAP]
                    for c, (m0, w) in enumerate(MC):
                        for n, (a, z) in enumerate(((whi_d, hhi), (whi_d, hlo), (wlo_d, hhi))):
                            r = mm(o, a[s][0:w, c, g * P:(g + 1) * P], z[0:w, c, :],
                                   start=(c == 0 and n == 0), stop=(c == len(MC) - 1 and n == 2))
                r.then_inc(S["o_done"], 1)

            def rows_out(e, s):
                wait(pe, "oT_done", e + 1)
                wait(pe, "rows_done", e)
                for g in range(DC):
                    for h in range(2):
                        r = tr(RW[h][0:HALF, g * P:(g + 1) * P], oT[:, g, h * HALF:(h + 1) * HALF], ident[:, :])
                r.then_inc(S["r_tr"], 1)

            pe.wait_ge(S["tables_ready"], 1)
            bring_x(0, 0)

            def expert(e, s):
                for c in range(3):
                    gate_up(e, s, c)
                if not (isinstance(e, int) and e == 0):
                    rows_out(e - 1, 1 - s)
                if not (isinstance(e, int) and e == EXP - 1):
                    bring_x(e + 1, 1 - s)
                down_rows(e, s)

            expert_steps(pe, expert)
            rows_out(EXP - 1, 1)

            pe.wait_ge(S["fin_last"], 16)
            for n in range(BATCH * NT):
                if n >= 8:
                    pe.wait_ge(S["fin_add"], n - 7)
                mm(psum[n % 8][:, :], ovfT[:, n * P:(n + 1) * P], last_out[:, :], start=True, stop=True).then_inc(S["fin_ps"], 1)


def kernel(x, ctx_2048, L0_xattn_time_decay, L0_xattn_time_first, L0_ffn_gate_weight, L0_ffn_Wg, L0_ffn_Wu,
           L0_ffn_Wd, L0_ffn_Sg, L0_ffn_Su, L0_ffn_Sd):
    import numpy as np
    import concourse.bacc as bacc
    from concourse.bass_utils import run_bass_kernel_spmd

    def put(a):
        return np.ascontiguousarray(a)

    def contract_first(w):
        w = np.asarray(w)
        w = w.reshape(w.shape[:-1] + (DC, P))
        return np.moveaxis(w, (-1, -2), (-3, -2))

    arrays = {
        "x": put(x),
        "ctxv": put(contract_first(ctx_2048)),
        "decay": put(np.asarray(L0_xattn_time_decay).reshape(DC, P).T),
        "first": put(np.asarray(L0_xattn_time_first).reshape(DC, P).T),
        "gate": put(contract_first(L0_ffn_gate_weight)),
        "wgu": put(np.concatenate([contract_first(L0_ffn_Wg), contract_first(L0_ffn_Wu)], axis=-1)),
        "wd": put(np.swapaxes(np.asarray(L0_ffn_Wd), 1, 2)),
        "sgu": put(np.concatenate([contract_first(L0_ffn_Sg), contract_first(L0_ffn_Su)], axis=-1)),
        "sd": put(np.asarray(L0_ffn_Sd).T),
    }
    nc = bacc.Bacc("TRN2", target_bir_lowering=False, num_devices=1)
    args = [nc.dram_tensor(f"in_{n}", a.shape, mybir.dt.from_np(a.dtype), kind="ExternalInput").ap() for n, a in arrays.items()]
    args.append(nc.dram_tensor("out_0", (BATCH, SEQ, D), F32, kind="ExternalOutput").ap())
    build(nc, *args)
    r = run_bass_kernel_spmd(nc, [{f"in_{n}": a for n, a in arrays.items()}], core_ids=[0])
    return r.results[0]["out_0"]
```

```python
import concourse.bass as bass
from concourse import mybir
from contextlib import ExitStack

F32, F32R, BF16, U32 = (mybir.dt.float32, mybir.dt.float32r, mybir.dt.bfloat16, mybir.dt.uint32)
ALU = mybir.AluOpType
ACT = mybir.ActivationFunctionType
AX = mybir.AxisListType

P = 128
BATCH, SEQ, D = 8, 256, 512
TOK = BATCH * SEQ
NT = SEQ // P
DC = D // P
EXP, M, CAP = 64, 352, 192
GROUPS, TOPG, TOPK = 8, 3, 6
GE = EXP // GROUPS
HALF = CAP // 2
MS = 704
MC = [(m, min(P, M - m)) for m in range(0, M, P)]
SC = [(m, min(P, MS - m)) for m in range(0, MS, P)]
EPS = 1e-5
NEG = -1e38
WKV_LINKS, ROUTE_LINKS = 5, 21
LAST_ROW = TOK
DUMP_ROW = TOK + EXP
ROWS = DUMP_ROW + CAP
HX = D + EXP
PAD = SEQ + 1


def build(nc, x, ctxv, decay, first, gate, wgu, wd, sgu, sd, out):
    hx_dram = nc.dram_tensor("hx_rows", (ROWS, HX), F32, kind="Internal").ap()
    y_dram = nc.dram_tensor("y_rows", (ROWS, D), F32, kind="Internal").ap()

    ctx = ExitStack()
    with ctx:
        def in_stack(stack):
            return lambda name, shape, dt=F32: stack.enter_context(nc.sbuf_tensor(name, shape, dt))

        def sem(name):
            return ctx.enter_context(nc.semaphore(name))

        sb = in_stack(ctx)
        psum = [ctx.enter_context(nc.psum_tensor(f"bank{i}", [P, 512], F32)) for i in range(8)]

        ident = sb("ident", [P, P])
        gtab = [sb(f"gather_ids{h}", [HALF, EXP], U32) for h in range(2)]
        stab = sb("scatter_ids1", [HALF, EXP], U32)
        last_slot = sb("last_slot", [HALF, 1])
        not_last = sb("not_last", [HALF, 1])
        xall = sb("xall", [P, BATCH * NT, D])
        ovfT = sb("ovfT", [EXP, TOK])
        raw_gu = [sb(f"raw_gu{s}", [P, DC, 2 * M]) for s in range(2)]
        raw_d = [sb(f"raw_d{s}", [P, len(MC), D]) for s in range(2)]

        shared_stack = ExitStack()
        sbs = in_stack(shared_stack)
        base_shared = nc.sbuf_base
        sgu_sb = sbs("sgu_sb", [P, DC, 2 * MS])
        sd_sb = sbs("sd_sb", [P, len(SC), D])
        shid = sbs("shid", [P, len(SC), SEQ])
        th = sbs("th", [P, 2, SEQ])
        hT = sbs("hT", [P, DC, SEQ])
        base_front = nc.sbuf_base

        front_stack = ExitStack()
        sbf = in_stack(front_stack)
        kn = sbf("kn", [P, NT, D])
        kb = sbf("kb", [P, DC, PAD])
        v = sbf("v", [P, DC, SEQ])
        wrep = sbf("wrep", [P, DC, PAD])
        pp = sbf("pp", [P, DC, PAD])
        d1 = sbf("d1", [P, DC, SEQ])
        d2 = sbf("d2", [P, DC, SEQ])
        d3 = sbf("d3", [P, DC, SEQ])
        e1 = sbf("e1", [P, DC, SEQ])
        e1b = sbf("e1b", [P, DC, PAD])
        e2b = sbf("e2b", [P, DC, PAD])
        e2bv = sbf("e2bv", [P, DC, PAD])
        aa = sbf("aa", [P, DC, PAD])
        bb = sbf("bb", [P, DC, PAD])
        hx = sbf("hx", [P, NT, D])
        gw = sbf("gw", [P, NT, EXP])
        gate_sb = sbf("gate_sb", [P, DC, EXP])
        wdec = sbf("wdec", [P, DC])
        ufirst = sbf("ufirst", [P, DC])
        nufirst = sbf("nufirst", [P, DC])
        st6 = sbf("st6", [P, NT, 6])
        mv1 = sbf("mv1", [P, NT, 2])
        mv2 = sbf("mv2", [P, NT, 2])
        ve = sbf("ve", [P, NT])
        rstd1 = sbf("rstd1", [P, NT])
        shift1 = sbf("shift1", [P, NT])
        shift2 = sbf("shift2", [P, NT])
        nmean = sbf("nmean", [P, NT])
        mone = sbf("mone", [P, NT])
        rstd2 = sbf("rstd2", [P, NT])
        eps_t = sbf("eps_t", [P, NT])
        mhalf = sbf("mhalf", [P, NT])
        lstrict = sbf("lstrict", [P, P], BF16)
        ones = sbf("ones", [P, P], BF16)
        iota_e = sbf("iota_e", [P, EXP])
        iota_ci = sbf("iota_ci", [P, CAP])
        iota_c = sbf("iota_c", [P, CAP], BF16)
        tri = sbf("tri", [P, GROUPS, GROUPS])
        pid1 = sbf("pid1", [P, 1])
        tokid = sbf("tokid", [P, NT])
        tileno = sbf("tileno", [P, NT])
        nmx = sbf("nmx", [P, NT])
        ssum = sbf("ssum", [P, NT])
        rsum = sbf("rsum", [P, NT])
        ex = sbf("ex", [P, NT, EXP])
        gm = sbf("gm", [P, NT, GROUPS])
        ggt = sbf("ggt", [P, NT, GROUPS, GROUPS])
        geq = sbf("geq", [P, NT, GROUPS, GROUPS])
        gcnt = sbf("gcnt", [P, NT, GROUPS])
        tmp = sbf("tmp", [P, NT, EXP])
        v8 = sbf("v8", [P, NT, 8])
        i8 = sbf("i8", [P, NT, 8], U32)
        i6 = sbf("i6", [P, NT, TOPK])
        eq6 = sbf("eq6", [P, NT, TOPK, EXP], BF16)
        pe6 = sbf("pe6", [P, NT, TOPK, EXP])
        mask = sbf("mask", [P, NT, EXP])
        maskb = sbf("maskb", [P, NT, EXP], BF16)
        cum = sbf("cum", [P, EXP], BF16)
        lastt = sbf("lastt", [P, P])
        posel = sbf("posel", [P, NT, TOPK])
        ovf = sbf("ovf", [P, NT, EXP])
        slot1h = sbf("slot1h", [P, NT, TOPK, CAP], BF16)
        val1h = sbf("val1h", [P, NT, TOPK, 2 * EXP], BF16)
        tabs = sbf("tabs", [HALF, 2, 2 * EXP])
        tval = sbf("tval", [HALF, 2, EXP])
        tz = sbf("tz", [HALF, 2, EXP])
        unused = sbf("unused", [HALF, 2])
        lastr = sbf("lastr", [HALF, EXP])
        lcol = sbf("lcol", [EXP, 1])
        lmat = sbf("lmat", [EXP, HALF])
        zrow = sbf("zrow", [P, HX])
        front_top = nc.sbuf_base
        front_stack.close()
        shared_stack.close()

        whi_gu, wlo_gu, whi_d, wlo_d = [None] * 2, [None] * 2, [None] * 2, [None] * 2

        def weight_slot(s):
            whi_gu[s] = sb(f"whi_gu{s}", [P, DC, 2 * M], F32R)
            wlo_gu[s] = sb(f"wlo_gu{s}", [P, DC, 2 * M], F32R)
            whi_d[s] = sb(f"whi_d{s}", [P, len(MC), D], F32R)
            wlo_d[s] = sb(f"wlo_d{s}", [P, len(MC), D], F32R)

        weight_slot(1)
        assert base_shared < nc.sbuf_base <= base_front, (base_shared, nc.sbuf_base, base_front)
        if base_front > nc.sbuf_base:
            sb("gap", [P, base_front - nc.sbuf_base], mybir.dt.uint8)
        weight_slot(0)
        xg = [sb(f"xg{s}", [HALF, 2, HX]) for s in range(2)]
        xhi = [sb(f"xhi{s}", [P, DC, CAP], F32R) for s in range(2)]
        xlo = [sb(f"xlo{s}", [P, DC, CAP], F32R) for s in range(2)]
        wcol = [sb(f"wcol{s}", [HALF, 2]) for s in range(2)]
        sil = sb("sil", [P, 2, CAP])
        hid = sb("hid", [P, 2, CAP])
        hhi = sb("hhi", [P, len(MC), CAP], F32R)
        hlo = sb("hlo", [P, len(MC), CAP], F32R)
        oT = sb("oT", [P, DC, CAP])
        rows = [sb(f"rows{s}", [HALF, 2, D]) for s in range(2)]
        gi = [[sb(f"gi{s}{h}", [HALF, 1], U32) for h in range(2)] for s in range(2)]
        si = [[sb(f"si{s}{h}", [HALF, 1], U32) for h in range(2)] for s in range(2)]
        last_out = sb("last_out", [EXP, D])

        T = [psum[0], psum[1]]
        UP = [psum[2], psum[3]]
        DN = psum[4]
        G = psum[5]
        logits = G[:, 0:NT * EXP].rearrange("p (t e) -> p t e", t=NT)
        pos = G[:, P:P + NT * EXP].rearrange("p (t e) -> p t e", t=NT)
        ovf_ps = G[:, 2 * P:3 * P]
        TAB = [psum[6], psum[7]]
        XT = [psum[0], psum[1]]
        GU = [psum[2], psum[3]]
        OT = [psum[4], psum[5]]
        RW = [psum[6], psum[7]]

        names = """params x_in v_in gate_in shared_w shared_d zero_out h_out gw_out y_out consts dve_const act_const dve_step pool_step
            wkv_step route_step stats_step held relu_done
            stat1 rstd1_ready kn_ready k_tr kb_ready pp_ready d1_ready d2_ready d3_ready decay_ready inject_ready injv_ready
            e1_ready e2_ready n2_ready aa_ready num_ready den_ready ln_ready r0_ready t_ready yT_ready y_tr
            stat2 rstd2_ready h_ready h_tr hT_ready gate_done mx_ready ex_ready mask_ready gw_ready pos_done
            ovf_ready ovf_tr ovfT_ready onehot_ready tab_done
            up_done th_ready shid_done hid_done down_done y_evac
            last_ready last_tr lmat_ready lastr_done tables_ready
            wgu_in0 wgu_in1 wd_in0 wd_in1 whi_gu_done wlo_gu_done whi_d_done wlo_d_done
            gathered0 gathered1 gi_ready si_ready x_tr xhi_done xlo_done gu_done sil_done mul_done hhi_done hlo_done
            o_done oT_done r_tr rows_done added fin_last fin_ps fin_add fin_out"""
        S = {n: sem(n) for n in names.split()}
        y_back = [sem(f"y_back{b}") for b in range(BATCH)]

        def wait(eng, name, count):
            if not isinstance(count, int) or count > 0:
                eng.wait_ge(S[name], count)

        def hold(eng):
            eng.sem_inc(S["held"], 1)

        block = ctx.enter_context(nc.Block())

        def front_steps(eng, step, end=1):
            step(0)
            step(1)
            with eng.Fori(2, BATCH - end) as i:
                step(i)
            for i in range(BATCH - end, BATCH):
                step(i)

        def is_first(i):
            return isinstance(i, int) and i == 0

        def is_last(i):
            return isinstance(i, int) and i == BATCH - 1

        def expert_steps(eng, step):
            for e in range(3):
                step(e, e % 2)
            with eng.Fori(1, EXP // 2 - 1) as t:
                step(2 * t + 1, 1)
                step(2 * t + 2, 0)
            step(EXP - 1, 1)

        def nth(e, s):
            return e // 2 if isinstance(e, int) else (e - s) // 2

        @block.sync
        def _(sp):
            sp.dma_start(wdec[:, :], decay).then_inc(S["params"], 16)
            sp.dma_start(ufirst[:, :], first).then_inc(S["params"], 16)
            def load_x(b):
                wait(sp, "x_in", 16 * b)
                sp.dma_start(xall[:, bass.ds(NT * b, NT), :],
                             x[bass.ds(b, 1)].rearrange("b (t p) d -> p (b t) d", p=P)).then_inc(S["x_in"], 16)

            def store_y(j):
                wait(sp, "y_evac", NT * (j + 1))
                sp.dma_start(y_dram[bass.ds(j * SEQ, SEQ), :].rearrange("(t p) d -> p t d", p=P),
                             xall[:, bass.ds(NT * j, NT), :]).then_inc(S["y_out"], 16)

            def store_gate(j):
                wait(sp, "gw_ready", j + 1)
                sp.dma_start(hx_dram[bass.ds(j * SEQ, SEQ), D:HX].rearrange("(t p) d -> p t d", p=P),
                             gw[:, :, :]).then_inc(S["gw_out"], 16)

            load_x(0)
            sp.dma_start(v[:, :, :], ctxv[0]).then_inc(S["v_in"], 16)
            load_x(1)
            sp.dma_start(gate_sb[:, :, :], gate).then_inc(S["gate_in"], 16)

            def step(i):
                if not (isinstance(i, int) and i >= BATCH - 2):
                    load_x(i + 2)
                if not is_last(i):
                    wait(sp, "n2_ready", i + 1)
                    sp.dma_start(v[:, :, :], ctxv[bass.ds(i + 1, 1)].rearrange("b p g t -> (b p) g t")).then_inc(S["v_in"], 16)
                if not is_first(i):
                    store_gate(i - 1)
                wait(sp, "h_ready", i + 1)
                sp.dma_start(hx_dram[bass.ds(i * SEQ, SEQ), 0:D].rearrange("(t p) d -> p t d", p=P),
                             hx[:, :, :]).then_inc(S["h_out"], 16)
                if not is_first(i):
                    store_y(i - 1)

            front_steps(sp, step, end=2)
            store_gate(BATCH - 1)
            store_y(BATCH - 1)

            def load(e, s):
                wait(sp, "wlo_gu_done", DC * (e - 1))
                sp.dma_start(raw_gu[s][:, :, :], wgu[bass.ds(e, 1)].rearrange("e p k m -> (e p) k m")).then_inc(S[f"wgu_in{s}"], 16)
                wait(sp, "wlo_d_done", e - 1)
                sp.dma_start(raw_d[s][:, 0:2, :], wd[bass.ds(e, 1), 0:2 * P, :].rearrange("e (c p) d -> p (e c) d", p=P)).then_inc(S[f"wd_in{s}"], 16)
                sp.dma_start(raw_d[s][0:MC[2][1], 2, :], wd[bass.ds(e, 1), 2 * P:M, :].rearrange("e p d -> (e p) d")).then_inc(S[f"wd_in{s}"], 16)

            load(2, 0)
            load(3, 1)
            with sp.Fori(2, EXP // 2) as t:
                load(2 * t, 0)
                load(2 * t + 1, 1)

            wait(sp, "added", 32 * EXP)
            sp.dma_start(last_out[:, :], y_dram[LAST_ROW:DUMP_ROW, :]).then_inc(S["fin_last"], 16)
            for b in range(BATCH):
                sp.dma_start(xall[:, NT * b:NT * (b + 1), :],
                             y_dram[b * SEQ:(b + 1) * SEQ, :].rearrange("(t p) d -> p t d", p=P)).then_inc(y_back[b], 16)
            for b in range(BATCH):
                wait(sp, "fin_add", NT * (b + 1))
                sp.dma_start(out[b].rearrange("(t p) d -> p t d", p=P), xall[:, NT * b:NT * (b + 1), :]).then_inc(S["fin_out"], 16)
            wait(sp, "fin_out", 16 * BATCH)
            wait(sp, "y_out", 16 * BATCH)
            wait(sp, "h_out", 16 * BATCH)
            wait(sp, "gw_out", 16 * BATCH)
            wait(sp, "zero_out", 64)

        @block.gpsimd
        def _(pool):
            nc.gpsimd.memset(ident[:, :], 0.0).then_inc(S["pool_step"], 1)
            nc.gpsimd.memset(ones[:, :], 1.0).then_inc(S["pool_step"], 1)
            nc.gpsimd.memset(tri[:, :, :], 1.0).then_inc(S["pool_step"], 1)
            nc.gpsimd.memset(last_slot[:, :], 0.0).then_inc(S["pool_step"], 1)
            nc.gpsimd.memset(not_last[:, :], 1.0).then_inc(S["pool_step"], 1)
            nc.gpsimd.memset(lmat[:, :], 0.0)
            nc.gpsimd.memset(zrow[:, :], 0.0).then_inc(S["pool_step"], 1)
            nc.gpsimd.memset(eps_t[:, :], EPS).then_inc(S["pool_step"], 1)
            nc.gpsimd.memset(mhalf[:, :], -0.5).then_inc(S["pool_step"], 1)
            nc.gpsimd.memset(mone[:, :], -1.0).then_inc(S["pool_step"], 1)
            pool.wait_ge(S["pool_step"], 9)
            nc.gpsimd.affine_select(out=ident[:, :], in_=ident[:, :], compare_op=ALU.not_equal, fill=1.0, base=0,
                                    pattern=[[-1, P]], channel_multiplier=1)
            nc.gpsimd.affine_select(out=lstrict[:, :], in_=ones[:, :], compare_op=ALU.is_gt, fill=0.0, base=0,
                                    pattern=[[1, P]], channel_multiplier=-1)
            nc.gpsimd.affine_select(out=tri[:, :, :], in_=tri[:, :, :], compare_op=ALU.is_gt, fill=0.0, base=0,
                                    pattern=[[1, GROUPS], [-1, GROUPS]], channel_multiplier=0)
            nc.gpsimd.affine_select(out=last_slot[:, :], in_=last_slot[:, :], compare_op=ALU.not_equal, fill=1.0,
                                    base=-(HALF - 1), pattern=[[0, 1]], channel_multiplier=1)
            nc.gpsimd.affine_select(out=not_last[:, :], in_=not_last[:, :], compare_op=ALU.not_equal, fill=0.0,
                                    base=-(HALF - 1), pattern=[[0, 1]], channel_multiplier=1)
            fl = dict(allow_small_or_imprecise_dtypes=True)
            nc.gpsimd.iota(iota_e[:, :], [[1, EXP]], base=0, channel_multiplier=0, **fl)
            nc.gpsimd.iota(iota_ci[:, :], [[1, CAP]], base=0, channel_multiplier=0, **fl)
            nc.gpsimd.iota(pid1[:, :], [[0, 1]], base=1, channel_multiplier=1, **fl)
            nc.gpsimd.iota(tokid[:, :], [[P, NT]], base=0, channel_multiplier=1, **fl)
            nc.gpsimd.iota(tileno[:, :], [[1, NT]], base=0, channel_multiplier=0, **fl)
            nc.gpsimd.iota(unused[:, :], [[HALF, 2]], base=DUMP_ROW + 1, channel_multiplier=1, **fl)
            nc.gpsimd.iota(lastr[:, :], [[1, EXP]], base=LAST_ROW, channel_multiplier=0, **fl).then_inc(S["consts"], 1)
            pool.wait_ge(S["consts"], 1)
            for r in range(TOK, ROWS, P):
                pool.dma_start(hx_dram[r:r + P, :], zrow[:, :]).then_inc(S["zero_out"], 16)
                pool.dma_start(y_dram[r:r + P, :], zrow[:, 0:D]).then_inc(S["zero_out"], 16)

            def norm(mv, rstd, shift, stat, ready, n, k):
                wait(pool, stat, n + 1)
                nc.gpsimd.tensor_tensor(nmean[:, :], mv[:, :, 0], mone[:, :], ALU.mult)
                nc.gpsimd.tensor_tensor(ve[:, :], mv[:, :, 1], eps_t[:, :], ALU.add).then_inc(S["pool_step"], 1)
                pool.wait_ge(S["pool_step"], 9 + 2 * k + 1)
                nc.gpsimd.tensor_tensor(rstd[:, :], ve[:, :], mhalf[:, :], ALU.pow).then_inc(S["pool_step"], 1)
                pool.wait_ge(S["pool_step"], 9 + 2 * k + 2)
                nc.gpsimd.tensor_tensor(shift[:, :], nmean[:, :], rstd[:, :], ALU.mult).then_inc(S[ready], 1)

            norm(mv1, rstd1, shift1, "stat1", "rstd1_ready", 0, 0)

            def step(i):
                kcur, ppcur, ppprev = kb[:, :, 1:PAD], pp[:, :, 1:PAD], pp[:, :, 0:SEQ]
                mul = lambda to, a, b: nc.gpsimd.tensor_tensor(to, a, b, ALU.mult)
                wait(pool, "pp_ready", i + 1)
                nc.gpsimd.tensor_tensor(d2[:, :, :], kcur, ppcur, ALU.subtract).then_inc(S["d2_ready"], 1)
                nc.gpsimd.tensor_tensor(d3[:, :, :], ppprev, kcur, ALU.subtract).then_inc(S["d3_ready"], 1)
                wait(pool, "v_in", 16 * (i + 1))
                wait(pool, "inject_ready", i + 1)
                mul(e2bv[:, :, 1:PAD], e2b[:, :, 1:PAD], v[:, :, :]).then_inc(S["injv_ready"], 1)
                if not is_last(i):
                    norm(mv1, rstd1, shift1, "stat1", "rstd1_ready", i + 1, 2 * i + 1)
                wait(pool, "e2_ready", i + 1)
                mul(d2[:, :, :], d3[:, :, :], v[:, :, :]).then_inc(S["n2_ready"], 1)
                wait(pool, "aa_ready", i + 1)
                mul(e1[:, :, :], e1[:, :, :], aa[:, :, 0:SEQ]).then_inc(S["num_ready"], 1)
                wait(pool, "r0_ready", i + 1)
                mul(d1[:, :, :], d1[:, :, :], d3[:, :, :]).then_inc(S["t_ready"], 1)
                norm(mv2, rstd2, shift2, "stat2", "rstd2_ready", i, 2 * i + 1 if is_last(i) else 2 * i + 2)

            front_steps(pool, step)

            def gather(e, s):
                wait(pool, "x_tr", e - 1)
                wait(pool, "xhi_done", e - 1)
                for h in range(2):
                    c = nc.gpsimd.tensor_copy(gi[s][h][:, :], gtab[h][:, bass.ds(e, 1)])
                c.then_inc(S["gi_ready"], 1)
                wait(pool, "gi_ready", e + 1)
                hold(pool)
                for h in range(2):
                    pool.indirect_dma_start(out=xg[s][:, h, :], out_offset=None, in_=hx_dram[:, :],
                                            in_offset=bass.IndirectOffsetOnAxis(ap=gi[s][h][:, :], axis=0),
                                            bounds_check=ROWS - 1, oob_is_err=True).then_inc(S[f"gathered{s}"], 16)

            def add(e, s):
                for h, tab in enumerate((gtab[0], stab)):
                    c = nc.gpsimd.tensor_copy(si[s][h][:, :], tab[:, bass.ds(e, 1)])
                c.then_inc(S["si_ready"], 1)
                wait(pool, "si_ready", e + 1)
                wait(pool, "rows_done", e + 1)
                wait(pool, "added", 32 * e)
                hold(pool)
                for h in range(2):
                    pool.indirect_dma_start(out=y_dram[:, :], out_offset=bass.IndirectOffsetOnAxis(ap=si[s][h][:, :], axis=0),
                                            in_=rows[s][:, h, :], in_offset=None, bounds_check=ROWS - 1, oob_is_err=True,
                                            compute_op=ALU.add).then_inc(S["added"], 16)

            wait(pool, "tables_ready", 1)
            wait(pool, "h_out", 16 * BATCH)
            wait(pool, "gw_out", 16 * BATCH)
            wait(pool, "zero_out", 64)
            gather(0, 0)
            wait(pool, "y_out", 16 * BATCH)

            def expert(e, s):
                if not (isinstance(e, int) and e == EXP - 1):
                    gather(e + 1, 1 - s)
                if not (isinstance(e, int) and e == 0):
                    add(e - 1, 1 - s)

            expert_steps(pool, expert)
            add(EXP - 1, 1)

        @block.scalar
        def _(act):
            act.dma_start(sgu_sb[:, :, :], sgu).then_inc(S["shared_w"], 16)
            act.dma_start(sd_sb[:, 0:5, :], sd[0:5 * P, :].rearrange("(c p) d -> p c d", p=P)).then_inc(S["shared_d"], 16)
            act.dma_start(sd_sb[0:SC[5][1], 5, :], sd[5 * P:MS, :]).then_inc(S["shared_d"], 16)
            for e in range(2):
                act.dma_start(raw_gu[e][:, :, :], wgu[e]).then_inc(S[f"wgu_in{e}"], 16)
                act.dma_start(raw_d[e][:, 0:2, :], wd[e, 0:2 * P, :].rearrange("(c p) d -> p c d", p=P)).then_inc(S[f"wd_in{e}"], 16)
                act.dma_start(raw_d[e][0:MC[2][1], 2, :], wd[e, 2 * P:M, :]).then_inc(S[f"wd_in{e}"], 16)
            act.wait_ge(S["params"], 32)
            nc.scalar.activation(wdec[:, :], wdec[:, :], ACT.Exp).then_inc(S["act_const"], 1)
            nc.scalar.activation(nufirst[:, :], ufirst[:, :], ACT.Copy, scale=-1.0).then_inc(S["act_const"], 1)
            act.wait_ge(S["dve_const"], 1)

            def evac_k(n):
                wait(act, "k_tr", n + 1)
                for h in range(2):
                    c = nc.scalar.activation(kb[:, 2 * h:2 * h + 2, 1:PAD], T[h][:, :].rearrange("p (g t) -> p g t", g=2), ACT.Copy)
                c.then_inc(S["kb_ready"], 1)

            def tanh(j, m):
                w = SC[m][1]
                wait(act, "up_done", 6 * j + m + 1)
                nc.scalar.activation(th[0:w, m % 2, :], UP[m % 2][0:w, 0:SEQ], ACT.Tanh, scale=0.5).then_inc(S["th_ready"], 1)

            def normalise(n, to, rstd, shift, ready_in, ready):
                wait(act, ready_in, n + 1)
                for t in range(NT):
                    c = nc.scalar.activation(to[:, t, :], xall[:, bass.ds(NT * n + t, 1), :].rearrange("p a d -> p (a d)"),
                                             ACT.Identity, bias=shift[:, t:t + 1], scale=rstd[:, t:t + 1])
                c.then_inc(S[ready], 1)

            def softmax_exp(j):
                wait(act, "mx_ready", j + 1)
                for t in range(NT):
                    c = nc.scalar.activation(ex[:, t, :], logits[:, t, :], ACT.Exp, bias=nmx[:, t:t + 1], accum_out=ssum[:, t:t + 1])
                c.then_inc(S["ex_ready"], 1)

            def overflow(j):
                wait(act, "ovf_tr", j + 1)
                for t in range(NT):
                    c = nc.scalar.activation(ovfT[:, bass.ds((j * NT + t) * P, P)], ovf_ps[t * EXP:(t + 1) * EXP, :], ACT.Copy)
                c.then_inc(S["ovfT_ready"], 1)

            def step(i):
                some, last = not is_first(i), is_last(i)
                if some:
                    softmax_exp(i - 1)
                wait(act, "d1_ready", i + 1)
                for g in range(DC):
                    c = nc.scalar.activation(e1b[:, g, 1:PAD], d1[:, g, :], ACT.Exp, bias=wdec[:, g:g + 1])
                c.then_inc(S["decay_ready"], 1)
                wait(act, "d2_ready", i + 1)
                nc.scalar.activation(e2b[:, :, 1:PAD], d2[:, :, :], ACT.Exp).then_inc(S["inject_ready"], 1)
                if some:
                    tanh(i - 1, 0)
                wait(act, "d3_ready", i + 1)
                for g in range(DC):
                    c = nc.scalar.activation(e1[:, g, :], d3[:, g, :], ACT.Relu, bias=ufirst[:, g:g + 1], scale=-1.0)
                c.then_inc(S["relu_done"], 1)
                if some:
                    tanh(i - 1, 1)
                for g in range(DC):
                    c = nc.scalar.activation(d3[:, g, :], d3[:, g, :], ACT.Relu, bias=nufirst[:, g:g + 1])
                c.then_inc(S["relu_done"], 1)
                wait(act, "relu_done", 2 * i + 1)
                nc.scalar.activation(e1[:, :, :], e1[:, :, :], ACT.Exp, scale=-1.0).then_inc(S["e1_ready"], 1)
                wait(act, "relu_done", 2 * i + 2)
                nc.scalar.activation(d3[:, :, :], d3[:, :, :], ACT.Exp, scale=-1.0).then_inc(S["e2_ready"], 1)
                if some:
                    tanh(i - 1, 2)
                if not last:
                    normalise(i + 1, kn, rstd1, shift1, "rstd1_ready", "kn_ready")
                if some:
                    tanh(i - 1, 3)
                wait(act, "den_ready", i + 1)
                wait(act, "n2_ready", i + 1)
                nc.scalar.activation(d3[:, :, :], d1[:, :, :], ACT.Ln).then_inc(S["ln_ready"], 1)
                wait(act, "ln_ready", i + 1)
                nc.scalar.activation(d3[:, :, :], d3[:, :, :], ACT.Exp, scale=-1.0).then_inc(S["r0_ready"], 1)
                if not last:
                    evac_k(i + 1)
                if some:
                    tanh(i - 1, 4)
                    tanh(i - 1, 5)
                wait(act, "h_out", 16 * i)
                normalise(i, hx, rstd2, shift2, "rstd2_ready", "h_ready")
                if some:
                    overflow(i - 1)
                wait(act, "h_tr", i + 1)
                for h in range(2):
                    c = nc.scalar.activation(hT[:, 2 * h:2 * h + 2, :], T[h][:, :].rearrange("p (g t) -> p g t", g=2), ACT.Copy)
                c.then_inc(S["hT_ready"], 1)

            normalise(0, kn, rstd1, shift1, "rstd1_ready", "kn_ready")
            evac_k(0)
            front_steps(act, step)
            softmax_exp(BATCH - 1)

            def whi(e, s, k):
                wait(act, f"wgu_in{s}", 16 * (nth(e, s) + 1))
                wait(act, "gu_done", 3 * (e - 1))
                nc.scalar.activation(whi_gu[s][:, k, :], raw_gu[s][:, k, :], ACT.Copy).then_inc(S["whi_gu_done"], 1)

            def whid(e, s):
                wait(act, f"wd_in{s}", 32 * (nth(e, s) + 1))
                wait(act, "o_done", e - 1)
                nc.scalar.activation(whi_d[s][:, 0:2, :], raw_d[s][:, 0:2, :], ACT.Copy)
                w = MC[2][1]
                nc.scalar.activation(whi_d[s][0:w, 2, :], raw_d[s][0:w, 2, :], ACT.Copy).then_inc(S["whi_d_done"], 1)

            def take_x(e, s):
                wait(act, "x_tr", e + 1)
                for h in range(2):
                    nc.scalar.activation(xhi[s][:, 2 * h:2 * h + 2, :], XT[h][:, 0:2 * CAP].rearrange("p (g c) -> p g c", g=2), ACT.Copy)
                wait(act, "rows_done", e - 1)
                nc.scalar.activation(wcol[s][:, 0:1], xg[s][:, 0, bass.ds(e + D, 1)], ACT.Copy)
                nc.scalar.activation(wcol[s][:, 1:2], xg[s][:, 1, bass.ds(e + D, 1)], ACT.Identity, bias=last_slot[:, :],
                                     scale=not_last[:, :]).then_inc(S["xhi_done"], 1)

            def silu(e, s, c):
                w = MC[c][1]
                b = (s + c) % 2
                wait(act, "gu_done", 3 * e + c + 1)
                wait(act, "mul_done", 3 * e + c - 1)
                nc.scalar.activation(sil[0:w, b, :], GU[b][0:w, 0:CAP], ACT.Silu).then_inc(S["sil_done"], 1)

            def weigh(e, s):
                wait(act, "r_tr", e + 1)
                wait(act, "added", 32 * (e - 1))
                for h in range(2):
                    c = nc.scalar.activation(rows[s][:, h, :], RW[h][0:HALF, :], ACT.Copy, scale=wcol[s][:, h:h + 1])
                c.then_inc(S["rows_done"], 1)

            tanh(BATCH - 1, 0)
            tanh(BATCH - 1, 1)
            overflow(BATCH - 1)
            act.wait_ge(S["tables_ready"], 1)
            for m in range(2, 6):
                whi(0, 0, m - 2)
                tanh(BATCH - 1, m)
            whid(0, 0)
            take_x(0, 0)
            act.wait_ge(S["y_evac"], NT * BATCH)

            def expert(e, s):
                some = not (isinstance(e, int) and e == 0)
                last = isinstance(e, int) and e == EXP - 1
                if not last:
                    whi(e + 1, 1 - s, 0)
                silu(e, s, 0)
                if not last:
                    whi(e + 1, 1 - s, 1)
                silu(e, s, 1)
                if not last:
                    whi(e + 1, 1 - s, 2)
                silu(e, s, 2)
                if some:
                    weigh(e - 1, 1 - s)
                if not last:
                    take_x(e + 1, 1 - s)
                    whi(e + 1, 1 - s, 3)
                    whid(e + 1, 1 - s)
                wait(act, "o_done", e + 1)
                for h in range(2):
                    c = nc.scalar.activation(oT[:, 2 * h:2 * h + 2, :], OT[h][:, 0:2 * CAP].rearrange("p (g c) -> p g c", g=2), ACT.Copy)
                c.then_inc(S["oT_done"], 1)

            expert_steps(act, expert)
            weigh(EXP - 1, 1)

        @block.vector
        def _(dve):
            V = nc.vector
            def chain(name, length):
                at, n = [0], [0]

                def start(i):
                    at[0], n[0] = i, 0

                def tick(ins):
                    n[0] += 1
                    ins.then_inc(S[name], 1)

                def sync():
                    dve.wait_ge(S[name], at[0] * length + n[0])

                def end():
                    assert n[0] == length, (name, n[0])

                return start, tick, sync, end

            wkv_start, wkv_tick, wkv_sync, wkv_end = chain("wkv_step", WKV_LINKS)
            route_start, route_tick, route_sync, route_end = chain("route_step", ROUTE_LINKS)

            dve.wait_ge(S["consts"], 1)
            V.memset(wrep[:, :, :], 1.0).then_inc(S["dve_step"], 1)
            V.memset(kb[:, :, 0:1], NEG)
            V.memset(e1b[:, :, 0:1], 0.0)
            V.memset(e2b[:, :, 0:1], 0.0)
            V.memset(e2bv[:, :, 0:1], 0.0)
            V.memset(cum[:, :], 0.0)
            V.memset(lastt[:, :], 0.0).then_inc(S["dve_step"], 1)
            dve.wait_ge(S["act_const"], 2)
            V.tensor_scalar(wdec[:, :], wdec[:, :], -1.0, None, ALU.mult).then_inc(S["dve_step"], 1)
            V.tensor_copy(iota_c[:, :], iota_ci[:, :]).then_inc(S["dve_step"], 1)
            dve.wait_ge(S["dve_step"], 4)
            V.memset(iota_c[:, CAP - 1:CAP], -1.0)
            for g in range(DC):
                V.tensor_scalar(wrep[:, g, 1:PAD], wrep[:, g, 1:PAD], wdec[:, g:g + 1], None, ALU.mult)
            V.memset(wrep[:, :, 0:1], NEG).then_inc(S["dve_const"], 1)
            dve.wait_ge(S["dve_const"], 1)

            def bn_stats(n, t):
                return V.bn_stats(st6[:, t, :], xall[:, bass.ds(NT * n + t, 1), :].rearrange("p a d -> p (a d)"))

            def aggregate(mv, ready, count):
                wait(dve, "stats_step", count)
                hold(dve)
                for t in range(NT):
                    r = V.bn_aggr(mv[:, t, :], st6[:, t, :])
                r.then_inc(S[ready], 1)

            def product_tanh(j, m):
                w = SC[m][1]
                wait(dve, "th_ready", 6 * j + m + 1)
                V.scalar_tensor_tensor(th[0:w, m % 2, :], th[0:w, m % 2, :], 1.0, UP[m % 2][0:w, 0:SEQ], ALU.add, ALU.mult).then_inc(S["shid_done"], 1)

            def product(j, m):
                w = SC[m][1]
                wait(dve, "shid_done", 6 * j + m + 1)
                if m == 0:
                    wait(dve, "down_done", NT * j)
                V.scalar_tensor_tensor(shid[0:w, m, :], th[0:w, m % 2, :], 0.5, UP[m % 2][0:w, SEQ:2 * SEQ], ALU.mult, ALU.mult).then_inc(S["hid_done"], 1)

            def take_y(j, t):
                wait(dve, "down_done", NT * j + t + 1)
                xt = xall[:, bass.ds(NT * j + t, 1), :].rearrange("p a d -> p (a d)")
                V.tensor_tensor(xt, xt, DN[:, :], ALU.add).then_inc(S["y_evac"], 1)

            def flat(a):
                return a[:, :, :].rearrange("p g t -> p (g t)")

            def groups(a):
                return a[:, :, :].rearrange("p t (g j) -> p t g j", g=GROUPS)

            def own(a, n):
                return a[:, :, :].unsqueeze(3).to_broadcast(list(a.shape) + [n])

            def each(a, n):
                return a.unsqueeze(2).to_broadcast([P, NT, n, a.shape[2]])

            def row_maximum(j):
                route_start(j)
                wait(dve, "gate_done", j + 1)
                V.tensor_reduce(nmx[:, :], logits, AX.X, ALU.max, negate=True).then_inc(S["mx_ready"], 1)

            def row_sum(j):
                wait(dve, "ex_ready", j + 1)
                route_tick(V.reciprocal(rsum[:, :], ssum[:, :]))

            def scores(j):
                route_sync()
                route_tick(V.tensor_tensor(ex[:, :, :], ex[:, :, :], rsum[:, :].unsqueeze(2).to_broadcast([P, NT, EXP]), ALU.mult))

            def group_maxima(j):
                route_sync()
                route_tick(V.tensor_reduce(gm[:, :, :], groups(ex), AX.X, ALU.max))

            def group_compare(j):
                route_sync()
                V.tensor_tensor(ggt[:], each(gm[:, :, :], GROUPS), own(gm, GROUPS), ALU.is_gt)
                route_tick(V.tensor_tensor(geq[:], each(gm[:, :, :], GROUPS), own(gm, GROUPS), ALU.is_equal))

            def group_ties(j):
                route_sync()
                route_tick(V.tensor_tensor(geq[:], geq[:], tri[:, :, :].unsqueeze(1).to_broadcast([P, NT, GROUPS, GROUPS]), ALU.mult))

            def group_beaten(j):
                route_sync()
                route_tick(V.tensor_tensor(ggt[:], ggt[:], geq[:], ALU.add))

            def group_count(j):
                route_sync()
                route_tick(V.tensor_reduce(gcnt[:, :, :], ggt[:], AX.X, ALU.add))

            def group_keep(j):
                route_sync()
                route_tick(V.tensor_scalar(gcnt[:, :, :], gcnt[:, :, :], float(TOPG), None, ALU.is_lt))

            def kept_scores(j):
                route_sync()
                route_tick(V.tensor_tensor(groups(tmp), groups(ex), own(gcnt, GE), ALU.mult))

            def largest(j):
                route_sync()
                hold(dve)
                for t in range(NT):
                    r = V.max(v8[:, t, :], tmp[:, t, :])
                route_tick(r)

            def where(j):
                route_sync()
                hold(dve)
                for t in range(NT):
                    r = V.max_index(i8[:, t, :], v8[:, t, :], tmp[:, t, :])
                route_tick(r)

            def where_float(j):
                route_sync()
                route_tick(V.tensor_copy(i6[:, :, :], i8[:, :, 0:TOPK]))

            def choices(j):
                route_sync()
                for t in range(NT):
                    r = V.tensor_tensor(eq6[:, t], iota_e[:, :].unsqueeze(1).to_broadcast([P, TOPK, EXP]),
                                        i6[:, t, :].unsqueeze(2).to_broadcast([P, TOPK, EXP]), ALU.is_equal)
                route_tick(r)

            def chosen(j):
                route_sync()
                route_tick(V.tensor_reduce(mask[:, :, :], eq6[:].rearrange("p t j e -> p t e j"), AX.X, ALU.add))

            def gate_weights(j):
                route_sync()
                V.tensor_copy(maskb[:, :, :], mask[:, :, :]).then_inc(S["mask_ready"], 1)
                wait(dve, "gw_out", 16 * j)
                V.tensor_tensor(gw[:, :, :], mask[:, :, :], tmp[:, :, :], ALU.mult).then_inc(S["gw_ready"], 1)

            def last_token(j, t):
                route_sync()
                route_tick(V.scalar_tensor_tensor(lastt[:, 0:EXP], mask[:, t, :], tokid[:, t:t + 1], lastt[:, 0:EXP], ALU.mult, ALU.max))

            def position_products(j):
                wait(dve, "pos_done", j + 1)
                for t in range(NT):
                    r = V.tensor_tensor(pe6[:, t], eq6[:, t], pos[:, t, :].unsqueeze(1).to_broadcast([P, TOPK, EXP]), ALU.mult)
                route_tick(r)

            def positions(j):
                route_sync()
                route_tick(V.tensor_reduce(posel[:, :, :], pe6[:], AX.X, ALU.add))

            def overflow(j):
                wait(dve, "gw_ready", j + 1)
                V.scalar_tensor_tensor(ovf[:, :, :], pos, float(CAP - 1), gw[:, :, :], ALU.is_ge, ALU.mult).then_inc(S["ovf_ready"], 1)

            def count_tile(j, t):
                route_sync()
                route_tick(V.tensor_tensor(cum[:, :], cum[:, :], maskb[:, t, :], ALU.add))

            def one_hot(j, t):
                route_sync()
                wait(dve, "tab_done", j)
                for k in range(TOPK):
                    V.tensor_scalar(slot1h[:, t, k, :], iota_c[:, :], posel[:, t, k:k + 1], None, ALU.is_equal)
                V.tensor_scalar(val1h[:, t, :, 0:EXP], eq6[:, t], pid1[:, :], None, ALU.mult)
                V.tensor_scalar(val1h[:, t, :, EXP:2 * EXP], eq6[:, t], tileno[:, t:t + 1], None, ALU.mult).then_inc(S["onehot_ready"], 1)

            def next_tokens(j):
                wait(dve, "onehot_ready", NT * (j + 1))
                V.tensor_scalar(tokid[:, :], tokid[:, :], float(SEQ), None, ALU.add)
                route_tick(V.tensor_scalar(tileno[:, :], tileno[:, :], float(NT), None, ALU.add))
                route_end()

            def step(i):
                some, last = not is_first(i), is_last(i)
                ppcur, ppprev = pp[:, :, 1:PAD], pp[:, :, 0:SEQ]
                wkv_start(i)
                route = lambda piece, *t: piece(i - 1, *t) if some else None
                wait(dve, "kb_ready", i + 1)
                V.tensor_tensor_scan(flat(pp), flat(wrep), flat(kb), NEG, ALU.add, ALU.max).then_inc(S["pp_ready"], 1)
                route(row_maximum)
                wait(dve, "pp_ready", i + 1)
                V.tensor_tensor(d1[:, :, :], ppprev, ppcur, ALU.subtract).then_inc(S["d1_ready"], 1)
                if not last:
                    wait(dve, "x_in", 16 * (i + 2))
                    hold(dve)
                    bn_stats(i + 1, 0)
                route(row_sum)
                if not last:
                    bn_stats(i + 1, 1).then_inc(S["stats_step"], 1)
                route(scores)
                if not last:
                    aggregate(mv1, "stat1", 2 * i + 2)
                route(group_maxima)
                route(group_compare)
                route(group_ties)
                route(group_beaten)
                route(group_count)
                route(group_keep)
                route(product_tanh, 0)
                route(kept_scores)
                route(product, 0)
                wait(dve, "decay_ready", i + 1)
                wait(dve, "inject_ready", i + 1)
                wkv_tick(V.tensor_tensor_scan(flat(bb), flat(e1b), flat(e2b), 0.0, ALU.mult, ALU.add))
                route(largest)
                route(product_tanh, 1)
                route(where)
                route(product, 1)
                route(where_float)
                wait(dve, "injv_ready", i + 1)
                wkv_tick(V.tensor_tensor_scan(flat(aa), flat(e1b), flat(e2bv), 0.0, ALU.mult, ALU.add))
                route(choices)
                wait(dve, "e1_ready", i + 1)
                wkv_sync()
                V.tensor_tensor(d1[:, :, :], e1[:, :, :], bb[:, :, 0:SEQ], ALU.mult).then_inc(S["aa_ready"], 1)
                route(chosen)
                wait(dve, "e2_ready", i + 1)
                wait(dve, "aa_ready", i + 1)
                V.tensor_tensor(d1[:, :, :], d1[:, :, :], d3[:, :, :], ALU.add).then_inc(S["den_ready"], 1)
                route(gate_weights)
                route(product_tanh, 2)
                route(last_token, 0)
                route(product, 2)
                route(last_token, 1)
                route(position_products)
                route(product_tanh, 3)
                route(positions)
                route(product, 3)
                wait(dve, "num_ready", i + 1)
                wkv_tick(V.tensor_tensor(e1[:, :, :], e1[:, :, :], d2[:, :, :], ALU.add))
                route(overflow)
                route(count_tile, 0)
                route(count_tile, 1)
                wait(dve, "r0_ready", i + 1)
                wkv_sync()
                wkv_tick(V.tensor_tensor(e1[:, :, :], e1[:, :, :], d3[:, :, :], ALU.mult))
                route(product_tanh, 4)
                route(product, 4)
                wait(dve, "t_ready", i + 1)
                wkv_sync()
                V.scalar_tensor_tensor(e1[:, :, :], d1[:, :, :], -2.0, e1[:, :, :], ALU.add, ALU.mult).then_inc(S["yT_ready"], 1)
                route(product_tanh, 5)
                route(product, 5)
                wait(dve, "y_tr", i + 1)
                for t in range(NT):
                    xt = xall[:, bass.ds(NT * i + t, 1), :].rearrange("p a d -> p (a d)")
                    q = V.tensor_tensor(xt, xt, T[t][:, :], ALU.subtract)
                wkv_tick(q)
                wkv_sync()
                hold(dve)
                bn_stats(i, 0)
                bn_stats(i, 1).then_inc(S["stats_step"], 1)
                aggregate(mv2, "stat2", 2 * i + 2 if last else 2 * i + 3)
                route(one_hot, 0)
                route(one_hot, 1)
                route(next_tokens)
                route(take_y, 0)
                route(take_y, 1)
                wkv_end()

            dve.wait_ge(S["x_in"], 16)
            hold(dve)
            bn_stats(0, 0)
            bn_stats(0, 1).then_inc(S["stats_step"], 1)
            aggregate(mv1, "stat1", 1)
            front_steps(dve, step)

            for piece in (row_maximum, row_sum, scores, group_maxima, group_compare, group_ties, group_beaten, group_count,
                          group_keep, kept_scores, largest, where, where_float, choices, chosen, gate_weights):
                piece(BATCH - 1)
            for t in range(NT):
                last_token(BATCH - 1, t)
            position_products(BATCH - 1)
            positions(BATCH - 1)
            for t in range(NT):
                count_tile(BATCH - 1, t)
            for t in range(NT):
                one_hot(BATCH - 1, t)
            overflow(BATCH - 1)
            next_tokens(BATCH - 1)

            n0 = 4
            m0 = [0]

            def tail_link(ins):
                m0[0] += 1
                ins.then_inc(S["dve_step"], 1)
                dve.wait_ge(S["dve_step"], n0 + m0[0])

            V.tensor_copy(st6[:, 0, 0:1], pid1[:, :]).then_inc(S["last_ready"], 1)
            dve.wait_ge(S["tab_done"], BATCH)
            for h in range(2):
                r = V.tensor_copy(tabs[:, h, :], TAB[h][0:HALF, 0:2 * EXP])
            tail_link(r)
            for h in range(2):
                tail_link(V.scalar_tensor_tensor(tval[:, h, :], tabs[:, h, EXP:2 * EXP], float(P), tabs[:, h, 0:EXP], ALU.mult, ALU.add))
                tail_link(V.tensor_scalar(tz[:, h, :], tval[:, h, :], 0.0, None, ALU.is_equal))
                tail_link(V.scalar_tensor_tensor(tval[:, h, :], tz[:, h, :], unused[:, h:h + 1], tval[:, h, :], ALU.mult, ALU.add))
                tail_link(V.tensor_scalar(tval[:, h, :], tval[:, h, :], -1.0, None, ALU.add))
            V.tensor_copy(gtab[0][:, :], tval[:, 0, :])
            dve.wait_ge(S["last_tr"], 1)
            tail_link(V.tensor_reduce(lcol[:, :], G[0:EXP, 3 * P:4 * P], AX.X, ALU.max))
            V.tensor_copy(lmat[:, HALF - 1:HALF], lcol[:, :]).then_inc(S["lmat_ready"], 1)
            tail_link(V.tensor_scalar(tval[:, 1, :], tval[:, 1, :], not_last[:, :], None, ALU.mult))
            tail_link(V.scalar_tensor_tensor(tz[:, 1, :], lastr[:, :], last_slot[:, :], tval[:, 1, :], ALU.mult, ALU.add))
            V.tensor_copy(stab[:, :], tz[:, 1, :])
            dve.wait_ge(S["lastr_done"], 1)
            V.tensor_tensor(gtab[1][:, :], tval[:, 1, :], T[0][0:HALF, 0:EXP], ALU.add).then_inc(S["tables_ready"], 1)

            def wlo(e, s, k):
                wait(dve, "whi_gu_done", DC * e + k + 1)
                V.tensor_tensor(wlo_gu[s][:, k, :], raw_gu[s][:, k, :], whi_gu[s][:, k, :].bitcast(F32), ALU.subtract).then_inc(S["wlo_gu_done"], 1)

            def wlod(e, s):
                wait(dve, "whi_d_done", e + 1)
                V.tensor_tensor(wlo_d[s][:, 0:2, :], raw_d[s][:, 0:2, :], whi_d[s][:, 0:2, :].bitcast(F32), ALU.subtract)
                w = MC[2][1]
                V.tensor_tensor(wlo_d[s][0:w, 2, :], raw_d[s][0:w, 2, :], whi_d[s][0:w, 2, :].bitcast(F32), ALU.subtract).then_inc(S["wlo_d_done"], 1)

            def xrest(e, s):
                wait(dve, "xhi_done", e + 1)
                for h in range(2):
                    r = V.tensor_tensor(xlo[s][:, 2 * h:2 * h + 2, :], XT[h][:, 0:2 * CAP].rearrange("p (g c) -> p g c", g=2),
                                        xhi[s][:, 2 * h:2 * h + 2, :].bitcast(F32), ALU.subtract)
                r.then_inc(S["xlo_done"], 1)

            def hidden(e, s, c):
                w = MC[c][1]
                b = (s + c) % 2
                wait(dve, "sil_done", 3 * e + c + 1)
                V.tensor_tensor(hid[0:w, b, :], sil[0:w, b, :], GU[b][0:w, CAP:2 * CAP], ALU.mult).then_inc(S["mul_done"], 1)
                wait(dve, "mul_done", 3 * e + c + 1)
                V.tensor_copy(hhi[0:w, c, :], hid[0:w, b, :]).then_inc(S["hhi_done"], 1)
                wait(dve, "hhi_done", 3 * e + c + 1)
                V.tensor_tensor(hlo[0:w, c, :], hid[0:w, b, :], hhi[0:w, c, :].bitcast(F32), ALU.subtract).then_inc(S["hlo_done"], 1)

            for m in range(6):
                if m >= 2:
                    wlo(0, 0, m - 2)
                product_tanh(BATCH - 1, m)
                product(BATCH - 1, m)
            wlod(0, 0)
            for t in range(NT):
                take_y(BATCH - 1, t)
            xrest(0, 0)

            def expert(e, s):
                last = isinstance(e, int) and e == EXP - 1
                for c in range(3):
                    if not last:
                        wlo(e + 1, 1 - s, c)
                    hidden(e, s, c)
                if not last:
                    xrest(e + 1, 1 - s)
                    wlo(e + 1, 1 - s, 3)
                    wlod(e + 1, 1 - s)

            expert_steps(dve, expert)

            for n in range(BATCH * NT):
                if n % NT == 0:
                    dve.wait_ge(y_back[n // NT], 16)
                dve.wait_ge(S["fin_ps"], n + 1)
                V.tensor_tensor(xall[:, n, :], xall[:, n, :], psum[n % 8][:, :], ALU.add).then_inc(S["fin_add"], 1)

        @block.tensor
        def _(pe):
            mm, tr = nc.tensor.matmul, nc.tensor.transpose

            def transpose_in(src, done):
                for g in range(DC):
                    for t in range(NT):
                        r = tr(T[g // 2][:, (g % 2) * SEQ + t * P:(g % 2) * SEQ + (t + 1) * P], src[:, t, g * P:(g + 1) * P], ident[:, :])
                r.then_inc(S[done], 1)

            def up(j, m):
                m0, w = SC[m]
                wait(pe, "hid_done", 6 * j + m - 1)
                for q in range(2):
                    for k in range(DC):
                        r = mm(UP[m % 2][0:w, q * SEQ:(q + 1) * SEQ], sgu_sb[:, k, q * MS + m0:q * MS + m0 + w], hT[:, k, :],
                               start=(k == 0), stop=(k == DC - 1))
                r.then_inc(S["up_done"], 1)

            def down(j, t):
                if t == 0:
                    wait(pe, "hid_done", 6 * (j + 1))
                wait(pe, "y_evac", NT * j + t)
                for m, (m0, w) in enumerate(SC):
                    r = mm(DN[:, :], shid[0:w, m, t * P:(t + 1) * P], sd_sb[0:w, m, :], start=(m == 0), stop=(m == len(SC) - 1))
                r.then_inc(S["down_done"], 1)

            def place(j):
                wait(pe, "mask_ready", j + 1)
                for t in range(NT):
                    mm(pos[:, t, :], ones[:, :], cum[:, :], start=True, stop=False)
                    if t:
                        mm(pos[:, t, :], ones[:, :], maskb[:, 0, :], start=False, stop=False)
                    r = mm(pos[:, t, :], lstrict[:, :], maskb[:, t, :], start=False, stop=True)
                r.then_inc(S["pos_done"], 1)

            def overflow(j):
                wait(pe, "ovf_ready", j + 1)
                wait(pe, "ovfT_ready", j)
                tr(ovf_ps, ovf[:, :, :].rearrange("p t e -> p (t e)"), ident[:, :]).then_inc(S["ovf_tr"], 1)

            def slots(j):
                wait(pe, "onehot_ready", NT * (j + 1))
                for h in range(2):
                    for t in range(NT):
                        for k in range(TOPK):
                            r = mm(TAB[h][0:HALF, 0:2 * EXP], slot1h[:, t, k, h * HALF:(h + 1) * HALF], val1h[:, t, k, :],
                                   start=(is_first(j) and t == 0 and k == 0), stop=(is_last(j) and t == NT - 1 and k == TOPK - 1))
                r.then_inc(S["tab_done"], 1)

            def step(i):
                some, last = not is_first(i), is_last(i)
                j = i - 1
                if some:
                    up(j, 0)
                    up(j, 1)
                    up(j, 2)
                    up(j, 3)
                    place(j)
                if not last:
                    wait(pe, "kn_ready", i + 2)
                    transpose_in(kn, "k_tr")
                if some:
                    up(j, 4)
                    up(j, 5)
                wait(pe, "yT_ready", i + 1)
                wait(pe, "kb_ready", i + 1 if last else i + 2)
                for t in range(NT):
                    for g in range(DC):
                        r = tr(T[t][:, g * P:(g + 1) * P], e1[:, g, t * P:(t + 1) * P], ident[:, :])
                r.then_inc(S["y_tr"], 1)
                if some:
                    overflow(j)
                    down(j, 0)
                wait(pe, "h_ready", i + 1)
                transpose_in(hx, "h_tr")
                if some:
                    slots(j)
                    down(j, 1)
                wait(pe, "hT_ready", i + 1)
                for t in range(NT):
                    for k in range(DC):
                        r = mm(logits[:, t, :], hT[:, k, t * P:(t + 1) * P], gate_sb[:, k, :], start=(k == 0), stop=(k == DC - 1))
                r.then_inc(S["gate_done"], 1)

            wait(pe, "consts", 1)
            wait(pe, "kn_ready", 1)
            transpose_in(kn, "k_tr")
            pe.wait_ge(S["gate_in"], 16)
            pe.wait_ge(S["shared_w"], 16)
            pe.wait_ge(S["shared_d"], 32)
            front_steps(pe, step)
            for m in range(2):
                up(BATCH - 1, m)
            place(BATCH - 1)
            overflow(BATCH - 1)
            slots(BATCH - 1)
            wait(pe, "ovfT_ready", BATCH)
            wait(pe, "last_ready", 1)
            tr(G[:, 3 * P:4 * P], lastt[:, :], ident[:, :]).then_inc(S["last_tr"], 1)
            wait(pe, "lmat_ready", 1)
            mm(T[0][0:HALF, 0:EXP], lmat[:, :], ident[0:EXP, 0:EXP], start=True, stop=True).then_inc(S["lastr_done"], 1)
            for m in range(2, 6):
                up(BATCH - 1, m)
            for t in range(NT):
                down(BATCH - 1, t)

            def bring_x(e, s):
                wait(pe, f"gathered{s}", 32 * (nth(e, s) + 1))
                wait(pe, "xlo_done", e)
                for k in range(DC):
                    for h in range(2):
                        at = (k % 2) * CAP + h * HALF
                        r = tr(XT[k // 2][:, at:at + HALF], xg[s][:, h, k * P:(k + 1) * P], ident[0:HALF, 0:HALF])
                r.then_inc(S["x_tr"], 1)

            def gate_up(e, s, c):
                m0, w = MC[c]
                b = (s + c) % 2
                if c == 0:
                    wait(pe, "xlo_done", e + 1)
                    wait(pe, "wlo_gu_done", DC * (e + 1))
                wait(pe, "mul_done", 3 * e + c - 1)
                for q in range(2):
                    for k in range(DC):
                        col = slice(q * M + m0, q * M + m0 + w)
                        for n, (a, z) in enumerate(((whi_gu, xhi), (whi_gu, xlo), (wlo_gu, xhi))):
                            r = mm(GU[b][0:w, q * CAP:(q + 1) * CAP], a[s][:, k, col], z[s][:, k, :],
                                   start=(k == 0 and n == 0), stop=(k == DC - 1 and n == 2))
                r.then_inc(S["gu_done"], 1)

            def down_rows(e, s):
                wait(pe, "hlo_done", 3 * (e + 1))
                wait(pe, "wlo_d_done", e + 1)
                wait(pe, "oT_done", e)
                for g in range(DC):
                    o = OT[g // 2][:, (g % 2) * CAP:(g % 2 + 1) * CAP]
                    for c, (m0, w) in enumerate(MC):
                        for n, (a, z) in enumerate(((whi_d, hhi), (whi_d, hlo), (wlo_d, hhi))):
                            r = mm(o, a[s][0:w, c, g * P:(g + 1) * P], z[0:w, c, :],
                                   start=(c == 0 and n == 0), stop=(c == len(MC) - 1 and n == 2))
                r.then_inc(S["o_done"], 1)

            def rows_out(e, s):
                wait(pe, "oT_done", e + 1)
                wait(pe, "rows_done", e)
                for g in range(DC):
                    for h in range(2):
                        r = tr(RW[h][0:HALF, g * P:(g + 1) * P], oT[:, g, h * HALF:(h + 1) * HALF], ident[:, :])
                r.then_inc(S["r_tr"], 1)

            pe.wait_ge(S["tables_ready"], 1)
            bring_x(0, 0)

            def expert(e, s):
                for c in range(3):
                    gate_up(e, s, c)
                if not (isinstance(e, int) and e == 0):
                    rows_out(e - 1, 1 - s)
                if not (isinstance(e, int) and e == EXP - 1):
                    bring_x(e + 1, 1 - s)
                down_rows(e, s)

            expert_steps(pe, expert)
            rows_out(EXP - 1, 1)

            pe.wait_ge(S["fin_last"], 16)
            for n in range(BATCH * NT):
                if n >= 8:
                    pe.wait_ge(S["fin_add"], n - 7)
                mm(psum[n % 8][:, :], ovfT[:, n * P:(n + 1) * P], last_out[:, :], start=True, stop=True).then_inc(S["fin_ps"], 1)


def kernel(x, ctx_2048, L0_xattn_time_decay, L0_xattn_time_first, L0_ffn_gate_weight, L0_ffn_Wg, L0_ffn_Wu,
           L0_ffn_Wd, L0_ffn_Sg, L0_ffn_Su, L0_ffn_Sd):
    import numpy as np
    import concourse.bacc as bacc
    from concourse.bass_utils import run_bass_kernel_spmd

    def put(a):
        return np.ascontiguousarray(a)

    def contract_first(w):
        w = np.asarray(w)
        w = w.reshape(w.shape[:-1] + (DC, P))
        return np.moveaxis(w, (-1, -2), (-3, -2))

    arrays = {
        "x": put(x),
        "ctxv": put(contract_first(ctx_2048)),
        "decay": put(np.asarray(L0_xattn_time_decay).reshape(DC, P).T),
        "first": put(np.asarray(L0_xattn_time_first).reshape(DC, P).T),
        "gate": put(contract_first(L0_ffn_gate_weight)),
        "wgu": put(np.concatenate([contract_first(L0_ffn_Wg), contract_first(L0_ffn_Wu)], axis=-1)),
        "wd": put(np.swapaxes(np.asarray(L0_ffn_Wd), 1, 2)),
        "sgu": put(np.concatenate([contract_first(L0_ffn_Sg), contract_first(L0_ffn_Su)], axis=-1)),
        "sd": put(np.asarray(L0_ffn_Sd).T),
    }
    nc = bacc.Bacc("TRN2", target_bir_lowering=False, num_devices=1)
    args = [nc.dram_tensor(f"in_{n}", a.shape, mybir.dt.from_np(a.dtype), kind="ExternalInput").ap() for n, a in arrays.items()]
    args.append(nc.dram_tensor("out_0", (BATCH, SEQ, D), F32, kind="ExternalOutput").ap())
    build(nc, *args)
    r = run_bass_kernel_spmd(nc, [{f"in_{n}": a for n, a in arrays.items()}], core_ids=[0])
    return r.results[0]["out_0"]
```

```python
import concourse.bass as bass
from concourse import mybir
from contextlib import ExitStack

F32, F32R, BF16, U32 = (mybir.dt.float32, mybir.dt.float32r, mybir.dt.bfloat16, mybir.dt.uint32)
ALU = mybir.AluOpType
ACT = mybir.ActivationFunctionType
AX = mybir.AxisListType

P = 128
BATCH, SEQ, D = 8, 256, 512
TOK = BATCH * SEQ
NT = SEQ // P
DC = D // P
EXP, M, CAP = 64, 352, 192
GROUPS, TOPG, TOPK = 8, 3, 6
GE = EXP // GROUPS
SA, SB = P, CAP - P
SLOTS = (SA, SB)
MS = 704
SR = (MS - 4 * P) // 2
MC = [(m, min(P, M - m)) for m in range(0, M, P)]
SD = 4
SC = [(m * P, P) for m in range(SD)] + [(SD * P + n * SR, SR) for n in range(2)]
EPS = 1e-5
NEG = -1e38
WKV_STEPS, ROUTE_STEPS = 5, 21
LAST_ROW = TOK
DUMP_ROW = TOK + EXP
ROWS = DUMP_ROW + CAP
HX = D + EXP
PAD = SEQ + 1


def build(nc, x, ctxv, decay, first, gate, wgu, wd, sgu, sd, out):
    hx_dram = nc.dram_tensor("hx_rows", (ROWS, HX), F32, kind="Internal").ap()
    y_dram = nc.dram_tensor("y_rows", (ROWS, D), F32, kind="Internal").ap()

    ctx = ExitStack()
    with ctx:
        def in_stack(stack):
            return lambda name, shape, dt=F32: stack.enter_context(nc.sbuf_tensor(name, shape, dt))

        def sem(name):
            return ctx.enter_context(nc.semaphore(name))

        sb = in_stack(ctx)
        psum = [ctx.enter_context(nc.psum_tensor(f"bank{i}", [P, 512], F32)) for i in range(8)]

        ident = sb("ident", [P, P])
        gtab = [sb(f"gather_ids{h}", [n, EXP], U32) for h, n in enumerate(SLOTS)]
        stab = sb("scatter_ids1", [SB, EXP], U32)
        last_slot = sb("last_slot", [SB, 1])
        not_last = sb("not_last", [SB, 1])
        xall = sb("xall", [P, BATCH * NT, D])
        ovfT = sb("ovfT", [P, BATCH * P])
        with ExitStack() as early:
            sgu_lo = early.enter_context(nc.sbuf_tensor("sgu_lo", [P, DC, 2 * MS], F32R))
            sd_lo = early.enter_context(nc.sbuf_tensor("sd_lo", [P, len(SC), D], F32R))
        raw_gu_all = sb("raw_gu", [P, 2 * DC * 2 * M])
        raw_d_all = sb("raw_d", [P, 2 * len(MC) * D])
        raw_gu = [raw_gu_all[:, s * DC * 2 * M:(s + 1) * DC * 2 * M].rearrange("p (k m) -> p k m", k=DC) for s in range(2)]
        raw_d = [raw_d_all[:, s * len(MC) * D:(s + 1) * len(MC) * D].rearrange("p (c d) -> p c d", c=len(MC)) for s in range(2)]
        sgu_raw = raw_gu_all[:, :].rearrange("p (k m) -> p k m", k=DC)
        sd_raw = raw_d_all[:, :].rearrange("p (c d) -> p c d", c=len(SC))

        shared_stack = ExitStack()
        sbs = in_stack(shared_stack)
        base_shared = nc.sbuf_base
        sgu_hi = sbs("sgu_hi", [P, DC, 2 * MS], F32R)
        sd_hi = sbs("sd_hi", [P, len(SC), D], F32R)
        shid_hi = sbs("shid_hi", [P, len(SC), SEQ], F32R)
        shid_lo = sbs("shid_lo", [P, len(SC), SEQ], F32R)
        th = sbs("th", [P, len(SC), SEQ])
        hT_hi = sbs("hT_hi", [P, DC, SEQ], F32R)
        hT_lo = sbs("hT_lo", [P, DC, SEQ], F32R)
        base_front = nc.sbuf_base

        front_stack = ExitStack()
        sbf = in_stack(front_stack)
        kn = sbf("kn", [P, NT, D])
        hx = kn
        hT = sbf("hT", [P, DC, SEQ])
        kb = sbf("kb", [P, DC, PAD])
        v = sbf("v", [P, DC, SEQ])
        wrep = sbf("wrep", [P, DC, PAD])
        pp = sbf("pp", [P, DC, PAD])
        d3 = sbf("d3", [P, DC, SEQ])
        e1 = sbf("e1", [P, DC, SEQ])
        e1b = sbf("e1b", [P, DC, PAD])
        e2b = sbf("e2b", [P, DC, PAD])
        e2bv = sbf("e2bv", [P, DC, PAD])
        aa = sbf("aa", [P, DC, PAD])
        bb = sbf("bb", [P, DC, PAD])
        gw = sbf("gw", [P, NT, EXP])
        gate_sb = sbf("gate_sb", [P, DC, EXP])
        wdec = sbf("wdec", [P, DC])
        ufirst = sbf("ufirst", [P, DC])
        nufirst = sbf("nufirst", [P, DC])
        st6 = sbf("st6", [P, NT, 6])
        mv1 = sbf("mv1", [P, NT, 2])
        mv2 = sbf("mv2", [P, NT, 2])
        ve = sbf("ve", [P, NT])
        rstd1 = sbf("rstd1", [P, NT])
        shift1 = sbf("shift1", [P, NT])
        shift2 = sbf("shift2", [P, NT])
        nmean = sbf("nmean", [P, NT])
        mone = sbf("mone", [P, NT])
        rstd2 = sbf("rstd2", [P, NT])
        eps_t = sbf("eps_t", [P, NT])
        mhalf = sbf("mhalf", [P, NT])
        lstrict = sbf("lstrict", [P, P], BF16)
        ones = sbf("ones", [P, P], BF16)
        iota_e = sbf("iota_e", [P, EXP])
        iota_ci = sbf("iota_ci", [P, CAP])
        iota_c = sbf("iota_c", [P, CAP], BF16)
        tri = sbf("tri", [P, GROUPS, GROUPS])
        pid1 = sbf("pid1", [P, 1])
        tokid = sbf("tokid", [P, NT])
        tileno = sbf("tileno", [P, NT])
        nmx = sbf("nmx", [P, NT])
        ssum = sbf("ssum", [P, NT])
        rsum = sbf("rsum", [P, NT])
        ex = sbf("ex", [P, NT, EXP])
        gm = sbf("gm", [P, NT, GROUPS])
        ggt = sbf("ggt", [P, NT, GROUPS, GROUPS])
        geq = sbf("geq", [P, NT, GROUPS, GROUPS])
        gcnt = sbf("gcnt", [P, NT, GROUPS])
        tmp = sbf("tmp", [P, NT, EXP])
        v8 = sbf("v8", [P, NT, 8])
        i8 = sbf("i8", [P, NT, 8], U32)
        i6 = sbf("i6", [P, NT, TOPK])
        eq6 = sbf("eq6", [P, NT, TOPK, EXP], BF16)
        pe6 = sbf("pe6", [P, NT, TOPK, EXP])
        mask = sbf("mask", [P, NT, EXP])
        maskb = sbf("maskb", [P, NT, EXP], BF16)
        cum = sbf("cum", [P, EXP], BF16)
        lastt = sbf("lastt", [P, P])
        lasts = sbf("lasts", [P, P])
        posel = sbf("posel", [P, NT, TOPK])
        ovf = sbf("ovf", [P, NT, EXP])
        slot1h = sbf("slot1h", [P, NT, TOPK, CAP], BF16)
        val1h = sbf("val1h", [P, NT, TOPK, 2 * EXP], BF16)
        tabs = sbf("tabs", [P, 2, 2 * EXP])
        tval = sbf("tval", [P, 2, EXP])
        tz = sbf("tz", [P, 2, EXP])
        unused = sbf("unused", [P, 2])
        lastr = sbf("lastr", [SB, EXP])
        lcol = sbf("lcol", [EXP, 1])
        lmat = sbf("lmat", [EXP, SB])
        zrow = pe6[:, :, :, :].rearrange("p t j e -> p (t j e)")[:, 0:HX]
        front_top = nc.sbuf_base
        front_stack.close()
        shared_stack.close()

        whi_gu, wlo_gu, whi_d, wlo_d = [None] * 2, [None] * 2, [None] * 2, [None] * 2

        def weight_slot(s):
            whi_gu[s] = sb(f"whi_gu{s}", [P, DC, 2 * M], F32R)
            wlo_gu[s] = sb(f"wlo_gu{s}", [P, DC, 2 * M], F32R)
            whi_d[s] = sb(f"whi_d{s}", [P, len(MC), D], F32R)
            wlo_d[s] = sb(f"wlo_d{s}", [P, len(MC), D], F32R)

        weight_slot(1)
        assert base_shared < nc.sbuf_base <= base_front, (base_shared, nc.sbuf_base, base_front)
        if base_front > nc.sbuf_base:
            sb("gap", [P, base_front - nc.sbuf_base], mybir.dt.uint8)
        weight_slot(0)
        AHI, BHL, ALO = slice(0, SA), slice(SA, SA + 2 * SB), slice(SA + 2 * SB, 2 * CAP)
        xp = sb("xp", [P, DC, 2 * CAP], F32R)
        hp = sb("hp", [P, len(MC), 2 * CAP], F32R)
        xg = [sb(f"xg{s}", [P, 2, HX]) for s in range(2)]
        wcol = [sb(f"wcol{s}", [P, 2]) for s in range(2)]
        sil_a = sb("sil_a", [P, M])
        hid_a = sb("hid_a", [P, M])
        low_b = sb("low_b", [SB, 2, M])
        sum_b = sb("sum_b", [SB, 2, M])
        sil_b = sb("sil_b", [SB, M])
        hid_b = sb("hid_b", [SB, M])
        rows = [sb(f"rows{s}", [P, 2, D]) for s in range(2)]
        row_low = sb("row_low", [SB, D])
        gi = [[sb(f"gi{s}{h}", [n, 1], U32) for h, n in enumerate(SLOTS)] for s in range(2)]
        si = [[sb(f"si{s}{h}", [n, 1], U32) for h, n in enumerate(SLOTS)] for s in range(2)]
        last_out = raw_d_all[:, 0:NT * D].rearrange("p (t d) -> p t d", t=NT)

        T = [psum[0], psum[1]]
        UP = [psum[2], psum[3]]
        DN = psum[4]
        G = psum[5]
        logits = G[:, 0:NT * EXP].rearrange("p (t e) -> p t e", t=NT)
        pos = G[:, P:P + NT * EXP].rearrange("p (t e) -> p t e", t=NT)
        ovf_ps = G[:, 2 * P:3 * P]
        TAB = [psum[6], psum[7]]
        TR = [psum[0], psum[1]]
        GA = [psum[2], psum[3]]
        GB = [psum[4], psum[5]]
        RA, RB = psum[6], psum[7]

        def turned(bank):
            return bank[:, 0:2 * CAP].rearrange("p (g c) -> p g c", g=2)

        names = """params x_in v_in gate_in shared_w shared_d zero_out h_out gw_out y_out consts dve_const act_const dve_step pool_step
            wkv_step route_step stats_step held relu_done
            stat1 rstd1_ready kn_ready k_tr kb_ready pp_ready d1_ready d2_ready d3_ready decay_ready inject_ready injv_ready
            e1_ready e2_ready n2_ready e1_min shi_done slo_done sdhi_done sdlo_done hThi_ready hTlo_ready split_step split_done aa_ready num_ready den_ready ln_ready r0_ready t_ready yT_ready y_tr
            stat2 rstd2_ready h_ready h_tr hT_ready gate_done mx_ready ex_ready mask_ready gw_ready pos_done
            ovf_ready ovf_tr ovfT_ready onehot_ready tab_done
            up_done th_ready shid_done hid_done down_done y_evac
            last_ready last_tr lmat_ready lastr_done tables_ready table_step
            wgu_in0 wgu_in1 wd_in0 wd_in1 whi_gu_done wlo_gu_done whi_d_done wlo_d_done
            gathered0 gathered1 gi_ready si_ready x_tr xhi_done wcol_done xlo_done ga_done gb_done sila_done hida_done
            bcopy_done bsum_done silb_done hidb_done hid_tr hhi_done hlo_done
            o_done rowcopy_done rows_done added last_zero fin_last fin_ps fin_add fin_out"""
        S = {n: sem(n) for n in names.split()}
        y_back = [sem(f"y_back{b}") for b in range(BATCH)]

        def any_yet(count):
            return not isinstance(count, int) or count > 0

        def hold(eng):
            eng.sem_inc(S["held"], 1)

        block = ctx.enter_context(nc.Block())

        def front_steps(eng, step, end=1):
            step(0)
            step(1)
            with eng.Fori(2, BATCH - end) as i:
                step(i)
            for i in range(BATCH - end, BATCH):
                step(i)

        def is_first(i):
            return isinstance(i, int) and i == 0

        def has_two_before(i):
            return not (isinstance(i, int) and i < 2)

        def is_last(i):
            return isinstance(i, int) and i == BATCH - 1

        def expert_steps(eng, step, end=1):
            for e in range(5):
                step(e, e % 2)
            with eng.Fori(2, (EXP - end) // 2) as t:
                step(2 * t + 1, 1)
                step(2 * t + 2, 0)
            for e in range(EXP - end, EXP):
                step(e, e % 2)

        def is_last_expert(e):
            return isinstance(e, int) and e == EXP - 1

        def nth(e, s):
            return e // 2 if isinstance(e, int) else (e - s) // 2

        @block.sync
        def _(sp):
            sp.dma_start(wdec[:, :], decay).then_inc(S["params"], 16)
            sp.dma_start(ufirst[:, :], first).then_inc(S["params"], 16)
            def load_x(b):
                if any_yet(16 * b):
                    sp.wait_ge(S["x_in"], 16 * b)
                sp.dma_start(xall[:, bass.ds(NT * b, NT), :],
                             x[bass.ds(b, 1)].rearrange("b (t p) d -> p (b t) d", p=P)).then_inc(S["x_in"], 16)

            def store_y(j):
                sp.wait_ge(S["y_evac"], NT * (j + 1))
                sp.dma_start(y_dram[bass.ds(j * SEQ, SEQ), :].rearrange("(t p) d -> p t d", p=P),
                             xall[:, bass.ds(NT * j, NT), :]).then_inc(S["y_out"], 16)

            def store_gate(j):
                sp.wait_ge(S["gw_ready"], j + 1)
                sp.dma_start(hx_dram[bass.ds(j * SEQ, SEQ), D:HX].rearrange("(t p) d -> p t d", p=P),
                             gw[:, :, :]).then_inc(S["gw_out"], 16)

            load_x(0)
            sp.dma_start(v[:, :, :], ctxv[0]).then_inc(S["v_in"], 16)
            load_x(1)
            sp.dma_start(gate_sb[:, :, :], gate).then_inc(S["gate_in"], 16)
            sp.dma_start(sgu_raw, sgu).then_inc(S["shared_w"], 16)
            sp.dma_start(sd_raw[:, 0:SD, :], sd[0:SD * P, :].rearrange("(c p) d -> p c d", p=P)).then_inc(S["shared_d"], 16)
            sp.dma_start(sd_raw[0:SR, SD:SD + 2, :], sd[SD * P:MS, :].rearrange("(c p) d -> p c d", p=SR)).then_inc(S["shared_d"], 16)

            def step(i):
                if not (isinstance(i, int) and i >= BATCH - 2):
                    load_x(i + 2)
                if not is_last(i):
                    sp.wait_ge(S["wkv_step"], WKV_STEPS * i + 3)
                    sp.dma_start(v[:, :, :], ctxv[bass.ds(i + 1, 1)].rearrange("b p g t -> (b p) g t")).then_inc(S["v_in"], 16)
                if not is_first(i):
                    store_gate(i - 1)
                sp.wait_ge(S["h_ready"], i + 1)
                sp.dma_start(hx_dram[bass.ds(i * SEQ, SEQ), 0:D].rearrange("(t p) d -> p t d", p=P),
                             hx[:, :, :]).then_inc(S["h_out"], 16)
                if has_two_before(i):
                    store_y(i - 2)

            front_steps(sp, step, end=2)
            store_y(BATCH - 2)
            store_gate(BATCH - 1)

            def load_gu(e):
                sp.dma_start(raw_gu[e], wgu[e]).then_inc(S[f"wgu_in{e}"], 16)

            def load_d(e):
                sp.dma_start(raw_d[e][:, 0:2, :], wd[e, 0:2 * P, :].rearrange("(c p) d -> p c d", p=P)).then_inc(S[f"wd_in{e}"], 16)
                sp.dma_start(raw_d[e][0:MC[2][1], 2, :], wd[e, 2 * P:M, :]).then_inc(S[f"wd_in{e}"], 16)

            sp.wait_ge(S["up_done"], 6 * BATCH)
            load_gu(0)
            load_gu(1)
            sp.wait_ge(S["down_done"], NT * BATCH)
            load_d(0)
            load_d(1)
            store_y(BATCH - 1)

            def load(e, s):
                if any_yet(DC * (e - 1)):
                    sp.wait_ge(S["wlo_gu_done"], DC * (e - 1))
                sp.dma_start(raw_gu[s], wgu[bass.ds(e, 1)].rearrange("e p k m -> (e p) k m")).then_inc(S[f"wgu_in{s}"], 16)
                if any_yet(e - 1):
                    sp.wait_ge(S["wlo_d_done"], e - 1)
                sp.dma_start(raw_d[s][:, 0:2, :], wd[bass.ds(e, 1), 0:2 * P, :].rearrange("e (c p) d -> p (e c) d", p=P)).then_inc(S[f"wd_in{s}"], 16)
                sp.dma_start(raw_d[s][0:MC[2][1], 2, :], wd[bass.ds(e, 1), 2 * P:M, :].rearrange("e p d -> (e p) d")).then_inc(S[f"wd_in{s}"], 16)

            load(2, 0)
            load(3, 1)
            with sp.Fori(2, EXP // 2) as t:
                load(2 * t, 0)
                load(2 * t + 1, 1)

            sp.wait_ge(S["added"], 32 * EXP)
            sp.wait_ge(S["last_zero"], 1)
            for t in range(NT):
                sp.dma_start(last_out[t * EXP:(t + 1) * EXP, t, :], y_dram[LAST_ROW:DUMP_ROW, :]).then_inc(S["fin_last"], 16)
            for b in range(BATCH):
                sp.dma_start(xall[:, NT * b:NT * (b + 1), :],
                             y_dram[b * SEQ:(b + 1) * SEQ, :].rearrange("(t p) d -> p t d", p=P)).then_inc(y_back[b], 16)
            for b in range(BATCH):
                sp.wait_ge(S["fin_add"], NT * (b + 1))
                sp.dma_start(out[b].rearrange("(t p) d -> p t d", p=P), xall[:, NT * b:NT * (b + 1), :]).then_inc(S["fin_out"], 16)
            sp.wait_ge(S["fin_out"], 16 * BATCH)
            sp.wait_ge(S["y_out"], 16 * BATCH)
            sp.wait_ge(S["h_out"], 16 * BATCH)
            sp.wait_ge(S["gw_out"], 16 * BATCH)
            sp.wait_ge(S["zero_out"], 64)

        @block.gpsimd
        def _(pool):
            nc.gpsimd.memset(ident[:, :], 0.0).then_inc(S["pool_step"], 1)
            nc.gpsimd.memset(ones[:, :], 1.0).then_inc(S["pool_step"], 1)
            nc.gpsimd.memset(tri[:, :, :], 1.0).then_inc(S["pool_step"], 1)
            nc.gpsimd.memset(last_slot[:, :], 0.0).then_inc(S["pool_step"], 1)
            nc.gpsimd.memset(not_last[:, :], 1.0).then_inc(S["pool_step"], 1)
            nc.gpsimd.memset(lmat[:, :], 0.0)
            nc.gpsimd.memset(zrow, 0.0).then_inc(S["pool_step"], 1)
            nc.gpsimd.memset(eps_t[:, :], EPS).then_inc(S["pool_step"], 1)
            nc.gpsimd.memset(mhalf[:, :], -0.5).then_inc(S["pool_step"], 1)
            nc.gpsimd.memset(mone[:, :], -1.0).then_inc(S["pool_step"], 1)
            pool.wait_ge(S["pool_step"], 9)
            nc.gpsimd.affine_select(out=ident[:, :], in_=ident[:, :], compare_op=ALU.not_equal, fill=1.0, base=0,
                                    pattern=[[-1, P]], channel_multiplier=1)
            nc.gpsimd.affine_select(out=lstrict[:, :], in_=ones[:, :], compare_op=ALU.is_gt, fill=0.0, base=0,
                                    pattern=[[1, P]], channel_multiplier=-1)
            nc.gpsimd.affine_select(out=tri[:, :, :], in_=tri[:, :, :], compare_op=ALU.is_gt, fill=0.0, base=0,
                                    pattern=[[1, GROUPS], [-1, GROUPS]], channel_multiplier=0)
            nc.gpsimd.affine_select(out=last_slot[:, :], in_=last_slot[:, :], compare_op=ALU.not_equal, fill=1.0,
                                    base=-(SB - 1), pattern=[[0, 1]], channel_multiplier=1)
            nc.gpsimd.affine_select(out=not_last[:, :], in_=not_last[:, :], compare_op=ALU.not_equal, fill=0.0,
                                    base=-(SB - 1), pattern=[[0, 1]], channel_multiplier=1)
            fl = dict(allow_small_or_imprecise_dtypes=True)
            nc.gpsimd.iota(iota_e[:, :], [[1, EXP]], base=0, channel_multiplier=0, **fl)
            nc.gpsimd.iota(iota_ci[:, :], [[1, CAP]], base=0, channel_multiplier=0, **fl)
            nc.gpsimd.iota(pid1[:, :], [[0, 1]], base=1, channel_multiplier=1, **fl)
            nc.gpsimd.iota(tokid[:, :], [[P, NT]], base=0, channel_multiplier=1, **fl)
            nc.gpsimd.iota(tileno[:, :], [[1, NT]], base=0, channel_multiplier=0, **fl)
            nc.gpsimd.iota(unused[:, :], [[SA, 2]], base=DUMP_ROW + 1, channel_multiplier=1, **fl)
            nc.gpsimd.iota(lastr[:, :], [[1, EXP]], base=LAST_ROW, channel_multiplier=0, **fl).then_inc(S["consts"], 1)
            pool.wait_ge(S["consts"], 1)
            def norm(mv, rstd, shift, stat, ready, n, k):
                pool.wait_ge(S[stat], n + 1)
                nc.gpsimd.tensor_tensor(nmean[:, :], mv[:, :, 0], mone[:, :], ALU.mult)
                nc.gpsimd.tensor_tensor(ve[:, :], mv[:, :, 1], eps_t[:, :], ALU.add).then_inc(S["pool_step"], 1)
                pool.wait_ge(S["pool_step"], 9 + 2 * k + 1)
                nc.gpsimd.tensor_tensor(rstd[:, :], ve[:, :], mhalf[:, :], ALU.pow).then_inc(S["pool_step"], 1)
                pool.wait_ge(S["pool_step"], 9 + 2 * k + 2)
                nc.gpsimd.tensor_tensor(shift[:, :], nmean[:, :], rstd[:, :], ALU.mult).then_inc(S[ready], 1)

            norm(mv1, rstd1, shift1, "stat1", "rstd1_ready", 0, 0)
            for r in range(TOK, ROWS, P):
                pool.dma_start(hx_dram[r:r + P, :], zrow).then_inc(S["zero_out"], 16)
                pool.dma_start(y_dram[r:r + P, :], zrow[:, 0:D]).then_inc(S["zero_out"], 16)

            def split(j, m):
                w = SC[m][1]
                pool.wait_ge(S["hid_done"], 6 * j + m + 1)
                if m == 0 and any_yet(NT * j):
                    pool.wait_ge(S["down_done"], NT * j)
                hold(pool)
                nc.gpsimd.tensor_copy(shid_hi[0:w, m, :], th[0:w, m, :]).then_inc(S["split_step"], 1)
                pool.wait_ge(S["split_step"], 6 * j + m + 1)
                nc.gpsimd.tensor_tensor(shid_lo[0:w, m, :], th[0:w, m, :], shid_hi[0:w, m, :].bitcast(F32),
                                        ALU.subtract).then_inc(S["split_done"], 1)

            def step(i):
                some = not is_first(i)
                kcur, ppcur, ppprev = kb[:, :, 1:PAD], pp[:, :, 1:PAD], pp[:, :, 0:SEQ]
                mul = lambda to, a, b: nc.gpsimd.tensor_tensor(to, a, b, ALU.mult)
                pool.wait_ge(S["pp_ready"], i + 1)
                nc.gpsimd.tensor_tensor(e2b[:, :, 1:PAD], kcur, ppcur, ALU.subtract).then_inc(S["d2_ready"], 1)
                nc.gpsimd.tensor_tensor(d3[:, :, :], ppprev, kcur, ALU.subtract).then_inc(S["d3_ready"], 1)
                pool.wait_ge(S["v_in"], 16 * (i + 1))
                pool.wait_ge(S["inject_ready"], i + 1)
                mul(e2bv[:, :, 1:PAD], e2b[:, :, 1:PAD], v[:, :, :]).then_inc(S["injv_ready"], 1)
                if not is_last(i):
                    norm(mv1, rstd1, shift1, "stat1", "rstd1_ready", i + 1, 2 * i + 1)
                pool.wait_ge(S["e2_ready"], i + 1)
                pool.wait_ge(S["injv_ready"], i + 1)
                mul(v[:, :, :], d3[:, :, :], v[:, :, :]).then_inc(S["n2_ready"], 1)
                pool.wait_ge(S["aa_ready"], i + 1)
                mul(e1[:, :, :], e1[:, :, :], aa[:, :, 0:SEQ]).then_inc(S["num_ready"], 1)
                pool.wait_ge(S["r0_ready"], i + 1)
                mul(bb[:, :, 0:SEQ], bb[:, :, 0:SEQ], d3[:, :, :]).then_inc(S["t_ready"], 1)
                if some:
                    split(i - 1, 0)
                    split(i - 1, 1)
                norm(mv2, rstd2, shift2, "stat2", "rstd2_ready", i, 2 * i + 1 if is_last(i) else 2 * i + 2)
                if some:
                    for m in range(2, 6):
                        split(i - 1, m)

            front_steps(pool, step)
            for m in range(6):
                split(BATCH - 1, m)

            def gather(e, s):
                if any_yet(e - 1):
                    pool.wait_ge(S["x_tr"], e - 1)
                if any_yet(e - 1):
                    pool.wait_ge(S["wcol_done"], e - 1)
                for h in range(2):
                    c = nc.gpsimd.tensor_copy(gi[s][h][:, :], gtab[h][:, bass.ds(e, 1)])
                c.then_inc(S["gi_ready"], 1)
                pool.wait_ge(S["gi_ready"], e + 1)
                hold(pool)
                for h, n in enumerate(SLOTS):
                    pool.indirect_dma_start(out=xg[s][0:n, h, :], out_offset=None, in_=hx_dram[:, :],
                                            in_offset=bass.IndirectOffsetOnAxis(ap=gi[s][h][:, :], axis=0),
                                            bounds_check=ROWS - 1, oob_is_err=True).then_inc(S[f"gathered{s}"], 16)

            def add(e, s):
                for h, tab in enumerate((gtab[0], stab)):
                    c = nc.gpsimd.tensor_copy(si[s][h][:, :], tab[:, bass.ds(e, 1)])
                c.then_inc(S["si_ready"], 1)
                pool.wait_ge(S["si_ready"], e + 1)
                pool.wait_ge(S["rows_done"], e + 1)
                if any_yet(32 * e):
                    pool.wait_ge(S["added"], 32 * e)
                hold(pool)
                for h, n in enumerate(SLOTS):
                    pool.indirect_dma_start(out=y_dram[:, :], out_offset=bass.IndirectOffsetOnAxis(ap=si[s][h][:, :], axis=0),
                                            in_=rows[s][0:n, h, :], in_offset=None, bounds_check=ROWS - 1, oob_is_err=True,
                                            compute_op=ALU.add).then_inc(S["added"], 16)

            pool.wait_ge(S["tables_ready"], 1)
            pool.wait_ge(S["h_out"], 16 * BATCH)
            pool.wait_ge(S["gw_out"], 16 * BATCH)
            pool.wait_ge(S["zero_out"], 64)
            gather(0, 0)
            gather(1, 1)
            pool.wait_ge(S["y_out"], 16 * BATCH)

            def expert(e, s):
                if not (isinstance(e, int) and e >= EXP - 2):
                    gather(e + 2, s)
                if not (isinstance(e, int) and e < 2):
                    add(e - 2, s)

            expert_steps(pool, expert, end=3)
            add(EXP - 2, 0)
            add(EXP - 1, 1)

        @block.scalar
        def _(act):
            act.wait_ge(S["params"], 32)
            nc.scalar.activation(wdec[:, :], wdec[:, :], ACT.Exp).then_inc(S["act_const"], 1)
            nc.scalar.activation(nufirst[:, :], ufirst[:, :], ACT.Copy, scale=-1.0).then_inc(S["act_const"], 1)
            act.wait_ge(S["dve_const"], 1)

            def evac_k(n):
                act.wait_ge(S["k_tr"], n + 1)
                for h in range(2):
                    c = nc.scalar.activation(kb[:, 2 * h:2 * h + 2, 1:PAD], T[h][:, :].rearrange("p (g t) -> p g t", g=2), ACT.Copy)
                c.then_inc(S["kb_ready"], 1)

            def tanh(j, m):
                w = SC[m][1]
                act.wait_ge(S["up_done"], 6 * j + m + 1)
                if any_yet(6 * (j - 1) + m + 1):
                    act.wait_ge(S["split_done"], 6 * (j - 1) + m + 1)
                nc.scalar.activation(th[0:w, m, :], UP[m % 2][0:w, 0:SEQ], ACT.Tanh, scale=0.5).then_inc(S["th_ready"], 1)

            def shared_high(k):
                act.wait_ge(S["shared_w"], 16)
                nc.scalar.activation(sgu_hi[:, k, :], sgu_raw[:, k, :], ACT.Copy).then_inc(S["shi_done"], 1)

            def shared_down_high():
                act.wait_ge(S["shared_d"], 32)
                nc.scalar.activation(sd_hi[:, 0:SD, :], sd_raw[:, 0:SD, :], ACT.Copy)
                nc.scalar.activation(sd_hi[0:SR, SD:SD + 2, :], sd_raw[0:SR, SD:SD + 2, :], ACT.Copy).then_inc(S["sdhi_done"], 1)

            def normalise(n, to, rstd, shift, ready_in, ready):
                act.wait_ge(S[ready_in], n + 1)
                for t in range(NT):
                    c = nc.scalar.activation(to[:, t, :], xall[:, bass.ds(NT * n + t, 1), :].rearrange("p a d -> p (a d)"),
                                             ACT.Identity, bias=shift[:, t:t + 1], scale=rstd[:, t:t + 1])
                c.then_inc(S[ready], 1)

            def softmax_exp(j):
                act.wait_ge(S["mx_ready"], j + 1)
                for t in range(NT):
                    c = nc.scalar.activation(ex[:, t, :], logits[:, t, :], ACT.Exp, bias=nmx[:, t:t + 1], accum_out=ssum[:, t:t + 1])
                c.then_inc(S["ex_ready"], 1)

            def overflow(j):
                act.wait_ge(S["ovf_tr"], j + 1)
                nc.scalar.activation(ovfT[:, bass.ds(j * P, P)], ovf_ps, ACT.Copy).then_inc(S["ovfT_ready"], 1)

            def step(i):
                some, last = not is_first(i), is_last(i)
                act.wait_ge(S["d1_ready"], i + 1)
                for g in range(DC):
                    c = nc.scalar.activation(e1b[:, g, 1:PAD], e1b[:, g, 1:PAD], ACT.Exp, bias=wdec[:, g:g + 1])
                c.then_inc(S["decay_ready"], 1)
                act.wait_ge(S["d2_ready"], i + 1)
                nc.scalar.activation(e2b[:, :, 1:PAD], e2b[:, :, 1:PAD], ACT.Exp).then_inc(S["inject_ready"], 1)
                if some:
                    softmax_exp(i - 1)
                act.wait_ge(S["e1_min"], i + 1)
                nc.scalar.activation(e1[:, :, :], e1[:, :, :], ACT.Exp).then_inc(S["e1_ready"], 1)
                for g in range(DC):
                    c = nc.scalar.activation(d3[:, g, :], d3[:, g, :], ACT.Relu, bias=nufirst[:, g:g + 1])
                c.then_inc(S["relu_done"], 1)
                act.wait_ge(S["relu_done"], i + 1)
                nc.scalar.activation(d3[:, :, :], d3[:, :, :], ACT.Exp, scale=-1.0).then_inc(S["e2_ready"], 1)
                if some:
                    tanh(i - 1, 0)
                if not last:
                    if any_yet(16 * i):
                        act.wait_ge(S["h_out"], 16 * i)
                    normalise(i + 1, kn, rstd1, shift1, "rstd1_ready", "kn_ready")
                act.wait_ge(S["den_ready"], i + 1)
                act.wait_ge(S["n2_ready"], i + 1)
                nc.scalar.activation(d3[:, :, :], bb[:, :, 0:SEQ], ACT.Ln).then_inc(S["ln_ready"], 1)
                act.wait_ge(S["ln_ready"], i + 1)
                nc.scalar.activation(d3[:, :, :], d3[:, :, :], ACT.Exp, scale=-1.0).then_inc(S["r0_ready"], 1)
                if not some:
                    for k in range(DC):
                        shared_high(k)
                    shared_down_high()
                if some:
                    tanh(i - 1, 1)
                if not last:
                    evac_k(i + 1)
                if some:
                    tanh(i - 1, 2)
                    tanh(i - 1, 3)
                if some:
                    tanh(i - 1, 4)
                if any_yet(16 * i):
                    act.wait_ge(S["h_out"], 16 * i)
                normalise(i, hx, rstd2, shift2, "rstd2_ready", "h_ready")
                if some:
                    tanh(i - 1, 5)
                act.wait_ge(S["h_tr"], i + 1)
                for h in range(2):
                    c = nc.scalar.activation(hT[:, 2 * h:2 * h + 2, :], T[h][:, :].rearrange("p (g t) -> p g t", g=2), ACT.Copy)
                c.then_inc(S["hT_ready"], 1)
                if some:
                    overflow(i - 1)
                for h in range(2):
                    c = nc.scalar.activation(hT_hi[:, 2 * h:2 * h + 2, :], T[h][:, :].rearrange("p (g t) -> p g t", g=2), ACT.Copy)
                c.then_inc(S["hThi_ready"], 1)

            normalise(0, kn, rstd1, shift1, "rstd1_ready", "kn_ready")
            evac_k(0)
            front_steps(act, step)
            softmax_exp(BATCH - 1)

            def whi(e, s, k):
                act.wait_ge(S[f"wgu_in{s}"], 16 * (nth(e, s) + 1))
                if any_yet(e - 1):
                    act.wait_ge(S["gb_done"], e - 1)
                nc.scalar.activation(whi_gu[s][:, k, :], raw_gu[s][:, k, :], ACT.Copy).then_inc(S["whi_gu_done"], 1)

            def whid(e, s):
                act.wait_ge(S[f"wd_in{s}"], 32 * (nth(e, s) + 1))
                if any_yet(e - 1):
                    act.wait_ge(S["o_done"], e - 1)
                nc.scalar.activation(whi_d[s][:, 0:2, :], raw_d[s][:, 0:2, :], ACT.Copy)
                w = MC[2][1]
                nc.scalar.activation(whi_d[s][0:w, 2, :], raw_d[s][0:w, 2, :], ACT.Copy).then_inc(S["whi_d_done"], 1)

            def take_x(e):
                act.wait_ge(S["x_tr"], e + 1)
                for h in range(2):
                    c = nc.scalar.activation(xp[:, 2 * h:2 * h + 2, 0:CAP], turned(TR[h]), ACT.Copy)
                c.then_inc(S["xhi_done"], 1)

            def take_weights(e, s):
                if any_yet(e - 1):
                    act.wait_ge(S["hidb_done"], e - 1)
                nc.scalar.activation(wcol[s][:, 0:1], xg[s][:, 0, bass.ds(e + D, 1)], ACT.Copy)
                nc.scalar.activation(wcol[s][0:SB, 1:2], xg[s][0:SB, 1, bass.ds(e + D, 1)], ACT.Identity, bias=last_slot[:, :],
                                     scale=not_last[:, :]).then_inc(S["wcol_done"], 1)

            def silu_a(e):
                act.wait_ge(S["ga_done"], e + 1)
                if any_yet(e):
                    act.wait_ge(S["hida_done"], e)
                nc.scalar.activation(sil_a[:, :], GA[0][:, 0:M], ACT.Silu).then_inc(S["sila_done"], 1)

            def low_parts(e):
                act.wait_ge(S["gb_done"], e + 1)
                if any_yet(e):
                    act.wait_ge(S["bsum_done"], e)
                for q in range(2):
                    c = nc.scalar.activation(low_b[:, q, :], GB[q][SB:2 * SB, 0:M], ACT.Copy)
                c.then_inc(S["bcopy_done"], 1)

            def silu_b(e):
                act.wait_ge(S["bsum_done"], e + 1)
                if any_yet(e):
                    act.wait_ge(S["hidb_done"], e)
                nc.scalar.activation(sil_b[:, :], sum_b[:, 0, :], ACT.Silu).then_inc(S["silb_done"], 1)

            def hidden_high(e):
                act.wait_ge(S["hid_tr"], e + 1)
                nc.scalar.activation(hp[:, 0:2, 0:CAP], turned(TR[0]), ACT.Copy)
                w = MC[2][1]
                nc.scalar.activation(hp[0:w, 2, 0:CAP], TR[1][0:w, 0:CAP], ACT.Copy).then_inc(S["hhi_done"], 1)

            def take_rows(e, s):
                act.wait_ge(S["o_done"], e + 1)
                if any_yet(32 * (e - 1)):
                    act.wait_ge(S["added"], 32 * (e - 1))
                if any_yet(e):
                    act.wait_ge(S["rows_done"], e)
                nc.scalar.activation(rows[s][:, 0, :], RA[:, :], ACT.Copy)
                nc.scalar.activation(row_low[:, :], RB[SB:2 * SB, :], ACT.Copy).then_inc(S["rowcopy_done"], 1)

            for m in range(6):
                tanh(BATCH - 1, m)
            overflow(BATCH - 1)
            act.wait_ge(S["tables_ready"], 1)
            for k in range(DC):
                whi(0, 0, k)
            take_x(0)
            take_weights(0, 0)
            act.wait_ge(S["y_evac"], NT * BATCH)

            def expert(e, s):
                last = is_last_expert(e)
                if not (isinstance(e, int) and e < 2):
                    take_rows(e - 2, s)
                if not last:
                    whi(e + 1, 1 - s, 0)
                    whi(e + 1, 1 - s, 1)
                whid(e, s)
                if not (isinstance(e, int) and e == 0):
                    hidden_high(e - 1)
                silu_a(e)
                if not last:
                    whi(e + 1, 1 - s, 2)
                    whi(e + 1, 1 - s, 3)
                low_parts(e)
                if not last:
                    take_x(e + 1)
                silu_b(e)
                if not last:
                    take_weights(e + 1, 1 - s)

            expert_steps(act, expert)
            take_rows(EXP - 2, 0)
            hidden_high(EXP - 1)
            take_rows(EXP - 1, 1)

        @block.vector
        def _(dve):
            V = nc.vector
            def bn_stats(n, t):
                return V.bn_stats(st6[:, t, :], xall[:, bass.ds(NT * n + t, 1), :].rearrange("p a d -> p (a d)"))

            def aggregate(mv, ready, count):
                dve.wait_ge(S["stats_step"], count)
                hold(dve)
                for t in range(NT):
                    r = V.bn_aggr(mv[:, t, :], st6[:, t, :])
                r.then_inc(S[ready], 1)

            def product_tanh(j, m):
                w = SC[m][1]
                dve.wait_ge(S["th_ready"], 6 * j + m + 1)
                V.scalar_tensor_tensor(th[0:w, m, :], th[0:w, m, :], 1.0, UP[m % 2][0:w, 0:SEQ], ALU.add, ALU.mult).then_inc(S["shid_done"], 1)

            def product(j, m):
                w = SC[m][1]
                dve.wait_ge(S["shid_done"], 6 * j + m + 1)
                V.scalar_tensor_tensor(th[0:w, m, :], th[0:w, m, :], 0.5, UP[m % 2][0:w, SEQ:2 * SEQ], ALU.mult, ALU.mult).then_inc(S["hid_done"], 1)

            def shared_low(k):
                dve.wait_ge(S["shi_done"], k + 1)
                V.tensor_tensor(sgu_lo[:, k, :], sgu_raw[:, k, :], sgu_hi[:, k, :].bitcast(F32), ALU.subtract).then_inc(S["slo_done"], 1)

            def shared_down_low():
                dve.wait_ge(S["sdhi_done"], 1)
                V.tensor_tensor(sd_lo[:, 0:SD, :], sd_raw[:, 0:SD, :], sd_hi[:, 0:SD, :].bitcast(F32), ALU.subtract)
                V.tensor_tensor(sd_lo[0:SR, SD:SD + 2, :], sd_raw[0:SR, SD:SD + 2, :], sd_hi[0:SR, SD:SD + 2, :].bitcast(F32),
                                ALU.subtract).then_inc(S["sdlo_done"], 1)

            def h_low(i):
                dve.wait_ge(S["hThi_ready"], i + 1)
                for h in range(2):
                    r = V.tensor_tensor(hT_lo[:, 2 * h:2 * h + 2, :], T[h][:, :].rearrange("p (g t) -> p g t", g=2),
                                        hT_hi[:, 2 * h:2 * h + 2, :].bitcast(F32), ALU.subtract)
                r.then_inc(S["hTlo_ready"], 1)

            def take_y(j, t):
                dve.wait_ge(S["down_done"], NT * j + t + 1)
                xt = xall[:, bass.ds(NT * j + t, 1), :].rearrange("p a d -> p (a d)")
                V.tensor_tensor(xt, xt, DN[:, :], ALU.add).then_inc(S["y_evac"], 1)

            def flat(a):
                return a[:, :, :].rearrange("p g t -> p (g t)")

            def groups(a):
                return a[:, :, :].rearrange("p t (g j) -> p t g j", g=GROUPS)

            def own(a, n):
                return a[:, :, :].unsqueeze(3).to_broadcast(list(a.shape) + [n])

            def each(a, n):
                return a.unsqueeze(2).to_broadcast([P, NT, n, a.shape[2]])

            def row_maximum(j):
                dve.wait_ge(S["gate_done"], j + 1)
                V.tensor_reduce(nmx[:, :], logits, AX.X, ALU.max, negate=True).then_inc(S["mx_ready"], 1)

            def row_sum(j):
                dve.wait_ge(S["ex_ready"], j + 1)
                V.reciprocal(rsum[:, :], ssum[:, :]).then_inc(S["route_step"], 1)

            def scores(j):
                dve.wait_ge(S["route_step"], ROUTE_STEPS * j + 1)
                V.tensor_tensor(ex[:, :, :], ex[:, :, :], rsum[:, :].unsqueeze(2).to_broadcast([P, NT, EXP]), ALU.mult).then_inc(S["route_step"], 1)

            def group_maxima(j):
                dve.wait_ge(S["route_step"], ROUTE_STEPS * j + 2)
                V.tensor_reduce(gm[:, :, :], groups(ex), AX.X, ALU.max).then_inc(S["route_step"], 1)

            def group_compare(j):
                dve.wait_ge(S["route_step"], ROUTE_STEPS * j + 3)
                V.tensor_tensor(ggt[:], each(gm[:, :, :], GROUPS), own(gm, GROUPS), ALU.is_gt)
                V.tensor_tensor(geq[:], each(gm[:, :, :], GROUPS), own(gm, GROUPS), ALU.is_equal).then_inc(S["route_step"], 1)

            def group_ties(j):
                dve.wait_ge(S["route_step"], ROUTE_STEPS * j + 4)
                V.tensor_tensor(geq[:], geq[:], tri[:, :, :].unsqueeze(1).to_broadcast([P, NT, GROUPS, GROUPS]), ALU.mult).then_inc(S["route_step"], 1)

            def group_beaten(j):
                dve.wait_ge(S["route_step"], ROUTE_STEPS * j + 5)
                V.tensor_tensor(ggt[:], ggt[:], geq[:], ALU.add).then_inc(S["route_step"], 1)

            def group_count(j):
                dve.wait_ge(S["route_step"], ROUTE_STEPS * j + 6)
                V.tensor_reduce(gcnt[:, :, :], ggt[:], AX.X, ALU.add).then_inc(S["route_step"], 1)

            def group_keep(j):
                dve.wait_ge(S["route_step"], ROUTE_STEPS * j + 7)
                V.tensor_scalar(gcnt[:, :, :], gcnt[:, :, :], float(TOPG), None, ALU.is_lt).then_inc(S["route_step"], 1)

            def kept_scores(j):
                dve.wait_ge(S["route_step"], ROUTE_STEPS * j + 8)
                V.tensor_tensor(groups(tmp), groups(ex), own(gcnt, GE), ALU.mult).then_inc(S["route_step"], 1)

            def largest(j):
                dve.wait_ge(S["route_step"], ROUTE_STEPS * j + 9)
                hold(dve)
                for t in range(NT):
                    r = V.max(v8[:, t, :], tmp[:, t, :])
                r.then_inc(S["route_step"], 1)

            def where(j):
                dve.wait_ge(S["route_step"], ROUTE_STEPS * j + 10)
                hold(dve)
                for t in range(NT):
                    r = V.max_index(i8[:, t, :], v8[:, t, :], tmp[:, t, :])
                r.then_inc(S["route_step"], 1)

            def where_float(j):
                dve.wait_ge(S["route_step"], ROUTE_STEPS * j + 11)
                V.tensor_copy(i6[:, :, :], i8[:, :, 0:TOPK]).then_inc(S["route_step"], 1)

            def choices(j):
                dve.wait_ge(S["route_step"], ROUTE_STEPS * j + 12)
                for t in range(NT):
                    r = V.tensor_tensor(eq6[:, t], iota_e[:, :].unsqueeze(1).to_broadcast([P, TOPK, EXP]),
                                        i6[:, t, :].unsqueeze(2).to_broadcast([P, TOPK, EXP]), ALU.is_equal)
                r.then_inc(S["route_step"], 1)

            def chosen(j):
                dve.wait_ge(S["route_step"], ROUTE_STEPS * j + 13)
                V.tensor_reduce(mask[:, :, :], eq6[:].rearrange("p t j e -> p t e j"), AX.X, ALU.add).then_inc(S["route_step"], 1)

            def gate_weights(j):
                dve.wait_ge(S["route_step"], ROUTE_STEPS * j + 14)
                V.tensor_copy(maskb[:, :, :], mask[:, :, :]).then_inc(S["mask_ready"], 1)
                if any_yet(16 * j):
                    dve.wait_ge(S["gw_out"], 16 * j)
                V.tensor_tensor(gw[:, :, :], mask[:, :, :], tmp[:, :, :], ALU.mult).then_inc(S["gw_ready"], 1)

            def last_token(j, t):
                dve.wait_ge(S["route_step"], ROUTE_STEPS * j + 14 + t)
                V.scalar_tensor_tensor(lastt[:, 0:EXP], mask[:, t, :], tokid[:, t:t + 1], lastt[:, 0:EXP], ALU.mult, ALU.max).then_inc(S["route_step"], 1)

            def position_products(j):
                dve.wait_ge(S["zero_out"], 64)
                dve.wait_ge(S["pos_done"], j + 1)
                for t in range(NT):
                    r = V.tensor_tensor(pe6[:, t], eq6[:, t], pos[:, t, :].unsqueeze(1).to_broadcast([P, TOPK, EXP]), ALU.mult)
                r.then_inc(S["route_step"], 1)

            def positions(j):
                dve.wait_ge(S["route_step"], ROUTE_STEPS * j + 17)
                V.tensor_reduce(posel[:, :, :], pe6[:], AX.X, ALU.add).then_inc(S["route_step"], 1)

            def overflow(j):
                dve.wait_ge(S["gw_ready"], j + 1)
                V.scalar_tensor_tensor(ovf[:, :, :], pos, float(CAP - 1), gw[:, :, :], ALU.is_ge, ALU.mult).then_inc(S["ovf_ready"], 1)

            def count_tile(j, t):
                dve.wait_ge(S["route_step"], ROUTE_STEPS * j + 18 + t)
                V.tensor_tensor(cum[:, :], cum[:, :], maskb[:, t, :], ALU.add).then_inc(S["route_step"], 1)

            def one_hot(j, t):
                dve.wait_ge(S["route_step"], ROUTE_STEPS * j + 18)
                if any_yet(j):
                    dve.wait_ge(S["tab_done"], j)
                for k in range(TOPK):
                    V.tensor_scalar(slot1h[:, t, k, :], iota_c[:, :], posel[:, t, k:k + 1], None, ALU.is_equal)
                V.tensor_scalar(val1h[:, t, :, 0:EXP], eq6[:, t], pid1[:, :], None, ALU.mult)
                V.tensor_scalar(val1h[:, t, :, EXP:2 * EXP], eq6[:, t], tileno[:, t:t + 1], None, ALU.mult).then_inc(S["onehot_ready"], 1)

            def next_tokens(j):
                dve.wait_ge(S["onehot_ready"], NT * (j + 1))
                V.tensor_scalar(tokid[:, :], tokid[:, :], float(SEQ), None, ALU.add)
                V.tensor_scalar(tileno[:, :], tileno[:, :], float(NT), None, ALU.add).then_inc(S["route_step"], 1)

            def step(i):
                some, last = not is_first(i), is_last(i)
                ppcur, ppprev = pp[:, :, 1:PAD], pp[:, :, 0:SEQ]
                route = lambda piece, *t: piece(i - 1, *t) if some else None
                dve.wait_ge(S["kb_ready"], i + 1)
                V.tensor_tensor_scan(flat(pp), flat(wrep), flat(kb), NEG, ALU.add, ALU.max).then_inc(S["pp_ready"], 1)
                dve.wait_ge(S["pp_ready"], i + 1)
                V.tensor_tensor(e1b[:, :, 1:PAD], ppprev, ppcur, ALU.subtract).then_inc(S["d1_ready"], 1)
                if some:
                    h_low(i - 1)
                if not last:
                    dve.wait_ge(S["x_in"], 16 * (i + 2))
                    hold(dve)
                    bn_stats(i + 1, 0)
                    bn_stats(i + 1, 1).then_inc(S["stats_step"], 1)
                route(row_maximum)
                if not last:
                    aggregate(mv1, "stat1", 2 * i + 2)
                dve.wait_ge(S["d3_ready"], i + 1)
                for g in range(DC):
                    q = V.tensor_scalar(e1[:, g, :], d3[:, g, :], ufirst[:, g:g + 1], 0.0, ALU.subtract, ALU.min)
                q.then_inc(S["e1_min"], 1)
                dve.wait_ge(S["decay_ready"], i + 1)
                dve.wait_ge(S["inject_ready"], i + 1)
                V.tensor_tensor_scan(flat(bb), flat(e1b), flat(e2b), 0.0, ALU.mult, ALU.add).then_inc(S["wkv_step"], 1)
                route(row_sum)
                dve.wait_ge(S["injv_ready"], i + 1)
                V.tensor_tensor_scan(flat(aa), flat(e1b), flat(e2bv), 0.0, ALU.mult, ALU.add).then_inc(S["wkv_step"], 1)
                route(scores)
                den = bb[:, :, 0:SEQ]
                dve.wait_ge(S["e1_ready"], i + 1)
                dve.wait_ge(S["wkv_step"], WKV_STEPS * i + 2)
                V.tensor_tensor(den, e1[:, :, :], den, ALU.mult).then_inc(S["aa_ready"], 1)
                route(group_maxima)
                if has_two_before(i):
                    take_y(i - 2, 0)
                route(group_compare)
                dve.wait_ge(S["e2_ready"], i + 1)
                dve.wait_ge(S["aa_ready"], i + 1)
                V.tensor_tensor(den, den, d3[:, :, :], ALU.add).then_inc(S["den_ready"], 1)
                route(group_ties)
                route(product_tanh, 0)
                route(group_beaten)
                route(product, 0)
                route(group_count)
                route(group_keep)
                route(kept_scores)
                route(largest)
                route(where)
                route(where_float)
                dve.wait_ge(S["num_ready"], i + 1)
                V.tensor_tensor(e1[:, :, :], e1[:, :, :], v[:, :, :], ALU.add).then_inc(S["wkv_step"], 1)
                route(choices)
                dve.wait_ge(S["r0_ready"], i + 1)
                dve.wait_ge(S["wkv_step"], WKV_STEPS * i + 3)
                V.tensor_tensor(e1[:, :, :], e1[:, :, :], d3[:, :, :], ALU.mult).then_inc(S["wkv_step"], 1)
                route(product_tanh, 1)
                route(product, 1)
                dve.wait_ge(S["t_ready"], i + 1)
                dve.wait_ge(S["wkv_step"], WKV_STEPS * i + 4)
                V.scalar_tensor_tensor(e1[:, :, :], den, -2.0, e1[:, :, :], ALU.add, ALU.mult).then_inc(S["yT_ready"], 1)
                route(chosen)
                route(gate_weights)
                route(product_tanh, 2)
                route(product, 2)
                route(product_tanh, 3)
                route(product, 3)
                if not some:
                    for k in range(DC):
                        shared_low(k)
                    shared_down_low()
                dve.wait_ge(S["y_tr"], i + 1)
                for t in range(NT):
                    xt = xall[:, bass.ds(NT * i + t, 1), :].rearrange("p a d -> p (a d)")
                    q = V.tensor_tensor(xt, xt, T[t][:, :], ALU.subtract)
                q.then_inc(S["wkv_step"], 1)
                route(last_token, 0)
                dve.wait_ge(S["wkv_step"], WKV_STEPS * i + 5)
                hold(dve)
                bn_stats(i, 0)
                bn_stats(i, 1).then_inc(S["stats_step"], 1)
                route(last_token, 1)
                aggregate(mv2, "stat2", 2 * i + 2 if last else 2 * i + 3)
                if has_two_before(i):
                    take_y(i - 2, 1)
                route(position_products)
                route(positions)
                route(overflow)
                route(count_tile, 0)
                route(count_tile, 1)
                route(one_hot, 0)
                route(product_tanh, 4)
                route(product, 4)
                route(one_hot, 1)
                route(next_tokens)
                route(product_tanh, 5)
                route(product, 5)

            dve.wait_ge(S["x_in"], 16)
            hold(dve)
            bn_stats(0, 0)
            bn_stats(0, 1).then_inc(S["stats_step"], 1)
            aggregate(mv1, "stat1", 1)
            dve.wait_ge(S["consts"], 1)
            V.memset(wrep[:, :, :], 1.0).then_inc(S["dve_step"], 1)
            V.memset(kb[:, :, 0:1], NEG)
            V.memset(e1b[:, :, 0:1], 0.0)
            V.memset(e2b[:, :, 0:1], 0.0)
            V.memset(e2bv[:, :, 0:1], 0.0)
            V.memset(cum[:, :], 0.0)
            V.memset(lastt[:, :], 0.0).then_inc(S["dve_step"], 1)
            dve.wait_ge(S["act_const"], 2)
            V.tensor_scalar(wdec[:, :], wdec[:, :], -1.0, None, ALU.mult).then_inc(S["dve_step"], 1)
            V.tensor_copy(iota_c[:, :], iota_ci[:, :]).then_inc(S["dve_step"], 1)
            dve.wait_ge(S["dve_step"], 4)
            V.memset(iota_c[:, CAP - 1:CAP], -1.0)
            for g in range(DC):
                V.tensor_scalar(wrep[:, g, 1:PAD], wrep[:, g, 1:PAD], wdec[:, g:g + 1], None, ALU.mult)
            V.memset(wrep[:, :, 0:1], NEG).then_inc(S["dve_const"], 1)
            dve.wait_ge(S["dve_const"], 1)

            front_steps(dve, step)

            j = BATCH - 1
            h_low(j)
            for piece in (row_maximum, row_sum, scores, group_maxima):
                piece(j)
            take_y(j - 1, 0)
            for piece in (group_compare, group_ties, group_beaten, group_count, group_keep, kept_scores):
                piece(j)
            product_tanh(j, 0)
            largest(j)
            product(j, 0)
            where(j)
            where_float(j)
            product_tanh(j, 1)
            choices(j)
            product(j, 1)
            chosen(j)
            gate_weights(j)
            last_token(j, 0)
            last_token(j, 1)
            take_y(j - 1, 1)
            dve.wait_ge(S["route_step"], ROUTE_STEPS * j + 16)
            V.tensor_copy(lasts[:, :], lastt[:, :]).then_inc(S["last_ready"], 1)
            product_tanh(j, 2)
            product(j, 2)
            product_tanh(j, 3)
            position_products(j)
            product(j, 3)
            positions(j)
            overflow(j)
            one_hot(j, 0)
            product_tanh(j, 4)
            product(j, 4)
            one_hot(j, 1)
            dve.wait_ge(S["last_tr"], 1)
            V.tensor_reduce(lcol[:, :], T[1][0:EXP, 0:P], AX.X, ALU.max).then_inc(S["table_step"], 1)
            product_tanh(j, 5)
            product(j, 5)
            dve.wait_ge(S["table_step"], 1)
            V.tensor_copy(lmat[:, SB - 1:SB], lcol[:, :]).then_inc(S["lmat_ready"], 1)

            dve.wait_ge(S["tab_done"], BATCH)
            V.tensor_copy(tabs[:, 0, :], TAB[0][:, 0:2 * EXP])
            V.tensor_copy(tabs[0:SB, 1, :], TAB[1][0:SB, 0:2 * EXP]).then_inc(S["table_step"], 1)
            for k, (h, n) in enumerate(enumerate(SLOTS)):
                tv, tu = tval[0:n, h, :], tz[0:n, h, :]
                dve.wait_ge(S["table_step"], 2 + 4 * k)
                V.scalar_tensor_tensor(tv, tabs[0:n, h, EXP:2 * EXP], float(P), tabs[0:n, h, 0:EXP], ALU.mult, ALU.add).then_inc(S["table_step"], 1)
                dve.wait_ge(S["table_step"], 3 + 4 * k)
                V.tensor_scalar(tu, tv, 0.0, None, ALU.is_equal).then_inc(S["table_step"], 1)
                dve.wait_ge(S["table_step"], 4 + 4 * k)
                V.scalar_tensor_tensor(tv, tu, unused[0:n, h:h + 1], tv, ALU.mult, ALU.add).then_inc(S["table_step"], 1)
                dve.wait_ge(S["table_step"], 5 + 4 * k)
                V.tensor_scalar(tv, tv, -1.0, None, ALU.add).then_inc(S["table_step"], 1)
            dve.wait_ge(S["table_step"], 10)
            V.tensor_copy(gtab[0][:, :], tval[:, 0, :])
            V.tensor_scalar(tval[0:SB, 1, :], tval[0:SB, 1, :], not_last[:, :], None, ALU.mult).then_inc(S["table_step"], 1)
            dve.wait_ge(S["table_step"], 11)
            V.scalar_tensor_tensor(tz[0:SB, 1, :], lastr[:, :], last_slot[:, :], tval[0:SB, 1, :], ALU.mult, ALU.add).then_inc(S["table_step"], 1)
            dve.wait_ge(S["table_step"], 12)
            V.tensor_copy(stab[:, :], tz[0:SB, 1, :])
            dve.wait_ge(S["lastr_done"], 1)
            V.tensor_tensor(gtab[1][:, :], tval[0:SB, 1, :], T[0][0:SB, 0:EXP], ALU.add).then_inc(S["tables_ready"], 1)

            def wlo(e, s, k):
                dve.wait_ge(S["whi_gu_done"], DC * e + k + 1)
                V.tensor_tensor(wlo_gu[s][:, k, :], raw_gu[s][:, k, :], whi_gu[s][:, k, :].bitcast(F32), ALU.subtract).then_inc(S["wlo_gu_done"], 1)

            def wlod(e, s):
                dve.wait_ge(S["whi_d_done"], e + 1)
                V.tensor_tensor(wlo_d[s][:, 0:2, :], raw_d[s][:, 0:2, :], whi_d[s][:, 0:2, :].bitcast(F32), ALU.subtract)
                w = MC[2][1]
                V.tensor_tensor(wlo_d[s][0:w, 2, :], raw_d[s][0:w, 2, :], whi_d[s][0:w, 2, :].bitcast(F32), ALU.subtract).then_inc(S["wlo_d_done"], 1)

            def low(to, start, bank, rows, chunks):
                lo = to[0:rows, start:start + chunks]
                src = turned(bank)[0:rows, 0:chunks]
                V.tensor_tensor(lo[:, :, ALO], src[:, :, 0:SA], lo[:, :, AHI].bitcast(F32), ALU.subtract)
                return V.tensor_tensor(lo[:, :, CAP:CAP + SB], src[:, :, SA:CAP], lo[:, :, SA:CAP].bitcast(F32), ALU.subtract)

            def x_low(e):
                dve.wait_ge(S["xhi_done"], e + 1)
                low(xp, 0, TR[0], P, 2)
                low(xp, 2, TR[1], P, 2).then_inc(S["xlo_done"], 1)

            def hidden_low(e):
                dve.wait_ge(S["hhi_done"], e + 1)
                low(hp, 0, TR[0], P, 2)
                low(hp, 2, TR[1], MC[2][1], 1).then_inc(S["hlo_done"], 1)

            def hidden_a(e, s):
                dve.wait_ge(S["sila_done"], e + 1)
                dve.wait_ge(S["wcol_done"], e + 1)
                if any_yet(e):
                    dve.wait_ge(S["hid_tr"], e)
                V.scalar_tensor_tensor(hid_a[:, :], sil_a[:, :], wcol[s][:, 0:1], GA[1][:, 0:M], ALU.mult, ALU.mult).then_inc(S["hida_done"], 1)

            def sum_parts(e):
                dve.wait_ge(S["bcopy_done"], e + 1)
                if any_yet(e):
                    dve.wait_ge(S["hidb_done"], e)
                for q in range(2):
                    r = V.tensor_tensor(sum_b[:, q, :], GB[q][0:SB, 0:M], low_b[:, q, :], ALU.add)
                r.then_inc(S["bsum_done"], 1)

            def hidden_b(e, s):
                dve.wait_ge(S["silb_done"], e + 1)
                V.scalar_tensor_tensor(hid_b[:, :], sil_b[:, :], wcol[s][0:SB, 1:2], sum_b[:, 1, :], ALU.mult, ALU.mult).then_inc(S["hidb_done"], 1)

            def sum_rows(e, s):
                dve.wait_ge(S["rowcopy_done"], e + 1)
                V.tensor_tensor(rows[s][0:SB, 1, :], RB[0:SB, :], row_low[:, :], ALU.add).then_inc(S["rows_done"], 1)

            wlo(0, 0, 0)
            take_y(BATCH - 1, 0)
            for k in range(1, DC):
                wlo(0, 0, k)
            take_y(BATCH - 1, 1)
            x_low(0)

            def expert(e, s):
                last = is_last_expert(e)
                if not (isinstance(e, int) and e < 2):
                    sum_rows(e - 2, s)
                if not last:
                    wlo(e + 1, 1 - s, 0)
                    wlo(e + 1, 1 - s, 1)
                wlod(e, s)
                if not (isinstance(e, int) and e == 0):
                    hidden_low(e - 1)
                hidden_a(e, s)
                if not last:
                    wlo(e + 1, 1 - s, 2)
                    wlo(e + 1, 1 - s, 3)
                sum_parts(e)
                if not last:
                    x_low(e + 1)
                hidden_b(e, s)

            expert_steps(dve, expert)
            V.memset(last_out, 0.0).then_inc(S["last_zero"], 1)
            sum_rows(EXP - 2, 0)
            hidden_low(EXP - 1)
            sum_rows(EXP - 1, 1)

            for n in range(BATCH * NT):
                if n % NT == 0:
                    dve.wait_ge(y_back[n // NT], 16)
                dve.wait_ge(S["fin_ps"], n + 1)
                V.tensor_tensor(xall[:, n, :], xall[:, n, :], psum[n % 8][:, :], ALU.add).then_inc(S["fin_add"], 1)

        @block.tensor
        def _(pe):
            mm, tr = nc.tensor.matmul, nc.tensor.transpose

            def transpose_in(src, done):
                for g in range(DC):
                    for t in range(NT):
                        r = tr(T[g // 2][:, (g % 2) * SEQ + t * P:(g % 2) * SEQ + (t + 1) * P], src[:, t, g * P:(g + 1) * P], ident[:, :])
                r.then_inc(S[done], 1)

            def up(j, m):
                m0, w = SC[m]
                if m == 0:
                    pe.wait_ge(S["hTlo_ready"], j + 1)
                    pe.wait_ge(S["slo_done"], DC)
                if any_yet(6 * j + m - 1):
                    pe.wait_ge(S["hid_done"], 6 * j + m - 1)
                for q in range(2):
                    for k in range(DC):
                        for n, (a, z) in enumerate(((sgu_hi, hT_hi), (sgu_hi, hT_lo), (sgu_lo, hT_hi))):
                            r = mm(UP[m % 2][0:w, q * SEQ:(q + 1) * SEQ], a[:, k, q * MS + m0:q * MS + m0 + w], z[:, k, :],
                                   start=(k == 0 and n == 0), stop=(k == DC - 1 and n == 2))
                r.then_inc(S["up_done"], 1)

            def down(j, t):
                if t == 0:
                    pe.wait_ge(S["split_done"], 6 * (j + 1))
                    pe.wait_ge(S["sdlo_done"], 1)
                if any_yet(NT * j + t):
                    pe.wait_ge(S["y_evac"], NT * j + t)
                for m, (m0, w) in enumerate(SC):
                    for n, (a, z) in enumerate(((shid_hi, sd_hi), (shid_hi, sd_lo), (shid_lo, sd_hi))):
                        r = mm(DN[:, :], a[0:w, m, t * P:(t + 1) * P], z[0:w, m, :],
                               start=(m == 0 and n == 0), stop=(m == len(SC) - 1 and n == 2))
                r.then_inc(S["down_done"], 1)

            def place(j):
                pe.wait_ge(S["mask_ready"], j + 1)
                for t in range(NT):
                    mm(pos[:, t, :], ones[:, :], cum[:, :], start=True, stop=False)
                    if t:
                        mm(pos[:, t, :], ones[:, :], maskb[:, 0, :], start=False, stop=False)
                    r = mm(pos[:, t, :], lstrict[:, :], maskb[:, t, :], start=False, stop=True)
                r.then_inc(S["pos_done"], 1)

            def overflow(j):
                pe.wait_ge(S["ovf_ready"], j + 1)
                if any_yet(j):
                    pe.wait_ge(S["ovfT_ready"], j)
                tr(ovf_ps, ovf[:, :, :].rearrange("p t e -> p (t e)"), ident[:, :]).then_inc(S["ovf_tr"], 1)

            def slots(j):
                pe.wait_ge(S["onehot_ready"], NT * (j + 1))
                for h, n in enumerate(SLOTS):
                    for t in range(NT):
                        for k in range(TOPK):
                            r = mm(TAB[h][0:n, 0:2 * EXP], slot1h[:, t, k, h * SA:h * SA + n], val1h[:, t, k, :],
                                   start=(is_first(j) and t == 0 and k == 0), stop=(is_last(j) and t == NT - 1 and k == TOPK - 1))
                r.then_inc(S["tab_done"], 1)

            def step(i):
                some, last = not is_first(i), is_last(i)
                j = i - 1
                if some:
                    up(j, 0)
                    up(j, 1)
                if has_two_before(i):
                    down(j - 1, 1)
                if not last:
                    pe.wait_ge(S["kn_ready"], i + 2)
                    transpose_in(kn, "k_tr")
                if some:
                    up(j, 2)
                    up(j, 3)
                pe.wait_ge(S["yT_ready"], i + 1)
                pe.wait_ge(S["kb_ready"], i + 1 if last else i + 2)
                for t in range(NT):
                    for g in range(DC):
                        r = tr(T[t][:, g * P:(g + 1) * P], e1[:, g, t * P:(t + 1) * P], ident[:, :])
                r.then_inc(S["y_tr"], 1)
                if some:
                    place(j)
                    up(j, 4)
                    up(j, 5)
                pe.wait_ge(S["h_ready"], i + 1)
                transpose_in(hx, "h_tr")
                if some:
                    overflow(j)
                pe.wait_ge(S["hT_ready"], i + 1)
                if some:
                    pe.wait_ge(S["ovfT_ready"], i)
                for t in range(NT):
                    for k in range(DC):
                        r = mm(logits[:, t, :], hT[:, k, t * P:(t + 1) * P], gate_sb[:, k, :], start=(k == 0), stop=(k == DC - 1))
                r.then_inc(S["gate_done"], 1)
                if some:
                    slots(j)
                    down(j, 0)

            pe.wait_ge(S["consts"], 1)
            pe.wait_ge(S["kn_ready"], 1)
            transpose_in(kn, "k_tr")
            pe.wait_ge(S["gate_in"], 16)
            front_steps(pe, step)
            j = BATCH - 1
            for m in range(2):
                up(j, m)
            down(j - 1, 1)
            for m in range(2, 4):
                up(j, m)
            place(j)
            for m in range(4, 6):
                up(j, m)
            overflow(j)
            pe.wait_ge(S["last_ready"], 1)
            tr(T[1][:, 0:P], lasts[:, :], ident[:, :]).then_inc(S["last_tr"], 1)
            slots(j)
            pe.wait_ge(S["lmat_ready"], 1)
            mm(T[0][0:SB, 0:EXP], lmat[:, :], ident[0:EXP, 0:EXP], start=True, stop=True).then_inc(S["lastr_done"], 1)
            down(j, 0)
            down(j, 1)

            def bring_x(e, s):
                pe.wait_ge(S[f"gathered{s}"], 32 * (nth(e, s) + 1))
                if any_yet(e - 1):
                    pe.wait_ge(S["hlo_done"], e - 1)
                for k in range(DC):
                    for h, n in enumerate(SLOTS):
                        at = (k % 2) * CAP + h * SA
                        r = tr(TR[k // 2][:, at:at + n], xg[s][0:n, h, k * P:(k + 1) * P], ident[0:n, 0:n])
                r.then_inc(S["x_tr"], 1)

            def gate_up_a(e, s):
                pe.wait_ge(S["xlo_done"], e + 1)
                pe.wait_ge(S["wlo_gu_done"], DC * (e + 1))
                if any_yet(e):
                    pe.wait_ge(S["hida_done"], e)
                for q in range(2):
                    for k in range(DC):
                        for n, (part, w) in enumerate(((AHI, whi_gu), (AHI, wlo_gu), (ALO, whi_gu))):
                            r = mm(GA[q][:, 0:M], xp[:, k, part], w[s][:, k, q * M:(q + 1) * M],
                                   start=(k == 0 and n == 0), stop=(k == DC - 1 and n == 2))
                r.then_inc(S["ga_done"], 1)

            def gate_up_b(e, s):
                if any_yet(e):
                    pe.wait_ge(S["bsum_done"], e)
                for q in range(2):
                    for k in range(DC):
                        for n, w in enumerate((whi_gu, wlo_gu)):
                            r = mm(GB[q][:, 0:M], xp[:, k, BHL], w[s][:, k, q * M:(q + 1) * M],
                                   start=(k == 0 and n == 0), stop=(k == DC - 1 and n == 1))
                r.then_inc(S["gb_done"], 1)

            def turn_hidden(e):
                pe.wait_ge(S["hida_done"], e + 1)
                pe.wait_ge(S["hidb_done"], e + 1)
                for c, (m0, w) in enumerate(MC):
                    at = (c % 2) * CAP
                    tr(TR[c // 2][0:w, at:at + SA], hid_a[:, m0:m0 + w], ident[:, :])
                    r = tr(TR[c // 2][0:w, at + SA:at + CAP], hid_b[:, m0:m0 + w], ident[0:SB, 0:SB])
                r.then_inc(S["hid_tr"], 1)

            def down_rows(e, s):
                pe.wait_ge(S["hlo_done"], e + 1)
                pe.wait_ge(S["wlo_d_done"], e + 1)
                if any_yet(e):
                    pe.wait_ge(S["rows_done"], e)
                for c, (m0, w) in enumerate(MC):
                    for n, (part, wt) in enumerate(((AHI, whi_d), (AHI, wlo_d), (ALO, whi_d))):
                        mm(RA[:, :], hp[0:w, c, part], wt[s][0:w, c, :], start=(c == 0 and n == 0), stop=(c == len(MC) - 1 and n == 2))
                    for n, wt in enumerate((whi_d, wlo_d)):
                        r = mm(RB[:, :], hp[0:w, c, BHL], wt[s][0:w, c, :], start=(c == 0 and n == 0), stop=(c == len(MC) - 1 and n == 1))
                r.then_inc(S["o_done"], 1)

            pe.wait_ge(S["tables_ready"], 1)
            bring_x(0, 0)

            def expert(e, s):
                some = not (isinstance(e, int) and e == 0)
                gate_up_a(e, s)
                if some:
                    turn_hidden(e - 1)
                gate_up_b(e, s)
                if not is_last_expert(e):
                    bring_x(e + 1, 1 - s)
                if some:
                    down_rows(e - 1, 1 - s)

            expert_steps(pe, expert)
            turn_hidden(EXP - 1)
            down_rows(EXP - 1, 1)

            pe.wait_ge(S["fin_last"], 16 * NT)
            for n in range(BATCH * NT):
                if n >= 8:
                    pe.wait_ge(S["fin_add"], n - 7)
                mm(psum[n % 8][:, :], ovfT[:, n // NT * P:(n // NT + 1) * P], last_out[:, n % NT, :], start=True, stop=True).then_inc(S["fin_ps"], 1)


def kernel(x, ctx_2048, L0_xattn_time_decay, L0_xattn_time_first, L0_ffn_gate_weight, L0_ffn_Wg, L0_ffn_Wu,
           L0_ffn_Wd, L0_ffn_Sg, L0_ffn_Su, L0_ffn_Sd):
    import numpy as np
    import concourse.bacc as bacc
    from concourse.bass_utils import run_bass_kernel_spmd

    def put(a):
        return np.ascontiguousarray(a)

    def contract_first(w):
        w = np.asarray(w)
        w = w.reshape(w.shape[:-1] + (DC, P))
        return np.moveaxis(w, (-1, -2), (-3, -2))

    arrays = {
        "x": put(x),
        "ctxv": put(contract_first(ctx_2048)),
        "decay": put(np.asarray(L0_xattn_time_decay).reshape(DC, P).T),
        "first": put(np.asarray(L0_xattn_time_first).reshape(DC, P).T),
        "gate": put(contract_first(L0_ffn_gate_weight)),
        "wgu": put(np.concatenate([contract_first(L0_ffn_Wg), contract_first(L0_ffn_Wu)], axis=-1)),
        "wd": put(np.swapaxes(np.asarray(L0_ffn_Wd), 1, 2)),
        "sgu": put(np.concatenate([contract_first(L0_ffn_Sg), contract_first(L0_ffn_Su)], axis=-1)),
        "sd": put(np.asarray(L0_ffn_Sd).T),
    }
    nc = bacc.Bacc("TRN2", target_bir_lowering=False, num_devices=1)
    args = [nc.dram_tensor(f"in_{n}", a.shape, mybir.dt.from_np(a.dtype), kind="ExternalInput").ap() for n, a in arrays.items()]
    args.append(nc.dram_tensor("out_0", (BATCH, SEQ, D), F32, kind="ExternalOutput").ap())
    build(nc, *args)
    r = run_bass_kernel_spmd(nc, [{f"in_{n}": a for n, a in arrays.items()}], core_ids=[0])
    return r.results[0]["out_0"]
```
